# Optimizing a Trainium2 kernel written in Bass

```python
import numpy as np
import jax
import jax.numpy as jnp

def _softmax(x, axis=-1):
    return jax.nn.softmax(x, axis=axis)

def _gelu(x):
    return jax.nn.gelu(x, approximate=True)

def _silu(x):
    return jax.nn.silu(x)

def _sigmoid(x):
    return jax.nn.sigmoid(x)

def _layernorm(x, axis=-1, eps=1e-05):
    m = jnp.mean(x, axis=axis, keepdims=True)
    v = jnp.var(x, axis=axis, keepdims=True)
    return (x - m) / jnp.sqrt(v + eps)

def _scatter_add(tgt, idx, src, axis=0):
    return tgt.at[idx].add(src)

def _segment_sum(src, seg, n):
    return jax.ops.segment_sum(src, seg, n)
kernel_name = 'mk_prb_d1_jaxref_r8_9cd6d6'

def setup_inputs(seed: int=0):
    np.random.seed(seed)
    _w = jnp.asarray

    def _L0_attn_setup():
        import jax, jax.numpy as jnp
        import numpy as np
        D_MODEL = 128
        HIDDEN = 256
        D_STATE = 16
        KERN = 3
        BATCH = 2
        SEQ = 256

        def _layernorm(x, g, b, eps=1e-05):
            m = jnp.mean(x, axis=-1, keepdims=True)
            v = jnp.var(x, axis=-1, keepdims=True)
            return (x - m) * jax.lax.rsqrt(v + eps) * g + b
        key = jax.random.key(seed)
        ks = jax.random.split(key, 10)
        w_scale = 0.02
        return {'x': jax.random.normal(ks[0], (BATCH, SEQ, D_MODEL), jnp.float32), 'W_x': jax.random.normal(ks[1], (HIDDEN, D_MODEL), jnp.float32) * w_scale, 'b_x': jnp.zeros((HIDDEN,), jnp.float32), 'W_g': jax.random.normal(ks[2], (HIDDEN, D_MODEL), jnp.float32) * w_scale, 'b_g': jnp.zeros((HIDDEN,), jnp.float32), 'conv_w': jax.random.normal(ks[3], (HIDDEN, 1, KERN), jnp.float32) * 0.3, 'conv_b': jnp.zeros((HIDDEN,), jnp.float32), 'A_raw': jax.random.normal(ks[4], (HIDDEN, D_STATE), jnp.float32), 'B_ssm': jax.random.normal(ks[5], (HIDDEN, D_STATE), jnp.float32), 'C_ssm': jax.random.normal(ks[6], (HIDDEN, D_STATE), jnp.float32), 'W_dt': jax.random.normal(ks[7], (HIDDEN, D_MODEL), jnp.float32) * w_scale, 'b_dt': jnp.zeros((HIDDEN,), jnp.float32), 'W_out': jax.random.normal(ks[8], (D_MODEL, HIDDEN), jnp.float32) * w_scale, 'b_out': jnp.zeros((D_MODEL,), jnp.float32), 'ln_g': jnp.ones((D_MODEL,), jnp.float32), 'ln_b': jnp.zeros((D_MODEL,), jnp.float32)}
    _L0_attn_in = _L0_attn_setup()

    def _L0_ffn_setup():
        import jax, jax.numpy as jnp
        import numpy as np
        HIDDEN = 128
        NUM_EXPERTS = 8
        TOP_K = 2
        B, S = (2, 256)
        key = jax.random.key(seed)
        k1, k2, k3, k4, k5 = jax.random.split(key, 5)
        d, dff, E = (HIDDEN, 4 * HIDDEN, NUM_EXPERTS)
        x = jax.random.normal(k1, (B, S, d), dtype=jnp.float32)
        W1 = jax.random.normal(k2, (E, d, dff), dtype=jnp.float32) * (1.0 / np.sqrt(d))
        b1 = jax.random.normal(k3, (E, dff), dtype=jnp.float32) * 0.01
        W2 = jax.random.normal(k4, (E, dff, d), dtype=jnp.float32) * (1.0 / np.sqrt(dff))
        b2 = jax.random.normal(k5, (E, d), dtype=jnp.float32) * 0.01
        return {'x': x, 'W1': W1, 'b1': b1, 'W2': W2, 'b2': b2}
    _L0_ffn_in = _L0_ffn_setup()
    _d = {'L0_attn_x': _L0_attn_in['x'], 'L0_attn_W_x': _L0_attn_in['W_x'], 'L0_attn_b_x': _L0_attn_in['b_x'], 'L0_attn_W_g': _L0_attn_in['W_g'], 'L0_attn_b_g': _L0_attn_in['b_g'], 'L0_attn_conv_w': _L0_attn_in['conv_w'], 'L0_attn_conv_b': _L0_attn_in['conv_b'], 'L0_attn_A_raw': _L0_attn_in['A_raw'], 'L0_attn_B_ssm': _L0_attn_in['B_ssm'], 'L0_attn_C_ssm': _L0_attn_in['C_ssm'], 'L0_attn_W_dt': _L0_attn_in['W_dt'], 'L0_attn_b_dt': _L0_attn_in['b_dt'], 'L0_attn_W_out': _L0_attn_in['W_out'], 'L0_attn_b_out': _L0_attn_in['b_out'], 'L0_attn_ln_g': _L0_attn_in['ln_g'], 'L0_attn_ln_b': _L0_attn_in['ln_b'], 'L0_ffn_W1': _L0_ffn_in['W1'], 'L0_ffn_b1': _L0_ffn_in['b1'], 'L0_ffn_W2': _L0_ffn_in['W2'], 'L0_ffn_b2': _L0_ffn_in['b2']}
    _x0 = _d['L0_attn_x']
    _d['L0_attn_x'] = jax.random.normal(jax.random.fold_in(jax.random.key(seed), 1), (32, 256, 128), dtype=_x0.dtype)
    del _x0
    return _d

def reference(L0_attn_x, L0_attn_W_x, L0_attn_b_x, L0_attn_W_g, L0_attn_b_g, L0_attn_conv_w, L0_attn_conv_b, L0_attn_A_raw, L0_attn_B_ssm, L0_attn_C_ssm, L0_attn_W_dt, L0_attn_b_dt, L0_attn_W_out, L0_attn_b_out, L0_attn_ln_g, L0_attn_ln_b, L0_ffn_W1, L0_ffn_b1, L0_ffn_W2, L0_ffn_b2):

    def _L0_attn_ref(x, W_x, b_x, W_g, b_g, conv_w, conv_b, A_raw, B_ssm, C_ssm, W_dt, b_dt, W_out, b_out, ln_g, ln_b):
        import jax, jax.numpy as jnp
        import numpy as np
        D_MODEL = 128
        HIDDEN = 256
        D_STATE = 16
        KERN = 3
        BATCH = 2
        SEQ = 256

        def _layernorm(x, g, b, eps=1e-05):
            m = jnp.mean(x, axis=-1, keepdims=True)
            v = jnp.var(x, axis=-1, keepdims=True)
            return (x - m) * jax.lax.rsqrt(v + eps) * g + b
        u = jnp.einsum('bld,hd->blh', x, W_x) + b_x
        g = jax.nn.sigmoid(jnp.einsum('bld,hd->blh', x, W_g) + b_g)
        pad = conv_w.shape[-1] // 2
        h = jax.lax.conv_general_dilated(jnp.transpose(u, (0, 2, 1)), conv_w, window_strides=(1,), padding=[(pad, pad)], feature_group_count=conv_w.shape[0], dimension_numbers=('NCH', 'OIH', 'NCH')) + conv_b[None, :, None]
        h = jnp.transpose(h, (0, 2, 1))
        u = u * g + h * (1.0 - g)
        dt = jax.nn.softplus(jnp.einsum('bld,hd->blh', x, W_dt) + b_dt).mean(axis=(0, 1))
        dt = jnp.clip(dt, 0.001, 2.0)
        A = -jax.nn.softplus(A_raw)
        A_d = jnp.exp(A * dt[:, None])
        B_d = (A_d - 1.0) / (A + 1e-06) * B_ssm
        Bsz, L, H = u.shape
        S = A_d.shape[1]

        def step(carry, u_t):
            new = A_d[None] * carry + B_d[None] * u_t[:, :, None]
            y_t = jnp.einsum('bhs,hs->bh', new, C_ssm)
            return (new, y_t)
        init = jnp.zeros((Bsz, H, S), dtype=u.dtype)
        _, ys = jax.lax.scan(step, init, jnp.transpose(u, (1, 0, 2)))
        y = jnp.transpose(ys, (1, 0, 2))
        out = jnp.einsum('blh,dh->bld', y, W_out) + b_out
        return _layernorm(x + out, ln_g, ln_b)

    def _L0_ffn_ref(x, W1, b1, W2, b2):
        import jax, jax.numpy as jnp
        import numpy as np
        HIDDEN = 128
        NUM_EXPERTS = 8
        TOP_K = 2
        B, S = (2, 256)
        Bm, Sm, d = x.shape
        E = W1.shape[0]
        x_flat = x.reshape(-1, d)
        h = jnp.mod(x_flat[:, :TOP_K].sum(axis=1).astype(jnp.int32), E)
        sel = jnp.stack([h, jnp.mod(h + 1, E)], axis=1)

        def step(acc, params):
            e, W1e, b1e, W2e, b2e = params
            w = jnp.any(sel == e, axis=1).astype(x.dtype) / TOP_K
            y = jnp.maximum(x_flat @ W1e + b1e, 0.0) @ W2e + b2e
            return (acc + w[:, None] * y, None)
        init = jnp.zeros_like(x_flat)
        out_flat, _ = jax.lax.scan(step, init, (jnp.arange(E), W1, b1, W2, b2))
        return out_flat.reshape(Bm, Sm, d)
    x = L0_attn_x
    xn = _layernorm(x, axis=-1)
    x = x + _L0_attn_ref(xn, L0_attn_W_x, L0_attn_b_x, L0_attn_W_g, L0_attn_b_g, L0_attn_conv_w, L0_attn_conv_b, L0_attn_A_raw, L0_attn_B_ssm, L0_attn_C_ssm, L0_attn_W_dt, L0_attn_b_dt, L0_attn_W_out, L0_attn_b_out, L0_attn_ln_g, L0_attn_ln_b) + _L0_ffn_ref(xn, L0_ffn_W1, L0_ffn_b1, L0_ffn_W2, L0_ffn_b2)
    return x

_drawn_inputs = setup_inputs


def setup_inputs(seed=0):
    import zlib

    import numpy as np

    out = dict(_drawn_inputs(seed))
    spreads = {'L0_attn_b_x': (0.0, 0.1),
     'L0_attn_b_g': (0.0, 0.8),
     'L0_attn_conv_b': (0.0, 0.1),
     'L0_attn_b_dt': (0.0, 2.0),
     'L0_attn_b_out': (0.0, 0.1),
     'L0_attn_ln_g': (1.0, 0.2),
     'L0_attn_ln_b': (0.0, 0.1)}
    factors = {'L0_attn_W_g': 5.976, 'L0_attn_W_dt': 64.0, 'L0_ffn_b1': 23.194, 'L0_ffn_b2': 8.0}
    for name, (base, spread) in spreads.items():
        noise = np.random.default_rng([zlib.crc32(name.encode()), seed]).standard_normal(out[name].shape)
        drawn = base * np.exp(spread * noise) if base else spread * noise
        out[name] = jnp.asarray(drawn.astype(out[name].dtype))
    for name, factor in factors.items():
        out[name] = (out[name] * factor).astype(out[name].dtype)
    return out
```

```python
from contextlib import ExitStack

import numpy as np

import concourse.bass as bass
from concourse import mybir

ALU = mybir.AluOpType
ACT = mybir.ActivationFunctionType
AX_X = mybir.AxisListType.X
F32 = mybir.dt.float32
F32R = mybir.dt.float32r
BF16 = mybir.dt.bfloat16
I32 = mybir.dt.int32
U32 = mybir.dt.uint32

P = 128
Q = 32
NQ = P // Q
FT = 256
EPS = 1e-5
SOFT = 20.0
DT_MIN, DT_MAX = 0.001, 2.0


def ssm_moe_layer(nc, x, W_x, b_x, W_g, b_g, conv_w, conv_b, A_raw, B_ssm, C_ssm, W_dt, b_dt,
                  W_out, b_out, ln_g, ln_b, W1, b1, W2, b2, out):
    B, L, D = x.shape
    H, S = A_raw.shape
    E, _, DFF = W1.shape
    assert D == P and H % P == 0 and DFF % P == 0 and L % P == 0
    NTOK = B * L
    NT = NTOK // P
    HB = H // P
    KB = DFF // P
    NC = L // Q
    BC = B * NC
    CH = 512
    NCH = NTOK // CH
    TPC = CH // P
    NG = P // NQ
    NPAIR = HB * NG // 2
    PPB = NG // 2
    MAXT = (NTOK + E * (FT - 1)) // FT
    ROWS = (MAXT + 2) * FT
    QT = 4
    TQ = NT // QT
    TA_ = 5
    GB = 4
    NGATE = B // GB
    FH = FT // P

    with ExitStack() as ctx:
        def sb(name, shape, dt=F32):
            return ctx.enter_context(nc.sbuf_tensor(name, shape, dt))

        def sem(name):
            return ctx.enter_context(nc.semaphore(name))

        xs_dram = nc.dram_tensor("sorted_tokens", [ROWS, D], F32).ap()
        ys_dram = nc.dram_tensor("sorted_outputs", [ROWS, D], F32).ap()

        RA = sb("RA", [P, NTOK])
        RB = sb("RB", [P, HB, NTOK])
        RC = sb("RC", [P, HB, NTOK])
        XN = RA[:, :].rearrange("p (t d) -> p t d", d=D)
        UT = [RA[:, :].rearrange("p (g c) -> p g c", g=NG), RC[:, 0, :].rearrange("p (g c) -> p g c", g=NG)]
        YT = [RC[:, 1, :], RA[:, :]]
        INTRA = RB[:, 0, :].rearrange("p (g m) -> p g m", m=P)
        NGRP = HB * NG
        INJ = RB[:, 1, 0:NGRP * NQ * S].rearrange("p (g m) -> p g m", m=NQ * S)
        READ = RB[:, 1, NGRP * NQ * S:NGRP * NQ * S + NPAIR * P].rearrange("p (r m) -> p r m", m=P)

        RR = sb("RR", [P, 8 * CH], F32R)
        xh = [RR[:, s * CH:(s + 1) * CH] for s in range(2)]
        xl = [RR[:, (2 + s) * CH:(3 + s) * CH] for s in range(2)]
        PW = RR[:, 4 * CH:4 * CH + 2 * 3 * HB * P].rearrange("p (v j m) -> p v j m", v=2, m=P)
        W1h = [RR[:, s * DFF:(s + 1) * DFF] for s in range(3)]
        W1l = [RR[:, (3 + s) * DFF:(4 + s) * DFF] for s in range(3)]
        XSPLIT = RR[:, 6 * DFF:6 * DFF + 2 * FT].rearrange("p (v h d) -> p v h d", v=2, h=FH)
        XT = RR[:, 6 * DFF + 2 * FT:6 * DFF + 4 * FT]

        AR = sb("AR", [P, 11 * CH])
        xin = [AR[:, s * CH:(s + 1) * CH].rearrange("p (t d) -> p t d", d=D) for s in range(2)]
        mb = [AR[:, (2 + s) * CH:(3 + s) * CH] for s in range(2)]
        eb = [AR[:, (4 + s) * CH:(5 + s) * CH] for s in range(2)]
        junk = AR[:, 6 * CH:7 * CH]
        W2S = [AR[:, s * DFF:(s + 1) * DFF].rearrange("p (k d) -> p k d", k=KB) for s in range(3)]
        W1RAW = [AR[:, 3 * CH:4 * CH], AR[:, 9 * CH:10 * CH], AR[:, 10 * CH:11 * CH]]

        def raw_slot(k):
            return k + 1 if k < 2 else 0 if k == 2 else k % 3

        def raw_loads(k):
            return sum(raw_slot(j) == raw_slot(k) for j in range(k + 1))

        HID = [AR[:, (4 + 2 * n) * CH:(6 + 2 * n) * CH].rearrange("p (k t) -> p k t", k=KB) for n in range(2)]
        XSIN = AR[:, 8 * CH:8 * CH + FT].rearrange("p (h d) -> p h d", h=FH)
        YSB = AR[:, 8 * CH + FT:9 * CH].rearrange("p (h d) -> p h d", h=FH)
        TG = AR[:, 9 * CH:11 * CH]

        identity = sb("identity", [P, P])
        vrows = sb("vrows", [8 + E * KB, P])
        VC = sb("VC", [P, 8 + E * KB])
        bx, bg, bdt, cb = (VC[:, 2 * n:2 * n + 2] for n in range(4))
        B1C = VC[:, 8:8 + E * KB].rearrange("p (e k) -> p e k", e=E)
        cw = sb("cw", [P, HB, 3])
        cwn = sb("cwn", [P, HB, 3])
        cbn = sb("cbn", [P, HB])
        WoT = sb("WoT", [P, HB, D])
        b2s = sb("b2s", [P, 3, D])
        b2p = sb("b2p", [P, D])
        lng = sb("lng", [P, D])
        lnb = sb("lnb", [P, D])
        bo = sb("bo", [1, D])
        ones1 = sb("ones1", [1, P])
        bdtm = sb("bdtm", [P, HB])
        Araw = sb("Araw", [P, HB, S])
        Bssm = sb("Bssm", [P, HB, S])
        Cssm = sb("Cssm", [P, HB, S])
        Aneg = sb("Aneg", [P, HB, S])
        aval = sb("aval", [P, HB, S])
        sv = sb("sv", [P, HB, S])
        sv2 = sb("sv2", [P, HB, S])
        acc1 = sb("acc1", [P, HB, NCH])
        acc2 = sb("acc2", [P, HB, NCH])
        dtv = sb("dtv", [P, HB, 2])
        mean = sb("mean", [P, NT])
        rstd = sb("rstd", [P, NT])
        nmr = sb("nmr", [P, NT])
        posi = sb("posi", [P, NT], U32)
        tsi = sb("tsi", [P, E + 1], I32)
        cmask = sb("cmask", [P, B * NC], BF16)
        A32 = sb("A32", [P, NPAIR])
        AP2 = sb("AP2", [P, 2, NPAIR])
        half4 = sb("half4", [P, 2, NQ])
        half = sb("half", [P, 2])
        jv = sb("jv", [P, Q + 1])
        jr = sb("jr", [P, Q])
        FST = sb("FST", [P, 8, 6])
        fs = [sb(f"fs{n}", [P, 8]) for n in range(5)]

        o = [0]

        def carve(region, n, dt=F32):
            a = region[:, o[0]:o[0] + n]
            o[0] += n
            return a if dt == F32 else a.bitcast(dt)

        RC1 = RC[:, 1, :]
        ZERO = carve(RC1, 10 * D)
        ST = carve(RC1, NT * 6).rearrange("p (t k) -> p t k", k=6)
        lt = [carve(RC1, NT) for _ in range(12)]
        ti = carve(RC1, NT, I32)
        OH = carve(RC1, E * NT // 2, BF16)
        PI = carve(RC1, E * NT)
        PA = carve(RC1, E * NT)
        ONE = carve(RC1, E * NT)
        ULT = carve(RC1, P // 2, BF16)
        ONEB = carve(RC1, P // 2, BF16)
        e9 = carve(RC1, E + 1)
        ts9 = carve(RC1, E + 1)
        e8 = [carve(RC1, E) for _ in range(5)]
        e8i = carve(RC1, E, I32)
        WRAW = carve(RC1, (3 * HB + HB) * D).rearrange("p (j d) -> p j d", d=D)

        NS2 = HB * S * (Q + 1)
        o[0] = 0
        EX = carve(RC1, NS2).rearrange("p (b s j) -> p b s j", b=HB, s=S)
        ER = carve(RC1, HB * S * Q).rearrange("p (b s j) -> p b s j", b=HB, s=S)
        KP = carve(RC1, HB * (2 * Q - 1)).rearrange("p (b j) -> p b j", b=HB)
        TA = carve(RC1, HB * (Q + 1) * Q)
        TB = carve(RC1, HB * (Q + 1) * Q)
        D0 = [AR[:, n * BC:(n + 1) * BC] for n in range(2)]
        SX = [AR[:, (2 + n) * BC:(3 + n) * BC] for n in range(2)]

        TB8 = 8
        NB8 = NT // TB8
        XR = RB[:, 0, :].rearrange("p (t d) -> p t d", d=D)
        NEARLY = 9 * CH // (TB8 * D)
        GA = [AR[:, 2 * CH + n * TB8 * D:2 * CH + (n + 1) * TB8 * D] for n in range(NEARLY)]
        GA += [RB[:, 1, n * TB8 * D:(n + 1) * TB8 * D] for n in range(NB8 - NEARLY)]
        GA = [g.rearrange("p (t d) -> p t d", d=D) for g in GA]
        o4 = (NB8 - NEARLY) * TB8 * D
        VV = [RB[:, 1, o4 + n * TB8 * D:o4 + (n + 1) * TB8 * D].rearrange("p (t d) -> p t d", d=D) for n in range(2)]
        PS = ctx.enter_context(nc.psum_tensor("PS", [P, 8, 512], F32))
        ps = [PS[:, n, :] for n in range(8)]

        s_x = [sem(f"x_loaded_{q}") for q in range(QT)]
        s_small = sem("small_loaded")
        s_wraw = sem("weights_loaded")
        s_const = sem("pool_constants")
        s_dve = sem("vector_chain")
        s_act = sem("scalar_chain")
        s_lnv = sem("variance_ready")
        s_lny = sem("rstd_estimate_ready")
        s_nmr = sem("scales_ready")
        s_nrm = sem("xn_quarter_ready_vector")
        s_nra = sem("xn_quarter_ready_scalar")
        s_wsh = sem("w1_high_ready")
        s_sph = sem("sorted_tile_high_ready")
        s_step = sem("pool_steps")
        s_step2 = sem("vector_steps")
        s_basel = sem("base_bias_added")
        s_actl = sem("last_log_ready")
        s_wt = sem("weights_transposed")
        s_wh = sem("weights_high_ready")
        s_wl = sem("weights_low_ready")
        s_vt = sem("vectors_transposed")
        s_vc = sem("vectors_ready")
        s_zero = sem("zero_tile_ready")
        s_fill = sem("sorted_tokens_cleared")
        s_oh = sem("one_hot_ready")
        s_rank = sem("ranks_ready")
        s_pos = sem("positions_ready")
        s_scat = sem("tokens_scattered")
        s_xin = [sem(f"chunk_copied_{s}") for s in range(2)]
        s_xt = [sem(f"chunk_transposed_{s}") for s in range(2)]
        s_hi = [sem(f"chunk_high_ready_{s}") for s in range(2)]
        s_lo = [sem(f"chunk_low_ready_{s}") for s in range(2)]
        s_pr = [[sem(f"projected_{n}_{hb}") for hb in range(HB)] for n in ("dt", "u", "g")]
        s_min = [sem(f"clamped_ready_{hb}") for hb in range(HB)]
        s_dte = [sem(f"dt_bank_read_{hb}") for hb in range(HB)]
        s_ue = [sem(f"u_stored_{hb}") for hb in range(HB)]
        s_ge = [sem(f"z_stored_{hb}") for hb in range(HB)]
        s_exp = [sem(f"exp_ready_{hb}") for hb in range(HB)]
        s_ln = [sem(f"softplus_summed_{hb}") for hb in range(HB)]
        s_sig = sem("gate_piece_ready")
        s_asp = sem("a_softplus_input")
        s_asq = sem("a_softplus_done")
        s_earg = sem("exponents_ready")
        s_eexp = sem("decays_ready")
        s_jv = sem("iotas_ready")
        s_mat = sem("matrices_ready")
        s_w1 = [sem(f"w1_loaded_{s}") for s in range(3)]
        s_w2 = [sem(f"w2_loaded_{s}") for s in range(3)]
        s_ws = sem("w1_split")
        s_b2 = sem("b2_pair_ready")
        s_xs = sem("sorted_tile_loaded")
        s_sp = sem("sorted_tile_split")
        s_tt = sem("sorted_tile_transposed")
        s_xtr = sem("sorted_tile_in_place")
        s_m1 = [sem(f"expert_{n}_hidden") for n in "ab"]
        s_re = [sem(f"expert_{n}_relu") for n in "ab"]
        s_m2 = sem("expert_output_summed")
        s_m2a = sem("first_expert_read")
        s_ysb = sem("expert_output_in_sbuf")
        s_yad = sem("expert_bias_added")
        s_yst = sem("expert_output_stored")
        s_inj = sem("injection_ready")
        s_d0 = sem("decay_row_ready")
        s_scan = sem("states_ready")
        s_yps = sem("pair_output_ready")
        s_yev = sem("pair_output_in_sbuf")
        s_ytr = sem("y_piece_transposed")
        s_gat = [sem(f"expert_outputs_gathered_{n}") for n in range(NB8)]
        s_xr = [sem(f"x_reloaded_{n}") for n in range(NB8)]
        s_po = sem("projection_out_ready")
        s_xa = sem("xn_again_ready")
        s_v = sem("residual_sum_ready")
        s_fv = sem("last_variance_ready")
        s_fy = sem("last_rstd_estimate")
        s_fr = sem("last_scales_ready")
        s_fn = sem("last_normalised")
        s_base = sem("base_ready")
        s_fo = sem("output_ready")
        s_out = [sem(f"output_stored_{n}") for n in range(2)]

        x_v = x.rearrange("b (s p) d -> p (b s) d", p=P)
        out_v = out.rearrange("b (s p) d -> p (b s) d", p=P)
        xs_v = xs_dram.rearrange("(t h p) d -> t p h d", h=FH, p=P)
        ys_v = ys_dram.rearrange("(t h p) d -> t p h d", h=FH, p=P)
        xs_z = xs_dram.rearrange("(p r) d -> p (r d)", p=P)
        ZR = 10
        XSR = ROWS // P
        NZ = -(-XSR // ZR)
        YR = (ROWS - NTOK) // P
        assert ZR < YR <= 2 * ZR
        small = [(vrows[0:2, :], b_x.rearrange("(b p) -> b p", p=P)), (vrows[2:4, :], b_g.rearrange("(b p) -> b p", p=P)),
                 (vrows[4:6, :], b_dt.rearrange("(b p) -> b p", p=P)), (vrows[6:8, :], conv_b.rearrange("(b p) -> b p", p=P)),
                 (vrows[8:8 + E * KB, :], b1.rearrange("e (k p) -> (e k) p", p=P)),
                 (cw[:, :, :], conv_w.rearrange("(b p) o k -> p b (o k)", p=P)),
                 (Araw[:, :, :], A_raw.rearrange("(b p) s -> p b s", p=P)),
                 (Bssm[:, :, :], B_ssm.rearrange("(b p) s -> p b s", p=P)),
                 (Cssm[:, :, :], C_ssm.rearrange("(b p) s -> p b s", p=P)),
                 (lng[:, :], ln_g.rearrange("(o d) -> o d", o=1).broadcast_to([P, D])),
                 (lnb[:, :], ln_b.rearrange("(o d) -> o d", o=1).broadcast_to([P, D])),
                 (bo[:, :], b_out.rearrange("(o d) -> o d", o=1))]
        NSMALL = len(small)

        def gate_cols(n):
            return slice(n * GB * L, (n + 1) * GB * L)

        def expert_bounds(eng):
            eng.wait_ge(s_pos, 1)
            return [0] + [eng.value_load(tsi[0:1, e:e + 1], min_val=e, max_val=MAXT) for e in range(1, E + 1)]

        block = ctx.enter_context(nc.Block())

        @block.sync
        def _(sp):
            sp.sem_inc(s_yst, 16)
            for q in range(QT):
                sp.dma_start(XN[:, q * TQ:(q + 1) * TQ, :], x_v[:, q * TQ:(q + 1) * TQ, :]).then_inc(s_x[q], 16)
            sp.wait_ge(s_zero, 1)
            for n in range(NZ):
                w = min(ZR, XSR - n * ZR) * D
                sp.dma_start(xs_z[:, n * ZR * D:n * ZR * D + w], ZERO[:, 0:w]).then_inc(s_fill, 16)
            sp.dma_start(ys_dram[NTOK:ROWS, :].rearrange("(p r) d -> p (r d)", p=P)[:, 0:ZR * D], ZERO).then_inc(s_fill, 16)
            sp.dma_start(ys_dram[NTOK:ROWS, :].rearrange("(p r) d -> p (r d)", p=P)[:, ZR * D:], ZERO[:, 0:YR * D - ZR * D]
                         ).then_inc(s_fill, 16)
            for k in range(2):
                sp.dma_start(W1RAW[raw_slot(k)], W1[k]).then_inc(s_w1[raw_slot(k)], 16)
            sp.wait_ge(s_nrm, QT)
            sp.wait_ge(s_nra, QT)
            for s in range(2):
                sp.dma_start(xin[s], XN[:, s * TPC:(s + 1) * TPC, :]).then_inc(s_xin[s], 16)
            with sp.Fori(1, NCH // 2) as i:
                for s in range(2):
                    sp.wait_ge(s_xt[s], i)
                    sp.dma_start(xin[s], XN[:, bass.ds((i * 2 + s) * TPC, TPC), :]).then_inc(s_xin[s], 16)

            def load_w1(k):
                sp.dma_start(W1RAW[raw_slot(k)], W1[k % E]).then_inc(s_w1[raw_slot(k)], 16)

            def load_w2(k):
                sp.dma_start(W2S[k % 3], W2[k % E].rearrange("(k p) d -> p k d", p=P)).then_inc(s_w2[k % 3], 16)
                sp.dma_start(b2s[:, k % 3, :], b2[k % E:k % E + 1, :].broadcast_to([P, D])).then_inc(s_w2[k % 3], 16)

            bounds = expert_bounds(sp)
            sp.wait_ge(s_scat, 16 * NT)
            sp.dma_start(XSIN, xs_v[0]).then_inc(s_xs, 16)
            for s in range(2):
                sp.wait_ge(s_xt[s], NCH // 2)
                load_w2(s)
            for hb in range(HB):
                sp.wait_ge(s_exp[hb], NCH)
                sp.wait_ge(s_dte[hb], NCH)
            load_w1(2)
            load_w2(2)
            sp.wait_ge(s_sp, 1)
            sp.dma_start(XSIN, xs_v[1]).then_inc(s_xs, 16)
            w1_before = {1: [3], 2: [4, 5], 3: [6], 4: [7], 5: [8]}
            for g in range(E):
                if 1 <= g < E - 1:
                    sp.wait_ge(s_m2, bounds[g])
                    load_w2(g + 2)
                for k in w1_before.get(g, []):
                    if k == 4:
                        sp.wait_ge(s_earg, 1)
                    if k == 3 or k >= 6:
                        sp.wait_ge(s_ws, k if k == 3 else k - 2)
                    load_w1(k)
                with sp.Fori(bounds[g], bounds[g + 1]) as i:
                    sp.wait_ge(s_sp, i + 2)
                    sp.dma_start(XSIN, xs_v[bass.ds(i + 2, 1)].rearrange("o p h d -> p (o h) d")).then_inc(s_xs, 16)
                    sp.wait_ge(s_yad, i + 1)
                    sp.dma_start(ys_v[bass.ds(i, 1)].rearrange("o p h d -> p (o h) d"), YSB).then_inc(s_yst, 16)

            sp.wait_ge(s_yps, NPAIR)
            sp.wait_ge(s_d0, NPAIR)
            for n in range(NB8):
                sp.dma_start(XR[:, n * TB8:(n + 1) * TB8, :], x_v[:, n * TB8:(n + 1) * TB8, :]).then_inc(s_xr[n], 16)
            for n in range(NB8):
                sp.wait_ge(s_fo, n + 1)
                sp.dma_start(out_v[:, n * TB8:(n + 1) * TB8, :], VV[n % 2]).then_inc(s_out[n % 2], 16)
            for n in range(2):
                sp.wait_ge(s_out[n], 16 * NB8 // 2)

        @block.gpsimd
        def _(pool):
            nc.gpsimd.memset(ZERO, 0.0).then_inc(s_zero, 1)
            nc.gpsimd.iota(jv[:, :], [[1, Q + 1]], base=0, channel_multiplier=0,
                           allow_small_or_imprecise_dtypes=True).then_inc(s_jv, 1)
            nc.gpsimd.iota(jr[:, :], [[-1, Q]], base=Q - 1, channel_multiplier=0,
                           allow_small_or_imprecise_dtypes=True).then_inc(s_jv, 1)
            nc.gpsimd.memset(identity[:, :], 0.0).then_inc(s_const, 1)
            nc.gpsimd.memset(ULT, 1.0).then_inc(s_const, 1)
            nc.gpsimd.memset(cmask[:, :], 1.0).then_inc(s_const, 1)
            pool.wait_ge(s_const, 3)
            nc.gpsimd.affine_select(out=identity[:, :], in_=identity[:, :], compare_op=ALU.not_equal, fill=1.0, base=0,
                                    pattern=[[-1, P]], channel_multiplier=1).then_inc(s_const, 1)
            nc.gpsimd.affine_select(out=ULT, in_=ULT, compare_op=ALU.is_gt, fill=0.0, base=0,
                                    pattern=[[1, P]], channel_multiplier=-1).then_inc(s_const, 1)
            nc.gpsimd.affine_select(out=cmask[:, :].rearrange("p (b c) -> p b c", c=NC),
                                    in_=cmask[:, :].rearrange("p (b c) -> p b c", c=NC), compare_op=ALU.is_gt,
                                    fill=0.0, base=0, pattern=[[0, B], [1, NC]], channel_multiplier=0).then_inc(s_const, 1)

            pool.wait_ge(s_pos, 1)
            pool.wait_ge(s_fill, 16 * (NZ + 2))
            for t in range(NT):
                nc.gpsimd.indirect_dma_start(out=xs_dram, out_offset=bass.IndirectOffsetOnAxis(ap=posi[:, t:t + 1], axis=0),
                                             in_=XN[:, t, :], in_offset=None).then_inc(s_scat, 16)

            def split_tile(i):
                pool.wait_ge(s_xs, (i + 1) * 16)
                if not isinstance(i, int):
                    pool.wait_ge(s_tt, i)
                pool.sem_inc(s_step, 1)
                nc.gpsimd.tensor_copy(XSPLIT[:, 0], XSIN).then_inc(s_sph, 1)
                pool.wait_ge(s_sph, i + 1)
                nc.gpsimd.tensor_tensor(XSPLIT[:, 1], XSIN, XSPLIT[:, 0].bitcast(F32), ALU.subtract).then_inc(s_sp, 1)

            bounds = expert_bounds(pool)
            for j in range(3):
                for hb in range(HB):
                    pool.wait_ge(s_pr[j][hb], NCH)
            split_tile(0)
            for g in range(E):
                pool.wait_ge(s_w2[g % 3], 32 * (g // 3 + 1))
                pool.wait_ge(s_w2[(g + 1) % 3], 32 * ((g + 1) // 3 + 1))
                if g >= 1:
                    pool.wait_ge(s_yad, bounds[g])
                nc.gpsimd.tensor_tensor(b2p[:, :], b2s[:, g % 3, :], b2s[:, (g + 1) % 3, :], ALU.add).then_inc(s_b2, 1)
                pool.wait_ge(s_b2, 2 * g + 1)
                nc.gpsimd.tensor_scalar(b2p[:, :], b2p[:, :], 0.5, 0.0, ALU.mult, ALU.add).then_inc(s_b2, 1)
                pool.wait_ge(s_b2, 2 * g + 2)
                with pool.Fori(bounds[g], bounds[g + 1]) as i:
                    split_tile(i + 1)
                    pool.wait_ge(s_ysb, i + 2)
                    nc.gpsimd.tensor_tensor(YSB, YSB, b2p[:, :].rearrange("p (o d) -> p o d", o=1).broadcast_to([P, FH, D]),
                                            ALU.add).then_inc(s_yad, 1)

            pool.wait_ge(s_yst, bounds[E] * 16 + 16)
            for n in range(NB8):
                if n == 0:
                    pool.wait_ge(s_m2, bounds[E])
                    pool.wait_ge(s_xtr, bounds[E] + 1)
                    pool.sem_inc(s_step, 1)
                    pool.wait_ge(s_mat, 1)
                if n == NEARLY:
                    pool.wait_ge(s_yps, NPAIR)
                for t in range(TB8):
                    nc.gpsimd.indirect_dma_start(out=GA[n][:, t, :], out_offset=None, in_=ys_dram,
                                                 in_offset=bass.IndirectOffsetOnAxis(
                                                     ap=posi[:, n * TB8 + t:n * TB8 + t + 1], axis=0)).then_inc(s_gat[n], 16)
            lnb_b = lnb[:, :].rearrange("p (o d) -> p o d", o=1).broadcast_to([P, TB8, D])
            for n in range(NB8):
                pool.wait_ge(s_gat[n], 16 * TB8)
                pool.wait_ge(s_small, 16 * NSMALL)
                nc.gpsimd.tensor_tensor(GA[n], GA[n], lnb_b, ALU.add).then_inc(s_basel, 1)
                pool.wait_ge(s_basel, n + 1)
                pool.wait_ge(s_xr[n], 16)
                nc.gpsimd.tensor_tensor(GA[n], GA[n], XR[:, n * TB8:(n + 1) * TB8, :], ALU.add).then_inc(s_base, 1)

        @block.scalar
        def _(act):
            act.sem_inc(s_ysb, 1)
            act.dma_start(WRAW[:, 0:HB, :], W_dt.rearrange("(b p) d -> p b d", p=P)).then_inc(s_wraw, 16)
            act.dma_start(WRAW[:, HB:2 * HB, :], W_x.rearrange("(b p) d -> p b d", p=P)).then_inc(s_wraw, 16)
            act.dma_start(WRAW[:, 2 * HB:3 * HB, :], W_g.rearrange("(b p) d -> p b d", p=P)).then_inc(s_wraw, 16)
            act.dma_start(WRAW[:, 3 * HB:4 * HB, :].rearrange("p b d -> p (b d)"), W_out).then_inc(s_wraw, 16)
            for dst, src in small:
                act.dma_start(dst, src, allow_slow_non_contiguous=True).then_inc(s_small, 16)

            nc.scalar.preload_act_table_set("natural_log_exp_and_others")
            def quarter(q):
                act.wait_ge(s_lnv, q + 1)
                c = slice(q * TQ, (q + 1) * TQ)
                nc.scalar.activation(lt[5][:, c], lt[4][:, c], ACT.Ln).then_inc(s_act, 1)
                act.wait_ge(s_act, q + 1)
                nc.scalar.activation(lt[6][:, c], lt[5][:, c], ACT.Exp, scale=-0.5).then_inc(s_lny, 1)

            def normalise(q):
                act.wait_ge(s_nmr, q + 1)
                for t in range((q + 1) * TQ - TA_, (q + 1) * TQ):
                    ins = nc.scalar.activation(XN[:, t, :], XN[:, t, :], ACT.Identity, scale=rstd[:, t:t + 1],
                                               bias=nmr[:, t:t + 1])
                ins.then_inc(s_nra, 1)

            quarter(0)
            for q in range(1, QT):
                quarter(q)
                normalise(q - 1)
            normalise(QT - 1)
            act.wait_ge(s_wt, 4 * HB)
            for n in range(3 * HB):
                nc.scalar.activation(PW[:, 0, n, :], ps[n // 4][:, (n % 4) * P:(n % 4 + 1) * P], ACT.Copy).then_inc(s_wh, 1)
            act.wait_ge(s_asp, 1)
            nc.scalar.activation(sv[:, :, :], sv[:, :, :], ACT.Exp).then_inc(s_asq, 1)
            act.wait_ge(s_asq, 1)
            nc.scalar.activation(sv[:, :, :], sv[:, :, :], ACT.Ln, bias=1.0).then_inc(s_asq, 1)

            def high(s, i):
                act.wait_ge(s_xt[s], i + 1)
                if not isinstance(i, int) or i:
                    act.wait_ge(s_pr[2][HB - 1], i * 2 + (s - 1))
                nc.scalar.activation(xh[s], ps[s], ACT.Copy).then_inc(s_hi[s], 1)

            def evacuate(s, i):
                c = i * 2 + s
                for hb in range(HB):
                    act.wait_ge(s_min[hb], c + 1)
                    nc.scalar.activation(eb[hb], mb[hb], ACT.Exp).then_inc(s_exp[hb], 1)
                    act.wait_ge(s_exp[hb], c + 1)
                    nc.scalar.activation(eb[hb], eb[hb], ACT.Ln, bias=1.0, accum_out=acc1[:, hb, bass.ds(c, 1)]
                                         ).then_inc(s_ln[hb], 1)
                for hb in range(HB):
                    act.wait_ge(s_pr[2][hb], c + 1)
                    nc.scalar.activation(RC[:, hb, bass.ds(c * CH, CH)], ps[6 + hb], ACT.Identity,
                                         bias=bg[:, hb:hb + 1]).then_inc(s_ge[hb], 1)

            act.wait_ge(s_vc, 1)
            act.wait_ge(s_pos, 1)
            act.wait_ge(s_fill, 16 * (NZ + 2))
            high(0, 0)
            high(1, 0)
            evacuate(0, 0)
            high(0, 1)
            evacuate(1, 0)
            with act.Fori(1, NCH // 2 - 1) as i:
                high(1, i)
                evacuate(0, i)
                high(0, i + 1)
                evacuate(1, i)
            i = NCH // 2 - 1
            high(1, i)
            evacuate(0, i)
            evacuate(1, i)

            NPIECE = HB * NGATE
            RCF = RC[:, :, :].rearrange("p b t -> p (b t)")
            nc.scalar.preload_act_table_set("sigmoid_and_others")

            def gate_piece(n):
                z = RCF[:, bass.ds(n * (GB * L), GB * L)]
                nc.scalar.activation(z, z, ACT.Sigmoid, scale=-1.0).then_inc(s_sig, 1)

            def place_tile(i):
                act.wait_ge(s_tt, i + 1)
                nc.scalar.activation(XT, ps[4], ACT.Copy).then_inc(s_xtr, 1)

            bounds = expert_bounds(act)
            for j in range(3):
                for hb in range(HB):
                    act.wait_ge(s_pr[j][hb], NCH)
            for k in range(2):
                act.wait_ge(s_w1[raw_slot(k)], 16)
                nc.scalar.activation(W1h[k], W1RAW[raw_slot(k)], ACT.Copy).then_inc(s_wsh, 1)
            for hb in range(HB):
                act.wait_ge(s_ge[hb], NCH)
            for hb in range(HB):
                act.wait_ge(s_dte[hb], NCH)
            place_tile(0)
            for g in range(E):
                if g == 2:
                    with act.If(bounds[2] < NPIECE):
                        with act.Fori(bounds[2], NPIECE) as n:
                            gate_piece(n)
                    act.wait_ge(s_earg, 1)
                    nc.scalar.activation(EX, EX, ACT.Exp)
                    nc.scalar.activation(ER, ER, ACT.Exp).then_inc(s_eexp, 1)
                    nc.scalar.preload_act_table_set("sigmoid_and_others")
                with act.Fori(bounds[g], bounds[g + 1]) as i:
                    for n in range(2):
                        e = (g + n) % E
                        for k in range(KB):
                            if k % 2 == 0:
                                act.wait_ge(s_m1[n], i * KB + (k + 2))
                            nc.scalar.activation(HID[n][:, k, :], ps[2 * n + k // 2][:, (k % 2) * FT:(k % 2 + 1) * FT],
                                                 ACT.Relu, bias=B1C[:, e, k:k + 1]).then_inc(s_re[n], 1)
                    place_tile(i + 1)
                    if g < 2:
                        with act.If(i < NPIECE):
                            gate_piece(nc.s_assert_within(i, 0, NPIECE - 1, skip_runtime_bounds_check_because="the If"))
                    act.wait_ge(s_m2, i + 1)
                    act.wait_ge(s_yst, i * 16 + 16)
                    for h in range(FH):
                        ins = nc.scalar.activation(YSB[:, h, :], ps[5 + h][:, 0:D], ACT.Copy, scale=0.5)
                    ins.then_inc(s_ysb, 1)

            for r in range(NPAIR):
                hb, rp = divmod(r, PPB)
                act.wait_ge(s_yps, r + 1)
                nc.scalar.activation(UT[hb][:, 2 * rp:2 * rp + 2, :],
                                     PS[:, 2 + 2 * (r % 3):4 + 2 * (r % 3), 0:BC], ACT.Copy).then_inc(s_yev, 1)

            def again(n):
                act.wait_ge(s_xr[n], 16)
                if n >= 2:
                    act.wait_ge(s_out[n % 2], 16 * (n // 2))
                for t in range(TB8):
                    ti_ = n * TB8 + t
                    ins = nc.scalar.activation(VV[n % 2][:, t, :], XR[:, ti_, :], ACT.Identity, scale=rstd[:, ti_:ti_ + 1],
                                               bias=nmr[:, ti_:ti_ + 1])
                ins.then_inc(s_xa, 1)

            nc.scalar.preload_act_table_set("natural_log_exp_and_others")
            again(0)
            for n in range(NB8):
                act.wait_ge(s_fv, n + 1)
                nc.scalar.activation(fs[2][:, :], fs[1][:, :], ACT.Ln).then_inc(s_actl, 1)
                act.wait_ge(s_actl, n + 1)
                nc.scalar.activation(fs[3][:, :], fs[2][:, :], ACT.Exp, scale=-0.5).then_inc(s_fy, 1)
                if n + 1 < NB8:
                    again(n + 1)
                act.wait_ge(s_fr, n + 1)
                for t in range(TB8):
                    ins = nc.scalar.activation(VV[n % 2][:, t, :], VV[n % 2][:, t, :], ACT.Identity,
                                               scale=fs[3][:, t:t + 1], bias=fs[4][:, t:t + 1])
                ins.then_inc(s_fn, 1)

        @block.vector
        def _(dve):
            count = [0]

            def link(ins):
                count[0] += 1
                ins.then_inc(s_dve, 1)
                dve.wait_ge(s_dve, count[0])

            V = nc.vector
            V.memset(ONE, 1.0)
            link(V.memset(ONEB, 1.0))
            V.memset(ones1[:, :], 1.0)
            V.memset(e9, 0.0)
            link(V.memset(ts9, 0.0))

            def refine(v, y, a, b_):
                link(V.tensor_tensor(a, y, y, ALU.mult))
                link(V.tensor_tensor(b_, a, v, ALU.mult))
                link(V.tensor_scalar(a, b_, -0.5, 1.5, ALU.mult, ALU.add))
                link(V.tensor_tensor(y, y, a, ALU.mult))

            def variance(st, m, v, t1, t2):
                V.tensor_tensor(m, st[:, :, 1], st[:, :, 4], ALU.add)
                V.tensor_tensor(t1, st[:, :, 1], st[:, :, 4], ALU.subtract)
                link(V.tensor_tensor(v, st[:, :, 2], st[:, :, 5], ALU.add))
                link(V.scalar_tensor_tensor(t2, t1, 0.25, t1, ALU.mult, ALU.mult))
                V.tensor_scalar(m, m, 0.5, None, ALU.mult)
                link(V.scalar_tensor_tensor(t1, v, 1.0 / D, t2, ALU.mult, ALU.add))

            def statistics(q):
                c = slice(q * TQ, (q + 1) * TQ)
                dve.wait_ge(s_x[q], 16)
                for t in range(q * TQ, (q + 1) * TQ):
                    ins = V.bn_stats(ST[:, t, :], XN[:, t, :])
                link(ins)
                variance(ST[:, c, :], mean[:, c], lt[3][:, c], lt[1][:, c], lt[2][:, c])
                V.tensor_scalar(lt[4][:, c], lt[1][:, c], EPS, None, ALU.add).then_inc(s_lnv, 1)

            def normalise(q):
                c = slice(q * TQ, (q + 1) * TQ)
                dve.wait_ge(s_lny, q + 1)
                link(V.tensor_copy(rstd[:, c], lt[6][:, c]))
                refine(lt[4][:, c], rstd[:, c], lt[7][:, c], lt[8][:, c])
                V.scalar_tensor_tensor(nmr[:, c], mean[:, c], -1.0, rstd[:, c], ALU.mult, ALU.mult).then_inc(s_nmr, 1)
                for t in range(q * TQ, (q + 1) * TQ - TA_):
                    ins = V.tensor_scalar(XN[:, t, :], XN[:, t, :], mean[:, t:t + 1], rstd[:, t:t + 1],
                                          ALU.subtract, ALU.mult)
                ins.then_inc(s_nrm, 1)

            statistics(0)
            for q in range(1, QT):
                statistics(q)
                normalise(q - 1)
            normalise(QT - 1)
            dve.wait_ge(s_nrm, QT)
            dve.wait_ge(s_nra, QT)

            s_, a_, f_, g_, h_, w_ = lt[0], lt[1], lt[2], lt[3], lt[5], lt[7]
            link(V.tensor_tensor(s_, XN[:, :, 0], XN[:, :, 1], ALU.add))
            link(V.scalar_tensor_tensor(a_, s_, -1.0, s_, ALU.mult, ALU.max))
            link(V.tensor_copy(ti, a_))
            link(V.tensor_copy(f_, ti))
            link(V.tensor_tensor(g_, f_, a_, ALU.is_gt))
            link(V.tensor_tensor(f_, f_, g_, ALU.subtract))
            for _ in range(2):
                link(V.tensor_scalar(g_, f_, float(E), -float(E), ALU.is_ge, ALU.mult))
                link(V.tensor_tensor(f_, f_, g_, ALU.add))
            link(V.tensor_scalar(w_, f_, -2.0, float(E), ALU.mult, ALU.add))
            link(V.scalar_tensor_tensor(h_, s_, 0.0, w_, ALU.is_lt, ALU.mult))
            link(V.tensor_tensor(h_, h_, f_, ALU.add))
            link(V.tensor_scalar(g_, h_, float(E), -float(E), ALU.is_ge, ALU.mult))
            link(V.tensor_tensor(h_, h_, g_, ALU.add))
            for e in range(E):
                ins = V.tensor_scalar(OH[:, e * NT:(e + 1) * NT], h_, float(e), None, ALU.is_equal)
            ins.then_inc(s_oh, 1)
            dve.wait_ge(s_rank, 2)
            link(V.tensor_tensor_scan(PI, ONE, ps[7], 0.0, ALU.mult, ALU.add))
            PI3 = PI.rearrange("p (e t) -> p e t", e=E)
            link(V.tensor_copy(e9[:, 1:E + 1], PI3[:, :, NT - 1]))
            cnt, qf, gt, nt, pad = e8
            link(V.tensor_tensor(cnt, e9[:, 1:E + 1], e9[:, 0:E], ALU.subtract))
            link(V.tensor_scalar(qf, cnt, float(FT - 1), 1.0 / FT, ALU.add, ALU.mult))
            link(V.tensor_copy(e8i, qf))
            link(V.tensor_copy(nt, e8i))
            link(V.tensor_tensor(gt, nt, qf, ALU.is_gt))
            link(V.tensor_tensor(nt, nt, gt, ALU.subtract))
            link(V.tensor_scalar(nt, nt, 1.0, None, ALU.max))
            link(V.tensor_tensor_scan(ts9[:, 1:E + 1], ONE[:, 0:E], nt, 0.0, ALU.mult, ALU.add))
            V.tensor_copy(tsi[:, :], ts9)
            link(V.scalar_tensor_tensor(pad, ts9[:, 0:E], float(FT), e9[:, 0:E], ALU.mult, ALU.subtract))
            link(V.tensor_tensor(PA, ps[6], PI, ALU.add))
            link(V.tensor_tensor(PA, ps[7], PA, ALU.subtract))
            PA3 = PA.rearrange("p (e t) -> p e t", e=E)
            link(V.tensor_tensor(PA3, pad.rearrange("p (e o) -> p e o", o=1).broadcast_to([P, E, NT]), PA3, ALU.subtract))
            link(V.tensor_tensor(PA, PA, OH, ALU.mult))
            link(V.tensor_reduce(lt[10], PA.rearrange("p (e t) -> p t e", e=E), AX_X, ALU.add))
            V.tensor_copy(posi[:, :], lt[10]).then_inc(s_pos, 1)

            dve.wait_ge(s_wh, 3 * HB)
            for n in range(3 * HB):
                ins = V.tensor_tensor(PW[:, 1, n, :], ps[n // 4][:, (n % 4) * P:(n % 4 + 1) * P],
                                      PW[:, 0, n, :].bitcast(F32), ALU.subtract)
            ins.then_inc(s_wl, 1)
            V.tensor_copy(WoT[:, :, :].rearrange("p b d -> p (b d)"), ps[1][:, 2 * P:4 * P]).then_inc(s_wl, 1)
            dve.wait_ge(s_vt, 1)
            link(V.tensor_copy(VC[:, :], ps[2][:, 0:8 + E * KB]))
            V.tensor_scalar(cwn[:, :, :].rearrange("p b k -> p (b k)"), cw[:, :, :].rearrange("p b k -> p (b k)"),
                            -1.0, None, ALU.mult)
            V.tensor_scalar(cbn[:, :], cb, -1.0, None, ALU.mult)
            V.tensor_scalar(sv[:, :, :], Araw[:, :, :], SOFT, None, ALU.min).then_inc(s_asp, 1)
            link(V.tensor_scalar(sv2[:, :, :], Araw[:, :, :], SOFT, None, ALU.subtract))
            link(V.tensor_scalar(sv2[:, :, :], sv2[:, :, :], 0.0, None, ALU.max))
            V.tensor_scalar(cwn[:, :, 1], cwn[:, :, 1], 1.0, None, ALU.add).then_inc(s_vc, 1)
            dve.wait_ge(s_vc, 1)

            def low(s, i):
                dve.wait_ge(s_hi[s], i + 1)
                V.tensor_tensor(xl[s], ps[s], xh[s].bitcast(F32), ALU.subtract).then_inc(s_lo[s], 1)

            def evacuate(s, i):
                c = i * 2 + s
                for hb in range(HB):
                    dve.wait_ge(s_pr[0][hb], c + 1)
                    if not isinstance(c, int) or c:
                        dve.wait_ge(s_exp[hb], c)
                    V.tensor_scalar(mb[hb], ps[2 + hb], bdt[:, hb:hb + 1], SOFT, ALU.add, ALU.min
                                    ).then_inc(s_min[hb], 1)
                    dve.wait_ge(s_min[hb], c + 1)
                    V.scalar_tensor_tensor(junk, ps[2 + hb], bdt[:, hb:hb + 1], mb[hb], ALU.add, ALU.subtract,
                                           accum_out=acc2[:, hb, bass.ds(c, 1)]).then_inc(s_dte[hb], 1)
                for hb in range(HB):
                    dve.wait_ge(s_pr[1][hb], c + 1)
                    V.tensor_scalar(RB[:, hb, bass.ds(c * CH, CH)], ps[4 + hb], bx[:, hb:hb + 1], None, ALU.add
                                    ).then_inc(s_ue[hb], 1)

            low(0, 0)
            low(1, 0)
            evacuate(0, 0)
            low(0, 1)
            evacuate(1, 0)
            with dve.Fori(1, NCH // 2 - 1) as i:
                low(1, i)
                evacuate(0, i)
                low(0, i + 1)
                evacuate(1, i)
            i = NCH // 2 - 1
            low(1, i)
            evacuate(0, i)
            evacuate(1, i)

            bounds = expert_bounds(dve)
            for hb in range(HB):
                dve.wait_ge(s_dte[hb], NCH)
                dve.wait_ge(s_ln[hb], NCH)
                dve.wait_ge(s_ue[hb], NCH)
            V.tensor_reduce(dtv[:, :, 0], acc1[:, :, :], AX_X, ALU.add)
            link(V.tensor_reduce(dtv[:, :, 1], acc2[:, :, :], AX_X, ALU.add))
            link(V.tensor_tensor(dtv[:, :, 0], dtv[:, :, 0], dtv[:, :, 1], ALU.add))
            link(V.tensor_scalar(dtv[:, :, 0], dtv[:, :, 0], 1.0 / NTOK, DT_MIN, ALU.mult, ALU.max))
            link(V.tensor_scalar(dtv[:, :, 0], dtv[:, :, 0], DT_MAX, None, ALU.min))
            dve.wait_ge(s_asq, 2)
            link(V.tensor_tensor(Aneg[:, :, :], sv[:, :, :], sv2[:, :, :], ALU.add))
            link(V.tensor_scalar(Aneg[:, :, :], Aneg[:, :, :], -1.0, None, ALU.mult))
            for hb in range(HB):
                link(V.tensor_scalar(aval[:, hb, :], Aneg[:, hb, :], dtv[:, hb, 0:1], None, ALU.mult))

            def split_low(k):
                V.tensor_tensor(W1l[k % 3], W1RAW[raw_slot(k)], W1h[k % 3].bitcast(F32), ALU.subtract).then_inc(s_ws, 1)

            def split_weights(k):
                dve.wait_ge(s_w1[raw_slot(k)], 16 * raw_loads(k))
                if k >= 3:
                    dve.wait_ge(s_m2, bounds[k - 2])
                dve.sem_inc(s_step2, 1)
                V.tensor_copy(W1h[k % 3], W1RAW[raw_slot(k)]).then_inc(s_wsh, 1)
                dve.wait_ge(s_wsh, k + 1)
                split_low(k)

            for k in range(2):
                dve.wait_ge(s_wsh, k + 1)
                split_low(k)
            dve.wait_ge(s_ws, 2)

            for hb in range(HB):
                for n in range(NGATE):
                    c = gate_cols(n)
                    u, z = RB[:, hb, c], RC[:, hb, c]
                    u3 = u.rearrange("p (b l) -> p b l", l=L)
                    t3 = TG.rearrange("p (b l) -> p b l", l=L)
                    link(V.tensor_scalar(TG, u, cwn[:, hb, 1:2], cbn[:, hb:hb + 1], ALU.mult, ALU.add))
                    link(V.scalar_tensor_tensor(t3[:, :, 1:L], u3[:, :, 0:L - 1], cwn[:, hb, 0:1], t3[:, :, 1:L],
                                                ALU.mult, ALU.add))
                    link(V.scalar_tensor_tensor(t3[:, :, 0:L - 1], u3[:, :, 1:L], cwn[:, hb, 2:3], t3[:, :, 0:L - 1],
                                                ALU.mult, ALU.add))
                    dve.wait_ge(s_sig, hb * NGATE + n + 1)
                    link(V.tensor_tensor(TG, TG, z, ALU.mult))
                    link(V.tensor_tensor(z, u, TG, ALU.subtract))
                    if hb == 0 and n == 0:
                        dve.wait_ge(s_scat, 16 * NT)
                        dve.wait_ge(s_xin[0], 16 * NCH // 2)
                        dve.wait_ge(s_xin[1], 16 * NCH // 2)
                    w = GB * NC
                    link(V.transpose(UT[hb][:, :, n * w:(n + 1) * w].rearrange("p g c -> p c g"),
                                     z.rearrange("p (c i) -> p c i", i=Q)))
                    if hb == 0 and n == 0:
                        split_weights(2)

            dve.wait_ge(s_jv, 2)
            av = aval[:, :, :].rearrange("p b (s o) -> p b s o", o=1)
            for hb in range(HB):
                V.tensor_tensor(EX[:, hb], av[:, hb].broadcast_to([P, S, Q + 1]),
                                jv[:, :].rearrange("p (o j) -> p o j", o=1).broadcast_to([P, S, Q + 1]), ALU.mult)
                ins = V.tensor_tensor(ER[:, hb], av[:, hb].broadcast_to([P, S, Q]),
                                      jr[:, :].rearrange("p (o j) -> p o j", o=1).broadcast_to([P, S, Q]), ALU.mult)
            ins.then_inc(s_earg, 1)
            V.memset(INTRA.rearrange("p g m -> p (g m)"), 0.0)
            V.memset(INJ.rearrange("p g m -> p (g m)"), 0.0)
            V.memset(KP.rearrange("p b j -> p (b j)"), 0.0)
            V.memset(READ.rearrange("p g m -> p (g m)"), 0.0)
            dve.wait_ge(s_const, 6)
            link(V.tensor_reduce(half4[:, :, :], identity[:, :].rearrange("p (q h s) -> p h q s", q=NQ, h=2), AX_X, ALU.add))
            link(V.tensor_reduce(half[:, :], half4[:, :, :], AX_X, ALU.add))
            for k in range(3, E + 1):
                split_weights(k)
            dve.wait_ge(s_eexp, 1)
            V.tensor_scalar(sv[:, :, :], EX[:, :, :, 1], -1.0, None, ALU.add)
            link(V.tensor_scalar(sv2[:, :, :], Aneg[:, :, :], 1e-6, None, ALU.add))
            link(V.reciprocal(sv2[:, :, :], sv2[:, :, :]))
            link(V.tensor_tensor(sv[:, :, :], sv[:, :, :], sv2[:, :, :], ALU.mult))
            link(V.tensor_tensor(sv[:, :, :], sv[:, :, :], Bssm[:, :, :], ALU.mult))
            link(V.tensor_tensor(sv2[:, :, :], sv[:, :, :], Cssm[:, :, :], ALU.mult))
            KT = TA[:, 0:HB * Q * S].rearrange("p (b j s) -> p b j s", b=HB, s=S)
            for hb in range(HB):
                ins = V.tensor_tensor(KT[:, hb], EX[:, hb, :, 0:Q].rearrange("p s j -> p j s"),
                                      sv2[:, hb, :].rearrange("p (o s) -> p o s", o=1).broadcast_to([P, Q, S]), ALU.mult)
            link(ins)
            for hb in range(HB):
                ins = V.tensor_reduce(KP[:, hb, Q - 1:2 * Q - 1], KT[:, hb], AX_X, ALU.add)
            link(ins)
            TO = TA[:, 0:HB * Q * Q].rearrange("p (b i j) -> p b i j", b=HB, j=Q)
            TT = TB[:, 0:HB * Q * Q].rearrange("p (b g i) -> p b g i", b=HB, i=Q)
            for j in range(Q):
                ins = V.tensor_copy(TO[:, :, :, j], KP[:, :, Q - 1 - j:2 * Q - 1 - j])
            link(ins)
            link(V.transpose(TB[:, 0:HB * Q * Q].rearrange("p (b g i) -> p b i g", b=HB, i=Q), TO))
            IN5 = RB[:, 0, :].rearrange("p (b g q i) -> p b g q i", b=HB, q=NQ, i=Q)
            for q in range(NQ):
                r = slice(Q * q, Q * q + Q)
                for hb in range(HB):
                    ins = V.tensor_copy(IN5[r, hb, :, q, :], TT[r, hb])
            link(ins)
            IE = TA[:, 0:HB * S * Q].rearrange("p (b s j) -> p b s j", b=HB, s=S)
            IT = TB[:, 0:HB * S * Q].rearrange("p (b g s) -> p b g s", b=HB, s=S)
            for hb in range(HB):
                ins = V.tensor_tensor(IE[:, hb], ER[:, hb],
                                      sv[:, hb, :].rearrange("p (s o) -> p s o", o=1).broadcast_to([P, S, Q]), ALU.mult)
            link(ins)
            link(V.transpose(TB[:, 0:HB * S * Q].rearrange("p (b g s) -> p b s g", b=HB, s=S), IE))
            INJ5 = INJ.rearrange("p (b g) (q s) -> p b g q s", b=HB, q=NQ)
            for q in range(NQ):
                r = slice(Q * q, Q * q + Q)
                for hb in range(HB):
                    ins = V.tensor_copy(INJ5[r, hb, :, q, :], IT[r, hb])
            link(ins)
            RD = TA.rearrange("p (b i x) -> p b i x", b=HB, x=Q)
            for hb in range(HB):
                for rep in range(Q // S):
                    V.tensor_tensor(RD[:, hb, 0:Q, rep * S:(rep + 1) * S],
                                    EX[:, hb, :, 1:Q + 1].rearrange("p s j -> p j s"),
                                    Cssm[:, hb, :].rearrange("p (o s) -> p o s", o=1).broadcast_to([P, Q, S]), ALU.mult)
                    ins = V.tensor_copy(RD[:, hb, Q, rep * S:(rep + 1) * S], EX[:, hb, :, Q])
            link(ins)
            for hb in range(HB):
                ins = V.transpose(TB.rearrange("p (b g i) -> p b i g", b=HB, i=Q + 1)[:, hb],
                                  RD[:, hb])
            link(ins)
            RT = TB.rearrange("p (r a i) -> p a r i", a=2, i=Q + 1)
            for ab in range(2):
                for q in range(NQ):
                    src = slice(Q * q, Q * (q + 1))
                    dst = slice(Q * (2 * ab + q // 2), Q * (2 * ab + q // 2 + 1))
                    V.tensor_scalar(READ[dst, :, q * Q:(q + 1) * Q], RT[src, ab, :, 0:Q], half[src, q % 2:q % 2 + 1], None,
                                    ALU.mult)
                    ins = V.tensor_scalar(AP2[dst, q % 2, :], RT[src, ab, :, Q], half[src, q % 2:q % 2 + 1], None, ALU.mult)
            link(ins)
            link(V.tensor_tensor(A32[:, :], AP2[:, 0, :], AP2[:, 1, :], ALU.add))
            dve.wait_ge(s_re[0], bounds[E] * KB)
            dve.wait_ge(s_yst, bounds[E] * 16 + 16)
            for n in range(2):
                ins = V.memset(ps[n][:, 0:BC].rearrange("p (b c) -> p b c", c=NC)[:, :, 0], 0.0)
            ins.then_inc(s_mat, 1)

            def y_pieces(hb):
                dve.wait_ge(s_yev, (hb + 1) * PPB)
                for n in range(NQP):
                    w = BC // NQP
                    link_(V.transpose(YT[hb][:, n * w * Q:(n + 1) * w * Q].rearrange("p (c i) -> p c i", i=Q),
                                      UT[hb][:, :, n * w:(n + 1) * w].rearrange("p g c -> p c g")))

            def link_(ins):
                ins.then_inc(s_ytr, 1)

            NQP = 4
            dve.wait_ge(s_m2, bounds[E])
            for r in range(NPAIR):
                if r >= 2:
                    dve.wait_ge(s_yps, r - 1)
                V.tensor_scalar(D0[r % 2], cmask[:, :], A32[:, r:r + 1], None, ALU.mult).then_inc(s_d0, 1)
                dve.wait_ge(s_d0, r + 1)
                dve.wait_ge(s_inj, r + 1)
                V.tensor_tensor_scan(SX[r % 2], D0[r % 2], ps[r % 2][:, 0:BC], 0.0, ALU.mult, ALU.add).then_inc(s_scan, 1)
                if r == PPB + 1:
                    y_pieces(0)
            y_pieces(1)

            lng_b = lng[:, :].rearrange("p (o d) -> p o d", o=1).broadcast_to([P, TB8, D])

            def sums(n):
                dve.wait_ge(s_xa, n + 1)
                vv = VV[n % 2]
                for j in range(2):
                    dve.wait_ge(s_po, 2 * n + j + 1)
                    half = vv[:, j * 4:(j + 1) * 4, :]
                    ins = V.tensor_tensor(half, ps[4 + (2 * n + j) % 4].rearrange("p (t d) -> p t d", d=D), half, ALU.add)
                    ins.then_inc(s_v, 1)
                dve.wait_ge(s_v, 2 * n + 2)
                for t in range(TB8):
                    ins = V.bn_stats(FST[:, t, :], vv[:, t, :])
                link(ins)
                variance(FST[:, :, :], fs[0][:, :], fs[1][:, :], fs[2][:, :], fs[4][:, :])
                V.tensor_scalar(fs[1][:, :], fs[2][:, :], EPS, None, ALU.add).then_inc(s_fv, 1)

            for n in range(NB8):
                vv = VV[n % 2]
                if n >= 1:
                    dve.wait_ge(s_fn, n)
                sums(n)
                dve.wait_ge(s_fy, n + 1)
                refine(fs[1][:, :], fs[3][:, :], fs[2][:, :], fs[4][:, :])
                V.scalar_tensor_tensor(fs[4][:, :], fs[0][:, :], -1.0, fs[3][:, :], ALU.mult, ALU.mult).then_inc(s_fr, 1)
                dve.wait_ge(s_fn, n + 1)
                link(V.tensor_tensor(vv, vv, lng_b, ALU.mult))
                dve.wait_ge(s_base, n + 1)
                V.tensor_tensor(vv, vv, GA[n], ALU.add).then_inc(s_fo, 1)

        @block.tensor
        def _(pe):
            T = nc.tensor
            pe.wait_ge(s_const, 6)
            pe.wait_ge(s_wraw, 64)
            for n in range(4 * HB):
                T.transpose(ps[n // 4][:, (n % 4) * P:(n % 4 + 1) * P], WRAW[:, n, :], identity[:, :]).then_inc(s_wt, 1)
            pe.wait_ge(s_small, 16 * NSMALL)
            R = 8 + E * KB
            T.transpose(ps[2][:, 0:R], vrows[:, :], identity[0:R, 0:R]).then_inc(s_vt, 1)
            pe.wait_ge(s_oh, 1)
            T.matmul(ps[6], ULT, OH, start=True, stop=True).then_inc(s_rank, 1)
            T.matmul(ps[7], ONEB, OH, start=True, stop=True).then_inc(s_rank, 1)

            def transpose_chunk(s, i):
                pe.wait_ge(s_xin[s], (i + 1) * 16)
                if not isinstance(i, int) or i:
                    pe.wait_ge(s_lo[s], i)
                for t in range(TPC):
                    ins = T.transpose(ps[s][:, t * P:(t + 1) * P], xin[s][:, t, :], identity[:, :])
                ins.then_inc(s_xt[s], 1)

            def project(s, i):
                c = i * 2 + s
                pe.wait_ge(s_lo[s], i + 1)
                for j in range(3):
                    free = (s_dte, s_ue, s_ge)[j]
                    for hb in range(HB):
                        if not isinstance(c, int) or c:
                            pe.wait_ge(free[hb], c)
                        n, bank = j * HB + hb, ps[2 + 2 * j + hb]
                        T.matmul(bank, PW[:, 0, n, :], xh[s], start=True, stop=False)
                        T.matmul(bank, PW[:, 0, n, :], xl[s], start=False, stop=False)
                        T.matmul(bank, PW[:, 1, n, :], xh[s], start=False, stop=True).then_inc(s_pr[j][hb], 1)

            pe.wait_ge(s_wl, 2)
            pe.wait_ge(s_vc, 1)
            pe.wait_ge(s_pos, 1)
            transpose_chunk(0, 0)
            transpose_chunk(1, 0)
            project(0, 0)
            transpose_chunk(0, 1)
            project(1, 0)
            with pe.Fori(1, NCH // 2 - 1) as i:
                transpose_chunk(1, i)
                project(0, i)
                transpose_chunk(0, i + 1)
                project(1, i)
            i = NCH // 2 - 1
            transpose_chunk(1, i)
            project(0, i)
            project(1, i)

            def transpose_tile(i):
                pe.wait_ge(s_sp, i + 1)
                for v in range(2):
                    for h in range(FH):
                        ins = T.transpose(ps[4][:, (v * FH + h) * P:(v * FH + h + 1) * P],
                                          XSPLIT[:, v, h, :].bitcast(F32), identity[:, :])
                ins.then_inc(s_tt, 1)

            bounds = expert_bounds(pe)
            for hb in range(HB):
                for f in (s_dte, s_ue, s_ge):
                    pe.wait_ge(f[hb], NCH)
            transpose_tile(0)
            for g in range(E):
                pe.wait_ge(s_ws, min(g + 2, E + 1))
                pe.wait_ge(s_w2[g % 3], 32 * (g // 3 + 1))
                pe.wait_ge(s_w2[(g + 1) % 3], 32 * ((g + 1) // 3 + 1))
                with pe.Fori(bounds[g], bounds[g + 1]) as i:
                    pe.wait_ge(s_xtr, i + 1)
                    for n in range(2):
                        slot = (g + n) % 3
                        for k in range(KB):
                            bank = ps[2 * n + k // 2][:, (k % 2) * FT:(k % 2 + 1) * FT]
                            w = slice(k * P, (k + 1) * P)
                            T.matmul(bank, W1h[slot][:, w], XT[:, 0:FT], start=True, stop=False)
                            T.matmul(bank, W1h[slot][:, w], XT[:, FT:2 * FT], start=False, stop=False)
                            T.matmul(bank, W1l[slot][:, w], XT[:, 0:FT], start=False, stop=True).then_inc(s_m1[n], 1)
                    transpose_tile(i + 1)
                    pe.wait_ge(s_ysb, i + 1)
                    for n in range(2):
                        slot = (g + n) % 3
                        for k in range(KB):
                            pe.wait_ge(s_re[n], i * KB + (k + 1))
                            for h in range(FH):
                                ins = T.matmul(ps[5 + h][:, 0:D], HID[n][:, k, h * P:(h + 1) * P], W2S[slot][:, k, :],
                                               start=(n == 0 and k == 0), stop=(n == 1 and k == KB - 1))
                    ins.then_inc(s_m2, 1)

            pe.wait_ge(s_mat, 1)
            pe.wait_ge(s_xtr, bounds[E] + 1)
            pe.wait_ge(s_ysb, bounds[E] + 1)

            def inject(r):
                hb, rp = divmod(r, PPB)
                if r >= 2:
                    pe.wait_ge(s_scan, r - 1)
                for ab in range(2):
                    g = 2 * rp + ab
                    u = UT[hb][:, g, :].rearrange("p (b c) -> p b c", c=NC)[:, :, 0:NC - 1]
                    dst = ps[r % 2][64 * ab:64 * ab + 64, 0:BC].rearrange("p (b c) -> p b c", c=NC)[:, :, 1:NC]
                    ins = T.matmul(dst, INJ[:, hb * NG + g, :], u, start=True, stop=True)
                ins.then_inc(s_inj, 1)

            inject(0)
            for r in range(NPAIR):
                hb, rp = divmod(r, PPB)
                if r >= 3:
                    pe.wait_ge(s_yev, r - 2)
                if r + 1 < NPAIR:
                    inject(r + 1)
                banks = [ps[2 + 2 * (r % 3) + ab][:, 0:BC] for ab in range(2)]
                for ab in range(2):
                    g = 2 * rp + ab
                    T.matmul(banks[ab], INTRA[:, hb * NG + g, :], UT[hb][:, g, :], start=True, stop=False)
                pe.wait_ge(s_scan, r + 1)
                for ab in range(2):
                    rows = slice(64 * ab, 64 * ab + 64)
                    ins = T.matmul(banks[ab], READ[rows, r, :], SX[r % 2][rows, :], start=False, stop=True)
                ins.then_inc(s_yps, 1)

            pe.wait_ge(s_yev, NPAIR)
            NQP = 4
            for n in range(NT // 4):
                pe.wait_ge(s_ytr, NQP + n * NQP // (NT // 4) + 1)
                if n >= 4:
                    pe.wait_ge(s_v, n - 3)
                for t in range(4):
                    tt = 4 * n + t
                    dst = ps[4 + n % 4][:, t * D:(t + 1) * D]
                    for hb in range(HB):
                        T.matmul(dst, YT[hb][:, tt * P:(tt + 1) * P], WoT[:, hb, :], start=(hb == 0), stop=False)
                    ins = T.matmul(dst, ones1[:, :], bo[:, :], start=False, stop=True)
                ins.then_inc(s_po, 1)


_INS = ['x', 'W_x', 'b_x', 'W_g', 'b_g', 'conv_w', 'conv_b', 'A_raw', 'B_ssm', 'C_ssm', 'W_dt', 'b_dt', 'W_out', 'b_out',
        'ln_g', 'ln_b']
_INS = ['L0_attn_' + n for n in _INS] + ['L0_ffn_' + n for n in ('W1', 'b1', 'W2', 'b2')]
_OUTS = [((32, 256, 128), 'float32')]


def kernel(**inputs):
    import numpy as _np
    import concourse.bacc as _bacc
    from concourse import mybir as _mybir
    from concourse.bass_utils import run_bass_kernel_spmd as _run

    nc = _bacc.Bacc("TRN2", target_bir_lowering=False, num_devices=1, dynamic_dma_scratch_size=8192)
    arrays, args = {}, []
    for name in _INS:
        a = _np.ascontiguousarray(inputs[name])
        arrays[f"in_{name}_dram"] = a
        args.append(nc.dram_tensor(f"in_{name}_dram", a.shape, _mybir.dt.from_np(a.dtype), kind="ExternalInput").ap())
    for i, (shape, dtype) in enumerate(_OUTS):
        dt = _mybir.dt.from_np(_np.dtype(dtype))
        args.append(nc.dram_tensor(f"out_{i}_dram", shape, dt, kind="ExternalOutput").ap())
    ssm_moe_layer(nc, *args)
    r = _run(nc, [arrays], core_ids=[0])
    got = tuple(r.results[0][f"out_{i}_dram"] for i in range(len(_OUTS)))
    return got[0]
```

```python
from contextlib import ExitStack

import numpy as np

import concourse.bass as bass
from concourse import mybir

ALU = mybir.AluOpType
ACT = mybir.ActivationFunctionType
AX_X = mybir.AxisListType.X
F32 = mybir.dt.float32
F32R = mybir.dt.float32r
BF16 = mybir.dt.bfloat16
I32 = mybir.dt.int32
U32 = mybir.dt.uint32

P = 128
Q = 32
NQ = P // Q
FT = 256
EPS = 1e-5
SOFT = 20.0
DT_MIN, DT_MAX = 0.001, 2.0


def ssm_moe_layer(nc, x, W_x, b_x, W_g, b_g, conv_w, conv_b, A_raw, B_ssm, C_ssm, W_dt, b_dt,
                  W_out, b_out, ln_g, ln_b, W1, b1, W2, b2, out):
    B, L, D = x.shape
    H, S = A_raw.shape
    E, _, DFF = W1.shape
    assert D == P and H % P == 0 and DFF % P == 0 and L % P == 0
    NTOK = B * L
    NT = NTOK // P
    HB = H // P
    KB = DFF // P
    NC = L // Q
    BC = B * NC
    CH = 512
    NCH = NTOK // CH
    TPC = CH // P
    NG = P // NQ
    NPAIR = HB * NG // 2
    PPB = NG // 2
    MAXT = (NTOK + E * (FT - 1)) // FT
    ROWS = (MAXT + 2) * FT
    QT = 4
    TQ = NT // QT
    TA_ = 11
    GB = 4
    NGATE = B // GB
    FH = FT // P
    AV = 2
    NYP = 8

    with ExitStack() as ctx:
        def sb(name, shape, dt=F32):
            return ctx.enter_context(nc.sbuf_tensor(name, shape, dt))

        def sem(name):
            return ctx.enter_context(nc.semaphore(name))

        xs_dram = nc.dram_tensor("sorted_tokens", [ROWS, D], F32).ap()
        ys_dram = nc.dram_tensor("sorted_outputs", [ROWS, D], F32).ap()

        RA = sb("RA", [P, NTOK])
        RB = sb("RB", [P, HB, NTOK])
        RC = sb("RC", [P, HB, NTOK])
        XN = RA[:, :].rearrange("p (t d) -> p t d", d=D)
        UT = [RA[:, :].rearrange("p (g c) -> p g c", g=NG), RC[:, 0, :].rearrange("p (g c) -> p g c", g=NG)]
        YT = [RC[:, 1, :], RA[:, :]]
        INTRA = RB[:, 0, :].rearrange("p (g m) -> p g m", m=P)
        NGRP = HB * NG
        INJ = RB[:, 1, 0:NGRP * NQ * S].rearrange("p (g m) -> p g m", m=NQ * S)
        READ = RB[:, 1, NGRP * NQ * S:NGRP * NQ * S + NPAIR * P].rearrange("p (r m) -> p r m", m=P)

        RR = sb("RR", [P, 8 * CH], F32R)
        xh = [RR[:, s * CH:(s + 1) * CH] for s in range(2)]
        xl = [RR[:, (2 + s) * CH:(3 + s) * CH] for s in range(2)]
        PW = RR[:, 4 * CH:4 * CH + 2 * 3 * HB * P].rearrange("p (v j m) -> p v j m", v=2, m=P)
        W1h = [RR[:, s * DFF:(s + 1) * DFF] for s in range(3)]
        W1l = [RR[:, (3 + s) * DFF:(4 + s) * DFF] for s in range(3)]
        XSPLIT = RR[:, 6 * DFF:6 * DFF + 2 * FT].rearrange("p (v h d) -> p v h d", v=2, h=FH)
        XT = RR[:, 6 * DFF + 2 * FT:6 * DFF + 4 * FT]

        AR = sb("AR", [P, 11 * CH])
        xin = [AR[:, s * CH:(s + 1) * CH].rearrange("p (t d) -> p t d", d=D) for s in range(2)]
        mb = [AR[:, (2 + s) * CH:(3 + s) * CH] for s in range(2)]
        eb = [AR[:, (4 + s) * CH:(5 + s) * CH] for s in range(2)]
        junk = AR[:, 6 * CH:7 * CH]
        W2S = [AR[:, s * DFF:(s + 1) * DFF].rearrange("p (k d) -> p k d", k=KB) for s in range(3)]
        W1RAW = [AR[:, 3 * CH:4 * CH], AR[:, 9 * CH:10 * CH], AR[:, 10 * CH:11 * CH]]

        def raw_slot(k):
            return k + 1 if k < 2 else 0 if k == 2 else k % 3

        def raw_loads(k):
            return sum(raw_slot(j) == raw_slot(k) for j in range(k + 1))

        HID = [AR[:, (4 + 2 * n) * CH:(6 + 2 * n) * CH].rearrange("p (k t) -> p k t", k=KB) for n in range(2)]
        XSIN = AR[:, 8 * CH:8 * CH + FT].rearrange("p (h d) -> p h d", h=FH)
        YSB = AR[:, 8 * CH + FT:9 * CH].rearrange("p (h d) -> p h d", h=FH)
        TG = AR[:, 9 * CH:11 * CH]

        identity = sb("identity", [P, P])
        vrows = sb("vrows", [8 + E * KB, P])
        VC = sb("VC", [P, 8 + E * KB])
        bx, bg, bdt, cb = (VC[:, 2 * n:2 * n + 2] for n in range(4))
        B1C = VC[:, 8:8 + E * KB].rearrange("p (e k) -> p e k", e=E)
        cw = sb("cw", [P, HB, 3])
        cwn = sb("cwn", [P, HB, 3])
        cbn = sb("cbn", [P, HB])
        WoT = sb("WoT", [P, HB, D])
        b2s = sb("b2s", [P, 3, D])
        b2p = sb("b2p", [P, D])
        lng = sb("lng", [P, D])
        lnb = sb("lnb", [P, D])
        bo = sb("bo", [P, D])
        bor = sb("bor", [P, D])
        bop = sb("bop", [P, D], BF16)
        first = sb("first", [P, P], BF16)
        bdtm = sb("bdtm", [P, HB])
        Araw = sb("Araw", [P, HB, S])
        Bssm = sb("Bssm", [P, HB, S])
        Cssm = sb("Cssm", [P, HB, S])
        Aneg = sb("Aneg", [P, HB, S])
        aval = sb("aval", [P, HB, S])
        sv = sb("sv", [P, HB, S])
        sv2 = sb("sv2", [P, HB, S])
        acc1 = sb("acc1", [P, HB, NCH])
        acc2 = sb("acc2", [P, HB, NCH])
        dtv = sb("dtv", [P, HB, 2])
        mean = sb("mean", [P, NT])
        rstd = sb("rstd", [P, NT])
        nmr = sb("nmr", [P, NT])
        posi = sb("posi", [P, NT], U32)
        tsi = sb("tsi", [P, E + 1], I32)
        cmask = sb("cmask", [P, B * NC], BF16)
        A32 = sb("A32", [P, NPAIR])
        AP2 = sb("AP2", [P, 2, NPAIR])
        half4 = sb("half4", [P, 2, NQ])
        half = sb("half", [P, 2])
        jv = sb("jv", [P, Q + 1])
        jr = sb("jr", [P, Q])
        FST = [sb(f"FST{k}", [P, 8, 6]) for k in range(2)]
        fs = [[sb(f"fs{n}_{k}", [P, 8]) for n in range(5)] for k in range(3)]

        o = [0]

        def carve(region, n, dt=F32):
            a = region[:, o[0]:o[0] + n]
            o[0] += n
            return a if dt == F32 else a.bitcast(dt)

        RC1 = RC[:, 1, :]
        ZERO = carve(RC1, 10 * D)
        ST = carve(RC1, NT * 6).rearrange("p (t k) -> p t k", k=6)
        lt = [carve(RC1, NT) for _ in range(12)]
        ti = carve(RC1, NT, I32)
        OH = carve(RC1, E * NT // 2, BF16)
        PI = carve(RC1, E * NT)
        PA = carve(RC1, E * NT)
        ONE = carve(RC1, E * NT)
        ULT = carve(RC1, P // 2, BF16)
        ONEB = carve(RC1, P // 2, BF16)
        e9 = carve(RC1, E + 1)
        ts9 = carve(RC1, E + 1)
        e8 = [carve(RC1, E) for _ in range(5)]
        e8i = carve(RC1, E, I32)
        WRAW = carve(RC1, (3 * HB + HB) * D).rearrange("p (j d) -> p j d", d=D)

        NS2 = HB * S * (Q + 1)
        o[0] = 0
        EX = carve(RC1, NS2).rearrange("p (b s j) -> p b s j", b=HB, s=S)
        ER = carve(RC1, HB * S * Q).rearrange("p (b s j) -> p b s j", b=HB, s=S)
        KP = carve(RC1, HB * (2 * Q - 1)).rearrange("p (b j) -> p b j", b=HB)
        TA = carve(RC1, HB * (Q + 1) * Q)
        TB = carve(RC1, HB * (Q + 1) * Q)
        D0 = [AR[:, n * BC:(n + 1) * BC] for n in range(2)]
        SX = [AR[:, (2 + n) * BC:(3 + n) * BC] for n in range(2)]

        TB8 = 8
        NB8 = NT // TB8
        TC = TB8 * D

        def batch(region, k):
            return region[:, k * TC:(k + 1) * TC].rearrange("p (t d) -> p t d", d=D)

        NAR = NB8 // 2
        GA = [batch(AR[:, 2 * CH:], n) for n in range(NAR)] + [batch(RB[:, 0, 0:NTOK // 2], n) for n in range(NB8 - NAR)]
        NV = 4
        INJ0, INJ1 = RB[:, 1, 0:NTOK // 4], RB[:, 1, NTOK // 4:NTOK // 2]
        READ0, READ1 = RB[:, 1, NTOK // 2:3 * NTOK // 4], RB[:, 1, 3 * NTOK // 4:NTOK]
        VV = [batch(INJ0, 0), batch(INJ0, 1), batch(INJ1, 0), batch(INJ1, 1)]
        XR = [batch(READ0, 0), batch(READ0, 1)] + [batch(RB[:, 0, NTOK // 2:], n) for n in range(4)]
        XR += [batch(READ1, 0), batch(READ1, 1)]
        assert NB8 == 8 and NG * P == NTOK // 2 and NG * NQ * S == NTOK // 4 and PPB * P == NTOK // 4
        PS = ctx.enter_context(nc.psum_tensor("PS", [P, 8, 512], F32))
        ps = [PS[:, n, :] for n in range(8)]

        s_x = [sem(f"x_loaded_{q}") for q in range(QT)]
        s_small = sem("small_loaded")
        s_wraw = sem("weights_loaded")
        s_const = sem("pool_constants")
        s_dve = sem("vector_chain")
        s_act = sem("scalar_chain")
        s_lnv = sem("variance_ready")
        s_lny = sem("rstd_estimate_ready")
        s_nmr = sem("scales_ready")
        s_nrm = sem("xn_quarter_ready_vector")
        s_nra = sem("xn_quarter_ready_scalar")
        s_wsh = sem("w1_high_ready")
        s_sph = sem("sorted_tile_high_ready")
        s_step = sem("pool_steps")
        s_step2 = sem("vector_steps")
        s_fg = sem("last_scaled")
        s_fp = sem("last_part_normalised_vector")
        s_actl = sem("last_log_ready")
        s_wt = sem("weights_transposed")
        s_wh = sem("weights_high_ready")
        s_wl = sem("weights_low_ready")
        s_vt = sem("vectors_transposed")
        s_vc = sem("vectors_ready")
        s_zero = sem("zero_tile_ready")
        s_fill = sem("sorted_tokens_cleared")
        s_oh = sem("one_hot_ready")
        s_rank = sem("ranks_ready")
        s_pos = sem("positions_ready")
        s_scat = sem("tokens_scattered")
        s_xin = [sem(f"chunk_copied_{s}") for s in range(2)]
        s_xt = [sem(f"chunk_transposed_{s}") for s in range(2)]
        s_hi = [sem(f"chunk_high_ready_{s}") for s in range(2)]
        s_lo = [sem(f"chunk_low_ready_{s}") for s in range(2)]
        s_pr = [[sem(f"projected_{n}_{hb}") for hb in range(HB)] for n in ("dt", "u", "g")]
        s_min = [sem(f"clamped_ready_{hb}") for hb in range(HB)]
        s_dte = [sem(f"dt_bank_read_{hb}") for hb in range(HB)]
        s_ue = [sem(f"u_stored_{hb}") for hb in range(HB)]
        s_ge = [sem(f"z_stored_{hb}") for hb in range(HB)]
        s_exp = [sem(f"exp_ready_{hb}") for hb in range(HB)]
        s_ln = [sem(f"softplus_summed_{hb}") for hb in range(HB)]
        s_sig = sem("gate_piece_ready")
        s_asp = sem("a_softplus_input")
        s_asq = sem("a_softplus_done")
        s_earg = sem("exponents_ready")
        s_eexp = sem("decays_ready")
        s_jv = sem("iotas_ready")
        s_mat = sem("matrices_ready")
        s_w1 = [sem(f"w1_loaded_{s}") for s in range(3)]
        s_w2 = [sem(f"w2_loaded_{s}") for s in range(3)]
        s_ws = sem("w1_split")
        s_b2 = sem("b2_pair_ready")
        s_xs = sem("sorted_tile_loaded")
        s_sp = sem("sorted_tile_split")
        s_tt = sem("sorted_tile_transposed")
        s_xtr = sem("sorted_tile_in_place")
        s_m1 = [sem(f"expert_{n}_hidden") for n in "ab"]
        s_re = [sem(f"expert_{n}_relu") for n in "ab"]
        s_m2 = sem("expert_output_summed")
        s_m2a = sem("first_expert_read")
        s_ysb = sem("expert_output_in_sbuf")
        s_yad = sem("expert_bias_added")
        s_yst = sem("expert_output_stored")
        s_inj = sem("injection_ready")
        s_d0 = sem("decay_row_ready")
        s_scan = sem("states_ready")
        s_yps = sem("pair_output_ready")
        s_yev = sem("pair_output_in_sbuf")
        s_ytr = sem("y_piece_transposed")
        s_gat = [sem(f"expert_outputs_gathered_{n}") for n in range(NB8)]
        s_xr = [sem(f"x_reloaded_{n}") for n in range(NB8)]
        s_po = sem("projection_out_ready")
        s_xa = sem("xn_again_ready")
        s_v = sem("residual_sum_ready")
        s_fv = sem("last_variance_ready")
        s_fy = sem("last_rstd_estimate")
        s_fr = sem("last_scales_ready")
        s_fn = sem("last_normalised")
        s_base = sem("base_ready")
        s_fo = sem("output_ready")
        s_out = [sem(f"output_stored_{n}") for n in range(NV)]

        x_v = x.rearrange("b (s p) d -> p (b s) d", p=P)
        out_v = out.rearrange("b (s p) d -> p (b s) d", p=P)
        xs_v = xs_dram.rearrange("(t h p) d -> t p h d", h=FH, p=P)
        ys_v = ys_dram.rearrange("(t h p) d -> t p h d", h=FH, p=P)
        xs_z = xs_dram.rearrange("(p r) d -> p (r d)", p=P)
        ZR = 10
        XSR = ROWS // P
        NZ = -(-XSR // ZR)
        YR = (ROWS - NTOK) // P
        assert ZR < YR <= 2 * ZR
        small = [(vrows[0:2, :], b_x.rearrange("(b p) -> b p", p=P)), (vrows[2:4, :], b_g.rearrange("(b p) -> b p", p=P)),
                 (vrows[4:6, :], b_dt.rearrange("(b p) -> b p", p=P)), (vrows[6:8, :], conv_b.rearrange("(b p) -> b p", p=P)),
                 (vrows[8:8 + E * KB, :], b1.rearrange("e (k p) -> (e k) p", p=P)),
                 (cw[:, :, :], conv_w.rearrange("(b p) o k -> p b (o k)", p=P)),
                 (Araw[:, :, :], A_raw.rearrange("(b p) s -> p b s", p=P)),
                 (Bssm[:, :, :], B_ssm.rearrange("(b p) s -> p b s", p=P)),
                 (Cssm[:, :, :], C_ssm.rearrange("(b p) s -> p b s", p=P)),
                 (lng[:, :], ln_g.rearrange("(o d) -> o d", o=1).broadcast_to([P, D])),
                 (lnb[:, :], ln_b.rearrange("(o d) -> o d", o=1).broadcast_to([P, D])),
                 (bo[:, :], b_out.rearrange("(o d) -> o d", o=1).broadcast_to([P, D]))]
        NSMALL = len(small)

        def gate_cols(n):
            return slice(n * GB * L, (n + 1) * GB * L)

        def expert_bounds(eng):
            eng.wait_ge(s_pos, 1)
            return [0] + [eng.value_load(tsi[0:1, e:e + 1], min_val=e, max_val=MAXT) for e in range(1, E + 1)]

        block = ctx.enter_context(nc.Block())

        @block.sync
        def _(sp):
            sp.sem_inc(s_yst, 16)
            for q in range(QT):
                sp.dma_start(XN[:, q * TQ:(q + 1) * TQ, :], x_v[:, q * TQ:(q + 1) * TQ, :]).then_inc(s_x[q], 16)
            for dst, src in small:
                sp.dma_start(dst, src, allow_slow_non_contiguous=True).then_inc(s_small, 16)
            sp.wait_ge(s_zero, 1)
            for n in range(NZ):
                w = min(ZR, XSR - n * ZR) * D
                sp.dma_start(xs_z[:, n * ZR * D:n * ZR * D + w], ZERO[:, 0:w]).then_inc(s_fill, 16)
            sp.dma_start(ys_dram[NTOK:ROWS, :].rearrange("(p r) d -> p (r d)", p=P)[:, 0:ZR * D], ZERO).then_inc(s_fill, 16)
            sp.dma_start(ys_dram[NTOK:ROWS, :].rearrange("(p r) d -> p (r d)", p=P)[:, ZR * D:], ZERO[:, 0:YR * D - ZR * D]
                         ).then_inc(s_fill, 16)
            for k in range(2):
                sp.dma_start(W1RAW[raw_slot(k)], W1[k]).then_inc(s_w1[raw_slot(k)], 16)
            sp.wait_ge(s_nrm, 1)
            sp.wait_ge(s_nra, 1)
            for s in range(2):
                sp.dma_start(xin[s], XN[:, s * TPC:(s + 1) * TPC, :]).then_inc(s_xin[s], 16)
            sp.wait_ge(s_nrm, QT)
            sp.wait_ge(s_nra, QT)
            with sp.Fori(1, NCH // 2) as i:
                for s in range(2):
                    sp.wait_ge(s_xt[s], i)
                    sp.dma_start(xin[s], XN[:, bass.ds((i * 2 + s) * TPC, TPC), :]).then_inc(s_xin[s], 16)

            def load_w1(k):
                sp.dma_start(W1RAW[raw_slot(k)], W1[k % E]).then_inc(s_w1[raw_slot(k)], 16)

            def load_w2(k):
                sp.dma_start(W2S[k % 3], W2[k % E].rearrange("(k p) d -> p k d", p=P)).then_inc(s_w2[k % 3], 16)
                sp.dma_start(b2s[:, k % 3, :], b2[k % E:k % E + 1, :].broadcast_to([P, D])).then_inc(s_w2[k % 3], 16)

            bounds = expert_bounds(sp)
            sp.wait_ge(s_scat, 16 * NT)
            sp.dma_start(XSIN, xs_v[0]).then_inc(s_xs, 16)
            for s in range(2):
                sp.wait_ge(s_xt[s], NCH // 2)
                load_w2(s)
            for hb in range(HB):
                sp.wait_ge(s_exp[hb], NCH)
                sp.wait_ge(s_dte[hb], NCH)
            load_w1(2)
            load_w2(2)
            sp.wait_ge(s_sp, 1)
            sp.dma_start(XSIN, xs_v[1]).then_inc(s_xs, 16)
            w1_before = {1: [3], 2: [4, 5], 3: [6], 4: [7], 5: [8]}
            for g in range(E):
                if 1 <= g < E - 1:
                    sp.wait_ge(s_m2, bounds[g])
                    load_w2(g + 2)
                for k in w1_before.get(g, []):
                    if k == 4:
                        sp.wait_ge(s_earg, 1)
                    if k == 3 or k >= 6:
                        sp.wait_ge(s_ws, k if k == 3 else k - 2)
                    load_w1(k)
                with sp.Fori(bounds[g], bounds[g + 1]) as i:
                    sp.wait_ge(s_sp, i + 2)
                    sp.dma_start(XSIN, xs_v[bass.ds(i + 2, 1)].rearrange("o p h d -> p (o h) d")).then_inc(s_xs, 16)
                    sp.wait_ge(s_yad, i + 1)
                    sp.dma_start(ys_v[bass.ds(i, 1)].rearrange("o p h d -> p (o h) d"), YSB).then_inc(s_yst, 16)

            for n in range(NB8):
                if n == 0:
                    sp.wait_ge(s_yps, PPB)
                if n == 2:
                    sp.wait_ge(s_yps, NPAIR)
                sp.dma_start(XR[n], x_v[:, n * TB8:(n + 1) * TB8, :]).then_inc(s_xr[n], 16)
            for n in range(NB8):
                sp.wait_ge(s_fo, n + 1)
                sp.dma_start(out_v[:, n * TB8:(n + 1) * TB8, :], VV[n % NV]).then_inc(s_out[n % NV], 16)
            for n in range(NV):
                sp.wait_ge(s_out[n], 16 * NB8 // NV)

        @block.gpsimd
        def _(pool):
            nc.gpsimd.memset(ZERO, 0.0).then_inc(s_zero, 1)
            nc.gpsimd.iota(jv[:, :], [[1, Q + 1]], base=0, channel_multiplier=0,
                           allow_small_or_imprecise_dtypes=True).then_inc(s_jv, 1)
            nc.gpsimd.iota(jr[:, :], [[-1, Q]], base=Q - 1, channel_multiplier=0,
                           allow_small_or_imprecise_dtypes=True).then_inc(s_jv, 1)
            nc.gpsimd.memset(identity[:, :], 0.0).then_inc(s_const, 1)
            nc.gpsimd.memset(ULT, 1.0).then_inc(s_const, 1)
            nc.gpsimd.memset(cmask[:, :], 1.0).then_inc(s_const, 1)
            pool.wait_ge(s_const, 3)
            nc.gpsimd.affine_select(out=identity[:, :], in_=identity[:, :], compare_op=ALU.not_equal, fill=1.0, base=0,
                                    pattern=[[-1, P]], channel_multiplier=1).then_inc(s_const, 1)
            nc.gpsimd.affine_select(out=ULT, in_=ULT, compare_op=ALU.is_gt, fill=0.0, base=0,
                                    pattern=[[1, P]], channel_multiplier=-1).then_inc(s_const, 1)
            nc.gpsimd.affine_select(out=cmask[:, :].rearrange("p (b c) -> p b c", c=NC),
                                    in_=cmask[:, :].rearrange("p (b c) -> p b c", c=NC), compare_op=ALU.is_gt,
                                    fill=0.0, base=0, pattern=[[0, B], [1, NC]], channel_multiplier=0).then_inc(s_const, 1)

            for q in range(QT):
                pool.wait_ge(s_nmr, q + 1)
                for t in range(q * TQ, (q + 1) * TQ - TA_):
                    ins = nc.gpsimd.tensor_scalar(XN[:, t, :], XN[:, t, :], mean[:, t:t + 1], rstd[:, t:t + 1],
                                                  ALU.subtract, ALU.mult)
                ins.then_inc(s_nrm, 1)

            pool.wait_ge(s_nrm, QT)
            pool.wait_ge(s_nra, QT)
            pool.wait_ge(s_pos, 1)
            pool.wait_ge(s_fill, 16 * (NZ + 2))
            for t in range(NT):
                nc.gpsimd.indirect_dma_start(out=xs_dram, out_offset=bass.IndirectOffsetOnAxis(ap=posi[:, t:t + 1], axis=0),
                                             in_=XN[:, t, :], in_offset=None).then_inc(s_scat, 16)

            def split_tile(i):
                pool.wait_ge(s_xs, (i + 1) * 16)
                if not isinstance(i, int) or i:
                    pool.wait_ge(s_tt, i)
                pool.sem_inc(s_step, 1)
                nc.gpsimd.tensor_copy(XSPLIT[:, 0], XSIN).then_inc(s_sph, 1)
                pool.wait_ge(s_sph, i + 1)
                nc.gpsimd.tensor_tensor(XSPLIT[:, 1], XSIN, XSPLIT[:, 0].bitcast(F32), ALU.subtract).then_inc(s_sp, 1)

            bounds = expert_bounds(pool)
            for j in range(3):
                for hb in range(HB):
                    pool.wait_ge(s_pr[j][hb], NCH)
            split_tile(0)
            split_tile(1)
            for g in range(E):
                pool.wait_ge(s_w2[g % 3], 32 * (g // 3 + 1))
                pool.wait_ge(s_w2[(g + 1) % 3], 32 * ((g + 1) // 3 + 1))
                if g >= 1:
                    pool.wait_ge(s_yad, bounds[g])
                nc.gpsimd.tensor_tensor(b2p[:, :], b2s[:, g % 3, :], b2s[:, (g + 1) % 3, :], ALU.add).then_inc(s_b2, 1)
                pool.wait_ge(s_b2, 3 * g + 1)
                nc.gpsimd.tensor_scalar(b2p[:, :], b2p[:, :], 0.5, 0.0, ALU.mult, ALU.add).then_inc(s_b2, 1)
                pool.wait_ge(s_b2, 3 * g + 2)
                pool.wait_ge(s_small, 16 * NSMALL)
                nc.gpsimd.tensor_tensor(b2p[:, :], b2p[:, :], lnb[:, :], ALU.add).then_inc(s_b2, 1)
                pool.wait_ge(s_b2, 3 * g + 3)
                with pool.Fori(bounds[g], bounds[g + 1]) as i:
                    split_tile(i + 2)
                    pool.wait_ge(s_ysb, i + 2)
                    nc.gpsimd.tensor_tensor(YSB, YSB, b2p[:, :].rearrange("p (o d) -> p o d", o=1).broadcast_to([P, FH, D]),
                                            ALU.add).then_inc(s_yad, 1)

            pool.wait_ge(s_yst, bounds[E] * 16 + 16)
            for n in range(NB8):
                if n == 0:
                    pool.wait_ge(s_m2, bounds[E])
                    pool.wait_ge(s_xtr, bounds[E] + 1)
                    pool.sem_inc(s_step, 1)
                    pool.wait_ge(s_mat, 1)
                if n == NAR:
                    pool.wait_ge(s_yps, PPB)
                for t in range(TB8):
                    nc.gpsimd.indirect_dma_start(out=GA[n][:, t, :], out_offset=None, in_=ys_dram,
                                                 in_offset=bass.IndirectOffsetOnAxis(
                                                     ap=posi[:, n * TB8 + t:n * TB8 + t + 1], axis=0)).then_inc(s_gat[n], 16)
            for n in range(NB8):
                pool.wait_ge(s_gat[n], 16 * TB8)
                pool.wait_ge(s_xr[n], 16)
                nc.gpsimd.tensor_tensor(GA[n], GA[n], XR[n], ALU.add).then_inc(s_base, 1)
            pool.wait_ge(s_base, NB8)
            for n in range(NB8):
                pool.wait_ge(s_fg, n + 1)
                nc.gpsimd.tensor_tensor(VV[n % NV], VV[n % NV], GA[n], ALU.add).then_inc(s_fo, 1)

        @block.scalar
        def _(act):
            act.sem_inc(s_ysb, 1)
            nc.scalar.preload_act_table_set("natural_log_exp_and_others")
            act.dma_start(WRAW[:, 0:HB, :], W_dt.rearrange("(b p) d -> p b d", p=P)).then_inc(s_wraw, 16)
            act.dma_start(WRAW[:, HB:2 * HB, :], W_x.rearrange("(b p) d -> p b d", p=P)).then_inc(s_wraw, 16)
            act.dma_start(WRAW[:, 2 * HB:3 * HB, :], W_g.rearrange("(b p) d -> p b d", p=P)).then_inc(s_wraw, 16)
            act.dma_start(WRAW[:, 3 * HB:4 * HB, :].rearrange("p b d -> p (b d)"), W_out).then_inc(s_wraw, 16)

            def quarter(q):
                act.wait_ge(s_lnv, q + 1)
                c = slice(q * TQ, (q + 1) * TQ)
                nc.scalar.activation(lt[5][:, c], lt[4][:, c], ACT.Ln).then_inc(s_act, 1)
                act.wait_ge(s_act, q + 1)
                nc.scalar.activation(lt[6][:, c], lt[5][:, c], ACT.Exp, scale=-0.5).then_inc(s_lny, 1)

            def normalise(q):
                act.wait_ge(s_nmr, q + 1)
                for t in range((q + 1) * TQ - TA_, (q + 1) * TQ):
                    ins = nc.scalar.activation(XN[:, t, :], XN[:, t, :], ACT.Identity, scale=rstd[:, t:t + 1],
                                               bias=nmr[:, t:t + 1])
                ins.then_inc(s_nra, 1)

            quarter(0)
            for q in range(1, QT):
                quarter(q)
                normalise(q - 1)
            act.wait_ge(s_wt, 4 * HB)
            for n in range(3 * HB):
                nc.scalar.activation(PW[:, 0, n, :], ps[n // 4][:, (n % 4) * P:(n % 4 + 1) * P], ACT.Copy).then_inc(s_wh, 1)
            normalise(QT - 1)

            def high(s, i):
                act.wait_ge(s_xt[s], i + 1)
                if not isinstance(i, int) or i:
                    act.wait_ge(s_pr[2][HB - 1], i * 2 + (s - 1))
                nc.scalar.activation(xh[s], ps[s], ACT.Copy).then_inc(s_hi[s], 1)

            def gate_input(c):
                for hb in range(HB):
                    act.wait_ge(s_pr[2][hb], c + 1)
                    nc.scalar.activation(RC[:, hb, bass.ds(c * CH, CH)], ps[6 + hb], ACT.Identity,
                                         bias=bg[:, hb:hb + 1]).then_inc(s_ge[hb], 1)

            def softplus(c):
                for hb in range(HB):
                    act.wait_ge(s_min[hb], c + 1)
                    nc.scalar.activation(eb[hb], mb[hb], ACT.Exp).then_inc(s_exp[hb], 1)
                    act.wait_ge(s_exp[hb], c + 1)
                    nc.scalar.activation(eb[hb], eb[hb], ACT.Ln, bias=1.0, accum_out=acc1[:, hb, bass.ds(c, 1)]
                                         ).then_inc(s_ln[hb], 1)

            high(0, 0)
            high(1, 0)
            act.wait_ge(s_vc, 1)
            bounds = expert_bounds(act)
            act.wait_ge(s_fill, 16 * (NZ + 2))
            softplus(0)
            high(0, 1)
            gate_input(0)
            softplus(1)
            with act.Fori(1, NCH // 2 - 1) as i:
                for s in range(2):
                    high(1 - s, i + s)
                    gate_input(i * 2 + (s - 1))
                    softplus(i * 2 + s)
            high(1, NCH // 2 - 1)
            gate_input(NCH - 3)
            softplus(NCH - 2)
            gate_input(NCH - 2)
            softplus(NCH - 1)
            gate_input(NCH - 1)

            NPIECE = HB * NGATE
            RCF = RC[:, :, :].rearrange("p b t -> p (b t)")

            def gate_piece(n):
                z = RCF[:, bass.ds(n * (GB * L), GB * L)]
                nc.scalar.activation(z, z, ACT.Sigmoid, scale=-1.0).then_inc(s_sig, 1)

            def place_tile(i):
                act.wait_ge(s_tt, i + 1)
                nc.scalar.activation(XT, ps[4], ACT.Copy).then_inc(s_xtr, 1)

            for k in range(2):
                act.wait_ge(s_w1[raw_slot(k)], 16)
                nc.scalar.activation(W1h[k], W1RAW[raw_slot(k)], ACT.Copy).then_inc(s_wsh, 1)
            place_tile(0)
            act.wait_ge(s_asp, 1)
            nc.scalar.activation(sv[:, :, :], sv[:, :, :], ACT.Exp).then_inc(s_asq, 1)
            act.wait_ge(s_asq, 1)
            nc.scalar.activation(sv[:, :, :], sv[:, :, :], ACT.Ln, bias=1.0).then_inc(s_asq, 1)
            nc.scalar.preload_act_table_set("sigmoid_and_others")
            for hb in range(HB):
                act.wait_ge(s_ge[hb], NCH)
                act.wait_ge(s_dte[hb], NCH)
            for g in range(E):
                if g == 2:
                    with act.If(bounds[2] < NPIECE):
                        with act.Fori(bounds[2], NPIECE) as n:
                            gate_piece(n)
                    nc.scalar.preload_act_table_set("natural_log_exp_and_others")
                    act.wait_ge(s_earg, 1)
                    nc.scalar.activation(EX, EX, ACT.Exp)
                    nc.scalar.activation(ER, ER, ACT.Exp).then_inc(s_eexp, 1)
                with act.Fori(bounds[g], bounds[g + 1]) as i:
                    for n in range(2):
                        e = (g + n) % E
                        for k in range(KB):
                            if k % 2 == 0:
                                act.wait_ge(s_m1[n], i * KB + (k + 2))
                            nc.scalar.activation(HID[n][:, k, :], ps[2 * n + k // 2][:, (k % 2) * FT:(k % 2 + 1) * FT],
                                                 ACT.Relu, bias=B1C[:, e, k:k + 1]).then_inc(s_re[n], 1)
                    place_tile(i + 1)
                    if g < 2:
                        with act.If(i < NPIECE):
                            gate_piece(nc.s_assert_within(i, 0, NPIECE - 1, skip_runtime_bounds_check_because="the If"))
                    act.wait_ge(s_m2, i + 1)
                    act.wait_ge(s_yst, i * 16 + 16)
                    for h in range(FH):
                        ins = nc.scalar.activation(YSB[:, h, :], ps[5 + h][:, 0:D], ACT.Copy, scale=0.5)
                    ins.then_inc(s_ysb, 1)

            def again(n):
                act.wait_ge(s_xr[n], 16)
                if n >= NV:
                    act.wait_ge(s_out[n % NV], 16 * (n // NV))
                for t in range(TB8):
                    ti_ = n * TB8 + t
                    ins = nc.scalar.activation(VV[n % NV][:, t, :], XR[n][:, t, :], ACT.Identity, scale=rstd[:, ti_:ti_ + 1],
                                               bias=nmr[:, ti_:ti_ + 1])
                ins.then_inc(s_xa, 1)

            AHEAD = 3
            for r in range(NPAIR):
                hb, rp = divmod(r, PPB)
                act.wait_ge(s_yps, r + 1)
                nc.scalar.activation(UT[hb][:, 2 * rp:2 * rp + 2, :],
                                     PS[:, 2 + 2 * (r % 3):4 + 2 * (r % 3), 0:BC], ACT.Copy).then_inc(s_yev, 1)
                if r in (NPAIR - 8, NPAIR - 5):
                    again((r - NPAIR + 8) // 3)
            again(2)

            def apply(n):
                f = fs[n % 3]
                act.wait_ge(s_fr, n + 1)
                for t in range(TB8 - AV):
                    ins = nc.scalar.activation(VV[n % NV][:, t, :], VV[n % NV][:, t, :], ACT.Identity,
                                               scale=f[3][:, t:t + 1], bias=f[4][:, t:t + 1])
                ins.then_inc(s_fn, 1)

            for n in range(NB8):
                f = fs[n % 3]
                act.wait_ge(s_fv, n + 1)
                nc.scalar.activation(f[2][:, :], f[1][:, :], ACT.Ln).then_inc(s_actl, 1)
                act.wait_ge(s_actl, n + 1)
                nc.scalar.activation(f[3][:, :], f[2][:, :], ACT.Exp, scale=-0.5).then_inc(s_fy, 1)
                if n >= 1:
                    apply(n - 1)
                if n + AHEAD - 1 < NB8 and n >= 1:
                    again(n + AHEAD - 1)
            apply(NB8 - 1)

        @block.vector
        def _(dve):
            count = [0]

            def link(ins):
                count[0] += 1
                ins.then_inc(s_dve, 1)
                dve.wait_ge(s_dve, count[0])

            V = nc.vector
            V.memset(ONE, 1.0)
            link(V.memset(ONEB, 1.0))
            link(V.memset(first[:, :], 0.0))
            for k in range(3):
                V.memset(first[Q * k:Q * k + 1, :], 1.0)
            V.memset(e9, 0.0)
            link(V.memset(ts9, 0.0))

            def refine(v, y, a, b_):
                link(V.tensor_tensor(a, y, y, ALU.mult))
                link(V.tensor_tensor(b_, a, v, ALU.mult))
                link(V.tensor_scalar(a, b_, -0.5, 1.5, ALU.mult, ALU.add))
                link(V.tensor_tensor(y, y, a, ALU.mult))

            def variance(st, m, v, t1, t2):
                V.tensor_tensor(m, st[:, :, 1], st[:, :, 4], ALU.add)
                V.tensor_tensor(t1, st[:, :, 1], st[:, :, 4], ALU.subtract)
                link(V.tensor_tensor(v, st[:, :, 2], st[:, :, 5], ALU.add))
                link(V.scalar_tensor_tensor(t2, t1, 0.25, t1, ALU.mult, ALU.mult))
                V.tensor_scalar(m, m, 0.5, None, ALU.mult)
                link(V.scalar_tensor_tensor(t1, v, 1.0 / D, t2, ALU.mult, ALU.add))

            xd = lt[9][:, 0:2 * TQ].rearrange("p (t k) -> p t k", k=2)
            def statistics(q):
                c = slice(q * TQ, (q + 1) * TQ)
                dve.wait_ge(s_x[q], 16)
                for t in range(q * TQ, (q + 1) * TQ):
                    ins = V.bn_stats(ST[:, t, :], XN[:, t, :])
                link(ins)
                variance(ST[:, c, :], mean[:, c], lt[3][:, c], lt[1][:, c], lt[2][:, c])
                V.tensor_scalar(lt[4][:, c], lt[1][:, c], EPS, None, ALU.add).then_inc(s_lnv, 1)

            def scales(q):
                c = slice(q * TQ, (q + 1) * TQ)
                dve.wait_ge(s_lny, q + 1)
                link(V.tensor_copy(rstd[:, c], lt[6][:, c]))
                refine(lt[4][:, c], rstd[:, c], lt[7][:, c], lt[8][:, c])
                link(V.tensor_tensor(xd, XN[:, c, 0:2], mean[:, c].rearrange("p (t o) -> p t o", o=1).broadcast_to([P, TQ, 2]),
                                     ALU.subtract))
                V.scalar_tensor_tensor(nmr[:, c], mean[:, c], -1.0, rstd[:, c], ALU.mult, ALU.mult).then_inc(s_nmr, 1)
                link(V.tensor_tensor(xd, xd, rstd[:, c].rearrange("p (t o) -> p t o", o=1).broadcast_to([P, TQ, 2]),
                                     ALU.mult))
                link(V.tensor_tensor(lt[0][:, c], xd[:, :, 0], xd[:, :, 1], ALU.add))

            statistics(0)
            for q in range(1, QT):
                statistics(q)
                scales(q - 1)
            scales(QT - 1)

            s_, a_, f_, g_, h_, w_ = lt[0], lt[1], lt[2], lt[3], lt[5], lt[7]
            link(V.scalar_tensor_tensor(a_, s_, -1.0, s_, ALU.mult, ALU.max))
            link(V.tensor_copy(ti, a_))
            link(V.tensor_copy(f_, ti))
            link(V.tensor_tensor(g_, f_, a_, ALU.is_gt))
            link(V.tensor_tensor(f_, f_, g_, ALU.subtract))
            for _ in range(2):
                link(V.tensor_scalar(g_, f_, float(E), -float(E), ALU.is_ge, ALU.mult))
                link(V.tensor_tensor(f_, f_, g_, ALU.add))
            link(V.tensor_scalar(w_, f_, -2.0, float(E), ALU.mult, ALU.add))
            link(V.scalar_tensor_tensor(h_, s_, 0.0, w_, ALU.is_lt, ALU.mult))
            link(V.tensor_tensor(h_, h_, f_, ALU.add))
            link(V.tensor_scalar(g_, h_, float(E), -float(E), ALU.is_ge, ALU.mult))
            link(V.tensor_tensor(h_, h_, g_, ALU.add))
            for e in range(E):
                ins = V.tensor_scalar(OH[:, e * NT:(e + 1) * NT], h_, float(e), None, ALU.is_equal)
            ins.then_inc(s_oh, 1)
            dve.wait_ge(s_wh, 3 * HB)
            for n in range(3 * HB):
                ins = V.tensor_tensor(PW[:, 1, n, :], ps[n // 4][:, (n % 4) * P:(n % 4 + 1) * P],
                                      PW[:, 0, n, :].bitcast(F32), ALU.subtract)
            ins.then_inc(s_wl, 1)
            V.tensor_copy(WoT[:, :, :].rearrange("p b d -> p (b d)"), ps[1][:, 2 * P:4 * P]).then_inc(s_wl, 1)
            dve.wait_ge(s_vt, 1)
            link(V.tensor_copy(VC[:, :], ps[2][:, 0:8 + E * KB]))
            V.tensor_scalar(cwn[:, :, :].rearrange("p b k -> p (b k)"), cw[:, :, :].rearrange("p b k -> p (b k)"),
                            -1.0, None, ALU.mult)
            V.tensor_scalar(cbn[:, :], cb, -1.0, None, ALU.mult)
            V.tensor_scalar(sv[:, :, :], Araw[:, :, :], SOFT, None, ALU.min).then_inc(s_asp, 1)
            link(V.tensor_scalar(sv2[:, :, :], Araw[:, :, :], SOFT, None, ALU.subtract))
            link(V.tensor_scalar(sv2[:, :, :], sv2[:, :, :], 0.0, None, ALU.max))
            V.tensor_scalar(cwn[:, :, 1], cwn[:, :, 1], 1.0, None, ALU.add).then_inc(s_vc, 1)
            dve.wait_ge(s_rank, 2)
            link(V.tensor_tensor_scan(PI, ONE, ps[7], 0.0, ALU.mult, ALU.add))
            PI3 = PI.rearrange("p (e t) -> p e t", e=E)
            V.tensor_tensor(PA, ps[6], PI, ALU.add)
            link(V.tensor_copy(e9[:, 1:E + 1], PI3[:, :, NT - 1]))
            cnt, qf, gt, nt, pad = e8
            V.tensor_tensor(PA, ps[7], PA, ALU.subtract)
            link(V.tensor_tensor(cnt, e9[:, 1:E + 1], e9[:, 0:E], ALU.subtract))
            link(V.tensor_scalar(qf, cnt, float(FT - 1), 1.0 / FT, ALU.add, ALU.mult))
            link(V.tensor_copy(e8i, qf))
            link(V.tensor_copy(nt, e8i))
            link(V.tensor_tensor(gt, nt, qf, ALU.is_gt))
            link(V.tensor_tensor(nt, nt, gt, ALU.subtract))
            link(V.tensor_scalar(nt, nt, 1.0, None, ALU.max))
            link(V.tensor_tensor_scan(ts9[:, 1:E + 1], ONE[:, 0:E], nt, 0.0, ALU.mult, ALU.add))
            V.tensor_copy(tsi[:, :], ts9)
            link(V.scalar_tensor_tensor(pad, ts9[:, 0:E], float(FT), e9[:, 0:E], ALU.mult, ALU.subtract))
            PA3 = PA.rearrange("p (e t) -> p e t", e=E)
            link(V.tensor_tensor(PA3, pad.rearrange("p (e o) -> p e o", o=1).broadcast_to([P, E, NT]), PA3, ALU.subtract))
            link(V.tensor_tensor(PA, PA, OH, ALU.mult))
            link(V.tensor_reduce(lt[10], PA.rearrange("p (e t) -> p t e", e=E), AX_X, ALU.add))
            V.tensor_copy(posi[:, :], lt[10]).then_inc(s_pos, 1)

            def low(s, i):
                dve.wait_ge(s_hi[s], i + 1)
                V.tensor_tensor(xl[s], ps[s], xh[s].bitcast(F32), ALU.subtract).then_inc(s_lo[s], 1)

            def clamp(c, hb):
                dve.wait_ge(s_pr[0][hb], c + 1)
                if not isinstance(c, int) or c:
                    dve.wait_ge(s_exp[hb], c)
                V.tensor_scalar(mb[hb], ps[2 + hb], bdt[:, hb:hb + 1], SOFT, ALU.add, ALU.min).then_inc(s_min[hb], 1)
                dve.wait_ge(s_min[hb], c + 1)
                V.scalar_tensor_tensor(junk, ps[2 + hb], bdt[:, hb:hb + 1], mb[hb], ALU.add, ALU.subtract,
                                       accum_out=acc2[:, hb, bass.ds(c, 1)]).then_inc(s_dte[hb], 1)

            def step(s, i, last=False):
                c = i * 2 + s
                clamp(c, 0)
                if not last:
                    low(1 - s, i + s)
                clamp(c, 1)
                for hb in range(HB):
                    dve.wait_ge(s_pr[1][hb], c + 1)
                    V.tensor_scalar(RB[:, hb, bass.ds(c * CH, CH)], ps[4 + hb], bx[:, hb:hb + 1], None, ALU.add
                                    ).then_inc(s_ue[hb], 1)

            low(0, 0)
            step(0, 0)
            step(1, 0)
            with dve.Fori(1, NCH // 2 - 1) as i:
                step(0, i)
                step(1, i)
            step(0, NCH // 2 - 1)
            step(1, NCH // 2 - 1, last=True)

            def split_low(k):
                V.tensor_tensor(W1l[k % 3], W1RAW[raw_slot(k)], W1h[k % 3].bitcast(F32), ALU.subtract).then_inc(s_ws, 1)

            for k in range(2):
                dve.wait_ge(s_wsh, k + 1)
                split_low(k)
            bounds = expert_bounds(dve)
            for hb in range(HB):
                dve.wait_ge(s_dte[hb], NCH)
                dve.wait_ge(s_ln[hb], NCH)
                dve.wait_ge(s_ue[hb], NCH)
            V.tensor_reduce(dtv[:, :, 0], acc1[:, :, :], AX_X, ALU.add)
            link(V.tensor_reduce(dtv[:, :, 1], acc2[:, :, :], AX_X, ALU.add))
            link(V.tensor_tensor(dtv[:, :, 0], dtv[:, :, 0], dtv[:, :, 1], ALU.add))
            link(V.tensor_scalar(dtv[:, :, 0], dtv[:, :, 0], 1.0 / NTOK, DT_MIN, ALU.mult, ALU.max))
            link(V.tensor_scalar(dtv[:, :, 0], dtv[:, :, 0], DT_MAX, None, ALU.min))
            dve.wait_ge(s_asq, 2)
            link(V.tensor_tensor(Aneg[:, :, :], sv[:, :, :], sv2[:, :, :], ALU.add))
            link(V.tensor_scalar(Aneg[:, :, :], Aneg[:, :, :], -1.0, None, ALU.mult))
            for hb in range(HB):
                link(V.tensor_scalar(aval[:, hb, :], Aneg[:, hb, :], dtv[:, hb, 0:1], None, ALU.mult))

            def split_weights(k):
                dve.wait_ge(s_w1[raw_slot(k)], 16 * raw_loads(k))
                if k >= 3:
                    dve.wait_ge(s_m2, bounds[k - 2])
                dve.sem_inc(s_step2, 1)
                V.tensor_copy(W1h[k % 3], W1RAW[raw_slot(k)]).then_inc(s_wsh, 1)
                dve.wait_ge(s_wsh, k + 1)
                split_low(k)

            dve.wait_ge(s_ws, 2)

            for hb in range(HB):
                for n in range(NGATE):
                    c = gate_cols(n)
                    u, z = RB[:, hb, c], RC[:, hb, c]
                    u3 = u.rearrange("p (b l) -> p b l", l=L)
                    t3 = TG.rearrange("p (b l) -> p b l", l=L)
                    link(V.tensor_scalar(TG, u, cwn[:, hb, 1:2], cbn[:, hb:hb + 1], ALU.mult, ALU.add))
                    link(V.scalar_tensor_tensor(t3[:, :, 1:L], u3[:, :, 0:L - 1], cwn[:, hb, 0:1], t3[:, :, 1:L],
                                                ALU.mult, ALU.add))
                    link(V.scalar_tensor_tensor(t3[:, :, 0:L - 1], u3[:, :, 1:L], cwn[:, hb, 2:3], t3[:, :, 0:L - 1],
                                                ALU.mult, ALU.add))
                    dve.wait_ge(s_sig, hb * NGATE + n + 1)
                    link(V.tensor_tensor(TG, TG, z, ALU.mult))
                    link(V.tensor_tensor(z, u, TG, ALU.subtract))
                    if hb == 0 and n == 0:
                        dve.wait_ge(s_scat, 16 * NT)
                        dve.wait_ge(s_xin[0], 16 * NCH // 2)
                        dve.wait_ge(s_xin[1], 16 * NCH // 2)
                    w = GB * NC
                    link(V.transpose(UT[hb][:, :, n * w:(n + 1) * w].rearrange("p g c -> p c g"),
                                     z.rearrange("p (c i) -> p c i", i=Q)))
                    if hb == 0 and n == 0:
                        split_weights(2)

            dve.wait_ge(s_jv, 2)
            av = aval[:, :, :].rearrange("p b (s o) -> p b s o", o=1)
            for hb in range(HB):
                V.tensor_tensor(EX[:, hb], av[:, hb].broadcast_to([P, S, Q + 1]),
                                jv[:, :].rearrange("p (o j) -> p o j", o=1).broadcast_to([P, S, Q + 1]), ALU.mult)
                ins = V.tensor_tensor(ER[:, hb], av[:, hb].broadcast_to([P, S, Q]),
                                      jr[:, :].rearrange("p (o j) -> p o j", o=1).broadcast_to([P, S, Q]), ALU.mult)
            ins.then_inc(s_earg, 1)
            V.memset(INTRA.rearrange("p g m -> p (g m)"), 0.0)
            V.memset(INJ.rearrange("p g m -> p (g m)"), 0.0)
            V.memset(KP.rearrange("p b j -> p (b j)"), 0.0)
            V.memset(READ.rearrange("p g m -> p (g m)"), 0.0)
            dve.wait_ge(s_const, 6)
            link(V.tensor_copy(bop[:, :], bo[:, :]))
            link(V.tensor_tensor(bor[:, :], bo[:, :], bop[:, :], ALU.subtract))
            V.tensor_copy(bop[Q:2 * Q, :], bor[Q:2 * Q, :])
            link(V.tensor_copy(bop[2 * Q:, :], bor[2 * Q:, :]))
            link(V.tensor_tensor(bor[2 * Q:, :], bor[2 * Q:, :], bop[2 * Q:, :], ALU.subtract))
            link(V.tensor_copy(bop[2 * Q:, :], bor[2 * Q:, :]))
            link(V.tensor_reduce(half4[:, :, :], identity[:, :].rearrange("p (q h s) -> p h q s", q=NQ, h=2), AX_X, ALU.add))
            link(V.tensor_reduce(half[:, :], half4[:, :, :], AX_X, ALU.add))
            for k in range(3, E + 1):
                split_weights(k)
            dve.wait_ge(s_eexp, 1)
            V.tensor_scalar(sv[:, :, :], EX[:, :, :, 1], -1.0, None, ALU.add)
            link(V.tensor_scalar(sv2[:, :, :], Aneg[:, :, :], 1e-6, None, ALU.add))
            link(V.reciprocal(sv2[:, :, :], sv2[:, :, :]))
            link(V.tensor_tensor(sv[:, :, :], sv[:, :, :], sv2[:, :, :], ALU.mult))
            link(V.tensor_tensor(sv[:, :, :], sv[:, :, :], Bssm[:, :, :], ALU.mult))
            link(V.tensor_tensor(sv2[:, :, :], sv[:, :, :], Cssm[:, :, :], ALU.mult))
            KT = TA[:, 0:HB * Q * S].rearrange("p (b j s) -> p b j s", b=HB, s=S)
            for hb in range(HB):
                ins = V.tensor_tensor(KT[:, hb], EX[:, hb, :, 0:Q].rearrange("p s j -> p j s"),
                                      sv2[:, hb, :].rearrange("p (o s) -> p o s", o=1).broadcast_to([P, Q, S]), ALU.mult)
            link(ins)
            for hb in range(HB):
                ins = V.tensor_reduce(KP[:, hb, Q - 1:2 * Q - 1], KT[:, hb], AX_X, ALU.add)
            link(ins)
            TO = TA[:, 0:HB * Q * Q].rearrange("p (b i j) -> p b i j", b=HB, j=Q)
            TT = TB[:, 0:HB * Q * Q].rearrange("p (b g i) -> p b g i", b=HB, i=Q)
            for j in range(Q):
                ins = V.tensor_copy(TO[:, :, :, j], KP[:, :, Q - 1 - j:2 * Q - 1 - j])
            link(ins)
            link(V.transpose(TB[:, 0:HB * Q * Q].rearrange("p (b g i) -> p b i g", b=HB, i=Q), TO))
            IN5 = RB[:, 0, :].rearrange("p (b g q i) -> p b g q i", b=HB, q=NQ, i=Q)
            for q in range(NQ):
                r = slice(Q * q, Q * q + Q)
                for hb in range(HB):
                    ins = V.tensor_copy(IN5[r, hb, :, q, :], TT[r, hb])
            link(ins)
            IE = TA[:, 0:HB * S * Q].rearrange("p (b s j) -> p b s j", b=HB, s=S)
            IT = TB[:, 0:HB * S * Q].rearrange("p (b g s) -> p b g s", b=HB, s=S)
            for hb in range(HB):
                ins = V.tensor_tensor(IE[:, hb], ER[:, hb],
                                      sv[:, hb, :].rearrange("p (s o) -> p s o", o=1).broadcast_to([P, S, Q]), ALU.mult)
            link(ins)
            link(V.transpose(TB[:, 0:HB * S * Q].rearrange("p (b g s) -> p b s g", b=HB, s=S), IE))
            INJ5 = INJ.rearrange("p (b g) (q s) -> p b g q s", b=HB, q=NQ)
            for q in range(NQ):
                r = slice(Q * q, Q * q + Q)
                for hb in range(HB):
                    ins = V.tensor_copy(INJ5[r, hb, :, q, :], IT[r, hb])
            link(ins)
            RD = TA.rearrange("p (b i x) -> p b i x", b=HB, x=Q)
            for hb in range(HB):
                for rep in range(Q // S):
                    V.tensor_tensor(RD[:, hb, 0:Q, rep * S:(rep + 1) * S],
                                    EX[:, hb, :, 1:Q + 1].rearrange("p s j -> p j s"),
                                    Cssm[:, hb, :].rearrange("p (o s) -> p o s", o=1).broadcast_to([P, Q, S]), ALU.mult)
                    ins = V.tensor_copy(RD[:, hb, Q, rep * S:(rep + 1) * S], EX[:, hb, :, Q])
            link(ins)
            for hb in range(HB):
                ins = V.transpose(TB.rearrange("p (b g i) -> p b i g", b=HB, i=Q + 1)[:, hb],
                                  RD[:, hb])
            link(ins)
            RT = TB.rearrange("p (r a i) -> p a r i", a=2, i=Q + 1)
            for ab in range(2):
                for q in range(NQ):
                    src = slice(Q * q, Q * (q + 1))
                    dst = slice(Q * (2 * ab + q // 2), Q * (2 * ab + q // 2 + 1))
                    V.tensor_scalar(READ[dst, :, q * Q:(q + 1) * Q], RT[src, ab, :, 0:Q], half[src, q % 2:q % 2 + 1], None,
                                    ALU.mult)
                    ins = V.tensor_scalar(AP2[dst, q % 2, :], RT[src, ab, :, Q], half[src, q % 2:q % 2 + 1], None, ALU.mult)
            link(ins)
            link(V.tensor_tensor(A32[:, :], AP2[:, 0, :], AP2[:, 1, :], ALU.add))
            dve.wait_ge(s_re[0], bounds[E] * KB)
            for n in range(2):
                ins = V.memset(ps[n][:, 0:BC].rearrange("p (b c) -> p b c", c=NC)[:, :, 0], 0.0)
            ins.then_inc(s_mat, 1)

            def y_piece(hb, n):
                if n == 0:
                    dve.wait_ge(s_yev, (hb + 1) * PPB)
                w = BC // NYP
                V.transpose(YT[hb][:, n * w * Q:(n + 1) * w * Q].rearrange("p (c i) -> p c i", i=Q),
                            UT[hb][:, :, n * w:(n + 1) * w].rearrange("p g c -> p c g")).then_inc(s_ytr, 1)

            dve.wait_ge(s_m2, bounds[E])
            for r in range(NPAIR):
                if r >= 2:
                    dve.wait_ge(s_yps, r - 1)
                V.tensor_scalar(D0[r % 2], cmask[:, :], A32[:, r:r + 1], None, ALU.mult).then_inc(s_d0, 1)
                dve.wait_ge(s_d0, r + 1)
                dve.wait_ge(s_inj, r + 1)
                V.tensor_tensor_scan(SX[r % 2], D0[r % 2], ps[r % 2][:, 0:BC], 0.0, ALU.mult, ALU.add).then_inc(s_scan, 1)
                if 1 <= r - PPB <= NYP:
                    y_piece(0, r - PPB - 1)
            for n in range(NYP):
                y_piece(1, n)

            lng_b = lng[:, :].rearrange("p (o d) -> p o d", o=1).broadcast_to([P, TB8, D])

            def sums(n):
                dve.wait_ge(s_xa, n + 1)
                vv, st, f = VV[n % NV], FST[n % 2], fs[n % 3]
                for j in range(2):
                    dve.wait_ge(s_po, 2 * n + j + 1)
                    half = vv[:, j * 4:(j + 1) * 4, :]
                    ins = V.tensor_tensor(half, ps[4 + (2 * n + j) % 4].rearrange("p (t d) -> p t d", d=D), half, ALU.add)
                    ins.then_inc(s_v, 1)
                dve.wait_ge(s_v, 2 * n + 2)
                for t in range(TB8):
                    ins = V.bn_stats(st[:, t, :], vv[:, t, :])
                link(ins)
                if n >= 3:
                    dve.wait_ge(s_fn, n - 2)
                variance(st[:, :, :], f[0][:, :], f[1][:, :], f[2][:, :], f[4][:, :])
                V.tensor_scalar(f[1][:, :], f[2][:, :], EPS, None, ALU.add).then_inc(s_fv, 1)

            def finish(n):
                vv = VV[n % NV]
                dve.wait_ge(s_fn, n + 1)
                dve.wait_ge(s_fp, n + 1)
                V.tensor_tensor(vv, vv, lng_b, ALU.mult).then_inc(s_fg, 1)

            sums(0)
            for n in range(NB8):
                f = fs[n % 3]
                dve.wait_ge(s_fy, n + 1)
                refine(f[1][:, :], f[3][:, :], f[2][:, :], f[4][:, :])
                V.scalar_tensor_tensor(f[4][:, :], f[0][:, :], -1.0, f[3][:, :], ALU.mult, ALU.mult).then_inc(s_fr, 1)
                dve.wait_ge(s_fr, n + 1)
                vv = VV[n % NV]
                for t in range(TB8 - AV, TB8):
                    ins = V.tensor_scalar(vv[:, t, :], vv[:, t, :], f[3][:, t:t + 1], f[4][:, t:t + 1], ALU.mult, ALU.add)
                ins.then_inc(s_fp, 1)
                if n + 1 < NB8:
                    sums(n + 1)
                if n >= 1:
                    finish(n - 1)
            finish(NB8 - 1)

        @block.tensor
        def _(pe):
            T = nc.tensor
            pe.wait_ge(s_const, 6)
            pe.wait_ge(s_wraw, 64)
            for n in range(4 * HB):
                T.transpose(ps[n // 4][:, (n % 4) * P:(n % 4 + 1) * P], WRAW[:, n, :], identity[:, :]).then_inc(s_wt, 1)
            pe.wait_ge(s_small, 16 * NSMALL)
            R = 8 + E * KB
            T.transpose(ps[2][:, 0:R], vrows[:, :], identity[0:R, 0:R]).then_inc(s_vt, 1)
            pe.wait_ge(s_oh, 1)
            T.matmul(ps[6], ULT, OH, start=True, stop=True).then_inc(s_rank, 1)
            T.matmul(ps[7], ONEB, OH, start=True, stop=True).then_inc(s_rank, 1)

            def transpose_chunk(s, i):
                pe.wait_ge(s_xin[s], (i + 1) * 16)
                if not isinstance(i, int) or i:
                    pe.wait_ge(s_lo[s], i)
                for t in range(TPC):
                    ins = T.transpose(ps[s][:, t * P:(t + 1) * P], xin[s][:, t, :], identity[:, :])
                ins.then_inc(s_xt[s], 1)

            def project(s, i):
                c = i * 2 + s
                pe.wait_ge(s_lo[s], i + 1)
                for j in range(3):
                    free = (s_dte, s_ue, s_ge)[j]
                    for hb in range(HB):
                        if not isinstance(c, int) or c:
                            pe.wait_ge(free[hb], c)
                        n, bank = j * HB + hb, ps[2 + 2 * j + hb]
                        T.matmul(bank, PW[:, 0, n, :], xh[s], start=True, stop=False)
                        T.matmul(bank, PW[:, 0, n, :], xl[s], start=False, stop=False)
                        T.matmul(bank, PW[:, 1, n, :], xh[s], start=False, stop=True).then_inc(s_pr[j][hb], 1)

            pe.wait_ge(s_wl, 2)
            transpose_chunk(0, 0)
            transpose_chunk(1, 0)
            pe.wait_ge(s_vc, 1)
            pe.wait_ge(s_pos, 1)
            project(0, 0)
            bounds = expert_bounds(pe)
            transpose_chunk(0, 1)
            project(1, 0)
            with pe.Fori(1, NCH // 2 - 1) as i:
                transpose_chunk(1, i)
                project(0, i)
                transpose_chunk(0, i + 1)
                project(1, i)
            i = NCH // 2 - 1
            transpose_chunk(1, i)
            project(0, i)
            project(1, i)

            def transpose_tile(i):
                pe.wait_ge(s_sp, i + 1)
                for v in range(2):
                    for h in range(FH):
                        ins = T.transpose(ps[4][:, (v * FH + h) * P:(v * FH + h + 1) * P],
                                          XSPLIT[:, v, h, :].bitcast(F32), identity[:, :])
                ins.then_inc(s_tt, 1)

            for hb in range(HB):
                pe.wait_ge(s_ue[hb], NCH)
            transpose_tile(0)
            for hb in range(HB):
                for f in (s_dte, s_ge):
                    pe.wait_ge(f[hb], NCH)
            for g in range(E):
                pe.wait_ge(s_ws, min(g + 2, E + 1))
                pe.wait_ge(s_w2[g % 3], 32 * (g // 3 + 1))
                pe.wait_ge(s_w2[(g + 1) % 3], 32 * ((g + 1) // 3 + 1))
                with pe.Fori(bounds[g], bounds[g + 1]) as i:
                    pe.wait_ge(s_xtr, i + 1)
                    for n in range(2):
                        slot = (g + n) % 3
                        for k in range(KB):
                            bank = ps[2 * n + k // 2][:, (k % 2) * FT:(k % 2 + 1) * FT]
                            w = slice(k * P, (k + 1) * P)
                            T.matmul(bank, W1h[slot][:, w], XT[:, 0:FT], start=True, stop=False)
                            T.matmul(bank, W1h[slot][:, w], XT[:, FT:2 * FT], start=False, stop=False)
                            T.matmul(bank, W1l[slot][:, w], XT[:, 0:FT], start=False, stop=True).then_inc(s_m1[n], 1)
                    transpose_tile(i + 1)
                    pe.wait_ge(s_ysb, i + 1)
                    for n in range(2):
                        slot = (g + n) % 3
                        for k in range(KB):
                            pe.wait_ge(s_re[n], i * KB + (k + 1))
                            for h in range(FH):
                                ins = T.matmul(ps[5 + h][:, 0:D], HID[n][:, k, h * P:(h + 1) * P], W2S[slot][:, k, :],
                                               start=(n == 0 and k == 0), stop=(n == 1 and k == KB - 1))
                    ins.then_inc(s_m2, 1)

            pe.wait_ge(s_mat, 1)

            def inject(r):
                hb, rp = divmod(r, PPB)
                if r >= 2:
                    pe.wait_ge(s_scan, r - 1)
                for ab in range(2):
                    g = 2 * rp + ab
                    u = UT[hb][:, g, :].rearrange("p (b c) -> p b c", c=NC)[:, :, 0:NC - 1]
                    dst = ps[r % 2][64 * ab:64 * ab + 64, 0:BC].rearrange("p (b c) -> p b c", c=NC)[:, :, 1:NC]
                    ins = T.matmul(dst, INJ[:, hb * NG + g, :], u, start=True, stop=True)
                ins.then_inc(s_inj, 1)

            inject(0)
            for r in range(NPAIR):
                hb, rp = divmod(r, PPB)
                if r >= 3:
                    pe.wait_ge(s_yev, r - 2)
                if r + 1 < NPAIR:
                    inject(r + 1)
                if r == 1:
                    pe.wait_ge(s_xtr, bounds[E] + 1)
                    pe.wait_ge(s_ysb, bounds[E] + 1)
                banks = [ps[2 + 2 * (r % 3) + ab][:, 0:BC] for ab in range(2)]
                for ab in range(2):
                    g = 2 * rp + ab
                    T.matmul(banks[ab], INTRA[:, hb * NG + g, :], UT[hb][:, g, :], start=True, stop=False)
                pe.wait_ge(s_scan, r + 1)
                for ab in range(2):
                    rows = slice(64 * ab, 64 * ab + 64)
                    ins = T.matmul(banks[ab], READ[rows, r, :], SX[r % 2][rows, :], start=False, stop=True)
                ins.then_inc(s_yps, 1)

            pe.wait_ge(s_yev, NPAIR)
            for n in range(NT // 4):
                pe.wait_ge(s_ytr, NYP + n * NYP // (NT // 4) + 1)
                if n >= 4:
                    pe.wait_ge(s_v, n - 3)
                for t in range(4):
                    tt = 4 * n + t
                    dst = ps[4 + n % 4][:, t * D:(t + 1) * D]
                    T.matmul(dst, first[:, :], bop[:, :], start=True, stop=False)
                    for hb in range(HB):
                        ins = T.matmul(dst, YT[hb][:, tt * P:(tt + 1) * P], WoT[:, hb, :], start=False, stop=(hb == HB - 1))
                ins.then_inc(s_po, 1)


_INS = ['x', 'W_x', 'b_x', 'W_g', 'b_g', 'conv_w', 'conv_b', 'A_raw', 'B_ssm', 'C_ssm', 'W_dt', 'b_dt', 'W_out', 'b_out',
        'ln_g', 'ln_b']
_INS = ['L0_attn_' + n for n in _INS] + ['L0_ffn_' + n for n in ('W1', 'b1', 'W2', 'b2')]
_OUTS = [((32, 256, 128), 'float32')]


def kernel(**inputs):
    import numpy as _np
    import concourse.bacc as _bacc
    from concourse import mybir as _mybir
    from concourse.bass_utils import run_bass_kernel_spmd as _run

    nc = _bacc.Bacc("TRN2", target_bir_lowering=False, num_devices=1, dynamic_dma_scratch_size=8192)
    arrays, args = {}, []
    for name in _INS:
        a = _np.ascontiguousarray(inputs[name])
        arrays[f"in_{name}_dram"] = a
        args.append(nc.dram_tensor(f"in_{name}_dram", a.shape, _mybir.dt.from_np(a.dtype), kind="ExternalInput").ap())
    for i, (shape, dtype) in enumerate(_OUTS):
        dt = _mybir.dt.from_np(_np.dtype(dtype))
        args.append(nc.dram_tensor(f"out_{i}_dram", shape, dt, kind="ExternalOutput").ap())
    ssm_moe_layer(nc, *args)
    r = _run(nc, [arrays], core_ids=[0])
    got = tuple(r.results[0][f"out_{i}_dram"] for i in range(len(_OUTS)))
    return got[0]
```

```python
from contextlib import ExitStack

import concourse.bass as bass
from concourse import mybir

ALU = mybir.AluOpType
ACT = mybir.ActivationFunctionType
AX_X = mybir.AxisListType.X
F32 = mybir.dt.float32
F32R = mybir.dt.float32r
BF16 = mybir.dt.bfloat16
I32 = mybir.dt.int32
U32 = mybir.dt.uint32

P = 128
Q = 32
NQ = P // Q
FT = 256
EPS = 1e-5
SOFT = 20.0
DT_MIN, DT_MAX = 0.001, 2.0


def ssm_moe_layer(nc, x, W_x, b_x, W_g, b_g, conv_w, conv_b, A_raw, B_ssm, C_ssm, W_dt, b_dt,
                  W_out, b_out, ln_g, ln_b, W1, b1, W2, b2, out):
    B, L, D = x.shape
    H, S = A_raw.shape
    E, _, DFF = W1.shape
    assert D == P and H % P == 0 and DFF % P == 0 and L % P == 0
    NTOK = B * L
    NT = NTOK // P
    HB = H // P
    KB = DFF // P
    NC = L // Q
    BC = B * NC
    CH = 512
    NCH = NTOK // CH
    TPC = CH // P
    NG = P // NQ
    NPAIR = HB * NG // 2
    PPB = NG // 2
    MAXT = (NTOK + E * (FT - 1)) // FT
    ROWS = (MAXT + 2) * FT
    QT = 4
    TQ = NT // QT
    NACT = 11
    GB = 4
    NGATE = B // GB
    FH = FT // P
    NPM = 6
    AVF = 3
    NYP = 8

    with ExitStack() as ctx:
        def sb(name, shape, dt=F32):
            return ctx.enter_context(nc.sbuf_tensor(name, shape, dt))

        def sem(name):
            return ctx.enter_context(nc.semaphore(name))

        xs_dram = nc.dram_tensor("sorted_tokens", [ROWS, D], F32).ap()
        ys_dram = nc.dram_tensor("sorted_outputs", [ROWS, D], F32).ap()

        RA = sb("RA", [P, NTOK])
        RB = sb("RB", [P, HB, NTOK])
        RC = sb("RC", [P, HB, NTOK])
        XN = RA[:, :].rearrange("p (t d) -> p t d", d=D)
        UT = [RA[:, :].rearrange("p (g c) -> p g c", g=NG), RC[:, 0, :].rearrange("p (g c) -> p g c", g=NG)]
        YT = [RC[:, 1, :], RA[:, :]]
        INTRA = RB[:, 0, :].rearrange("p (g m) -> p g m", m=P)
        NGRP = HB * NG
        INJ = RB[:, 1, 0:NGRP * NQ * S].rearrange("p (g m) -> p g m", m=NQ * S)
        READ = RB[:, 1, NGRP * NQ * S:NGRP * NQ * S + NPAIR * P].rearrange("p (r m) -> p r m", m=P)

        RR = sb("RR", [P, 7 * CH], F32R)
        xh = [RR[:, s * CH:(s + 1) * CH] for s in range(2)]
        xl = [RR[:, (2 + s) * CH:(3 + s) * CH] for s in range(2)]
        PW = RR[:, 4 * CH:4 * CH + 2 * 3 * HB * P].rearrange("p (v j m) -> p v j m", v=2, m=P)
        W1h = [RR[:, o * DFF:(o + 1) * DFF] for o in (0, 1, 4)]
        W1l = [RR[:, o * DFF:(o + 1) * DFF] for o in (2, 3, 5)]
        XT = RR[:, 6 * DFF:6 * DFF + 2 * FT]
        XTF = sb("XTF", [P, FT])

        AR = sb("AR", [P, 11 * CH])
        xin = [AR[:, s * CH:(s + 1) * CH].rearrange("p (t d) -> p t d", d=D) for s in range(2)]
        mb = [AR[:, (2 + s) * CH:(3 + s) * CH] for s in range(2)]
        eb = [AR[:, (4 + s) * CH:(5 + s) * CH] for s in range(2)]
        junk = AR[:, 6 * CH:7 * CH]
        W2S = [AR[:, s * DFF:(s + 1) * DFF].rearrange("p (k d) -> p k d", k=KB) for s in range(3)]
        W1RAW = [AR[:, 3 * CH:4 * CH], AR[:, 9 * CH:10 * CH], AR[:, 10 * CH:11 * CH]]

        def raw_slot(k):
            return k + 1 if k < 2 else 0 if k == 2 else k % 3

        def raw_loads(k):
            return sum(raw_slot(j) == raw_slot(k) for j in range(k + 1))

        HID = [AR[:, (4 + 2 * n) * CH:(6 + 2 * n) * CH].rearrange("p (k t) -> p k t", k=KB) for n in range(2)]
        XSIN = AR[:, 8 * CH:8 * CH + FT].rearrange("p (h d) -> p h d", h=FH)
        YSB = AR[:, 8 * CH + FT:9 * CH].rearrange("p (h d) -> p h d", h=FH)
        TG = AR[:, 9 * CH:11 * CH]

        identity = sb("identity", [P, P])
        vrows = sb("vrows", [8 + E * KB, P])
        VC = sb("VC", [P, 8 + E * KB])
        bx, bg, bdt, cb = (VC[:, 2 * n:2 * n + 2] for n in range(4))
        B1C = VC[:, 8:8 + E * KB].rearrange("p (e k) -> p e k", e=E)
        cw = sb("cw", [P, HB, 3])
        cwn = sb("cwn", [P, HB, 3])
        cbn = sb("cbn", [P, HB])
        WoT = sb("WoT", [P, HB, D])
        b2s = sb("b2s", [P, 3, D])
        b2p = sb("b2p", [P, D])
        lng = sb("lng", [P, D])
        lnb = sb("lnb", [P, D])
        bo = sb("bo", [P, D])
        bor = sb("bor", [P, D])
        bop = sb("bop", [P, D], BF16)
        first = sb("first", [P, P], BF16)
        bdtm = sb("bdtm", [P, HB])
        Araw = sb("Araw", [P, HB, S])
        Bssm = sb("Bssm", [P, HB, S])
        Cssm = sb("Cssm", [P, HB, S])
        Aneg = sb("Aneg", [P, HB, S])
        aval = sb("aval", [P, HB, S])
        sv = sb("sv", [P, HB, S])
        sv2 = sb("sv2", [P, HB, S])
        acc1 = sb("acc1", [P, HB, NCH])
        acc2 = sb("acc2", [P, HB, NCH])
        dtv = sb("dtv", [P, HB, 2])
        mean = sb("mean", [P, NT])
        rstd = sb("rstd", [P, NT])
        nmr = sb("nmr", [P, NT])
        posi = sb("posi", [P, NT], U32)
        tsi = sb("tsi", [P, E + 1], I32)
        cmask = sb("cmask", [P, B * NC], BF16)
        A32 = sb("A32", [P, NPAIR])
        AP2 = sb("AP2", [P, 2, NPAIR])
        half4 = sb("half4", [P, 2, NQ])
        half = sb("half", [P, 2])
        jv = sb("jv", [P, Q + 1])
        jr = sb("jr", [P, Q])
        FST = [sb(f"FST{k}", [P, 8, 6]) for k in range(2)]
        fs = [[sb(f"fs{n}_{k}", [P, 8]) for n in range(5)] for k in range(3)]

        o = [0]

        def carve(region, n, dt=F32):
            a = region[:, o[0]:o[0] + n]
            o[0] += n
            return a if dt == F32 else a.bitcast(dt)

        RC1 = RC[:, 1, :]
        ZERO = carve(RC1, 10 * D)
        ST = carve(RC1, NT * 6).rearrange("p (t k) -> p t k", k=6)
        lt = [carve(RC1, NT) for _ in range(12)]
        ti = carve(RC1, NT, I32)
        OH = carve(RC1, E * NT // 2, BF16)
        PI = carve(RC1, E * NT)
        PA = carve(RC1, E * NT)
        ONE = carve(RC1, E * NT)
        ULT = carve(RC1, P // 2, BF16)
        ONEB = carve(RC1, P // 2, BF16)
        e9 = carve(RC1, E + 1)
        ts9 = carve(RC1, E + 1)
        e8 = [carve(RC1, E) for _ in range(5)]
        e8i = carve(RC1, E, I32)
        WRAW = carve(RC1, (3 * HB + HB) * D).rearrange("p (j d) -> p j d", d=D)

        NS2 = HB * S * (Q + 1)
        o[0] = 0
        EX = carve(RC1, NS2).rearrange("p (b s j) -> p b s j", b=HB, s=S)
        ER = carve(RC1, HB * S * Q).rearrange("p (b s j) -> p b s j", b=HB, s=S)
        KP = carve(RC1, HB * (2 * Q - 1)).rearrange("p (b j) -> p b j", b=HB)
        TA = carve(RC1, HB * (Q + 1) * Q)
        TB = carve(RC1, HB * (Q + 1) * Q)
        D0 = [AR[:, n * BC:(n + 1) * BC] for n in range(2)]
        SX = [AR[:, (2 + n) * BC:(3 + n) * BC] for n in range(2)]

        TB8 = 8
        NB8 = NT // TB8
        TC = TB8 * D

        def batch(region, k):
            return region[:, k * TC:(k + 1) * TC].rearrange("p (t d) -> p t d", d=D)

        NAR = NB8 // 2
        GA = [batch(AR[:, 2 * CH:], n) for n in range(NAR)] + [batch(RB[:, 0, 0:NTOK // 2], n) for n in range(NB8 - NAR)]
        TH = NTOK // 4
        VV = [batch(RB[:, 1, o4:], k) for o4 in (0, 2 * TH, TH, 3 * TH) for k in range(2)]
        assert NB8 == 8 and NG * P == NTOK // 2 and NG * NQ * S == NTOK // 4 and PPB * P == NTOK // 4
        PS = ctx.enter_context(nc.psum_tensor("PS", [P, 8, 512], F32))
        ps = [PS[:, n, :] for n in range(8)]

        lng_b = lng[:, :].rearrange("p (o d) -> p o d", o=1).broadcast_to([P, TB8, D])

        def vpsum(n, t):
            return ps[(2 * n + t // 4) % 8][:, (t % 4) * D:(t % 4 + 1) * D]

        s_x = [sem(f"x_loaded_{q}") for q in range(QT)]
        s_small = sem("small_loaded")
        s_wraw = sem("weights_loaded")
        s_const = sem("pool_constants")
        s_dve = sem("vector_chain")
        s_act = sem("scalar_chain")
        s_lnv = sem("variance_ready")
        s_lny = sem("rstd_estimate_ready")
        s_nmr = sem("scales_ready")
        s_nrm = sem("xn_quarter_ready_vector")
        s_nra = sem("xn_quarter_ready_scalar")
        s_wsh = sem("w1_high_ready")
        s_step = sem("pool_steps")
        s_step2 = sem("vector_steps")
        s_fg = sem("last_scaled")
        s_fp = sem("last_part_normalised_vector")
        s_actl = sem("last_log_ready")
        s_wt = sem("weights_transposed")
        s_wh = sem("weights_high_ready")
        s_wl = sem("weights_low_ready")
        s_vt = sem("vectors_transposed")
        s_vc = sem("vectors_ready")
        s_zero = sem("zero_tile_ready")
        s_fill = sem("sorted_tokens_cleared")
        s_oh = sem("one_hot_ready")
        s_rank = sem("ranks_ready")
        s_bnd = sem("group_bounds_ready")
        s_pos = sem("positions_ready")
        s_scat = sem("tokens_scattered")
        s_xin = [sem(f"chunk_copied_{s}") for s in range(2)]
        s_xt = [sem(f"chunk_transposed_{s}") for s in range(2)]
        s_hi = [sem(f"chunk_high_ready_{s}") for s in range(2)]
        s_lo = [sem(f"chunk_low_ready_{s}") for s in range(2)]
        s_pr = [[sem(f"projected_{n}_{hb}") for hb in range(HB)] for n in ("dt", "u", "g")]
        s_min = [sem(f"clamped_ready_{hb}") for hb in range(HB)]
        s_dte = [sem(f"dt_bank_read_{hb}") for hb in range(HB)]
        s_ue = [sem(f"u_stored_{hb}") for hb in range(HB)]
        s_ge = [sem(f"z_stored_{hb}") for hb in range(HB)]
        s_exp = [sem(f"exp_ready_{hb}") for hb in range(HB)]
        s_ln = [sem(f"softplus_summed_{hb}") for hb in range(HB)]
        s_sig = sem("gate_piece_ready")
        s_asp = sem("a_softplus_input")
        s_asq = sem("a_softplus_done")
        s_earg = sem("exponents_ready")
        s_eexp = sem("decays_ready")
        s_jv = sem("iotas_ready")
        s_mat = sem("matrices_ready")
        s_w1 = [sem(f"w1_loaded_{s}") for s in range(3)]
        s_w2 = [sem(f"w2_loaded_{s}") for s in range(3)]
        s_ws = sem("w1_split")
        s_b2 = sem("b2_pair_ready")
        s_xs = sem("sorted_tile_loaded")
        s_tt = sem("sorted_tile_transposed")
        s_xtr = sem("sorted_tile_in_place")
        s_xlo = sem("sorted_tile_low_ready")
        s_m1 = [sem(f"expert_{n}_hidden") for n in "ab"]
        s_re = [sem(f"expert_{n}_relu") for n in "ab"]
        s_m2 = sem("expert_output_summed")
        s_ysb = sem("expert_output_in_sbuf")
        s_yad = sem("expert_bias_added")
        s_yst = sem("expert_output_stored")
        s_inj = sem("injection_ready")
        s_d0 = sem("decay_row_ready")
        s_scan = sem("states_ready")
        s_yps = sem("pair_output_ready")
        s_yev = sem("pair_output_in_sbuf")
        s_ytr = sem("y_piece_transposed")
        s_gat = [sem(f"expert_outputs_gathered_{n}") for n in range(NB8)]
        s_xr = [sem(f"x_reloaded_{n}") for n in range(NB8)]
        s_po = sem("projection_out_ready")
        s_xa = sem("xn_again_ready")
        s_fv = sem("last_variance_ready")
        s_fy = sem("last_rstd_estimate")
        s_fr = sem("last_scales_ready")
        s_fn = sem("last_normalised")
        s_base = sem("base_ready")
        s_fo = sem("output_ready")
        s_flast = sem("last_output_ready")
        s_out = sem("output_stored")

        x_v = x.rearrange("b (s p) d -> p (b s) d", p=P)
        out_v = out.rearrange("b (s p) d -> p (b s) d", p=P)
        xs_v = xs_dram.rearrange("(t h p) d -> t p h d", h=FH, p=P)
        ys_v = ys_dram.rearrange("(t h p) d -> t p h d", h=FH, p=P)
        xs_z = xs_dram.rearrange("(p r) d -> p (r d)", p=P)
        ZR = 10
        XSR = ROWS // P
        NZ = -(-XSR // ZR)
        YR = (ROWS - NTOK) // P
        assert ZR < YR <= 2 * ZR
        small = [(vrows[0:2, :], b_x.rearrange("(b p) -> b p", p=P)), (vrows[2:4, :], b_g.rearrange("(b p) -> b p", p=P)),
                 (vrows[4:6, :], b_dt.rearrange("(b p) -> b p", p=P)), (vrows[6:8, :], conv_b.rearrange("(b p) -> b p", p=P)),
                 (vrows[8:8 + E * KB, :], b1.rearrange("e (k p) -> (e k) p", p=P)),
                 (cw[:, :, :], conv_w.rearrange("(b p) o k -> p b (o k)", p=P)),
                 (Araw[:, :, :], A_raw.rearrange("(b p) s -> p b s", p=P)),
                 (Bssm[:, :, :], B_ssm.rearrange("(b p) s -> p b s", p=P)),
                 (Cssm[:, :, :], C_ssm.rearrange("(b p) s -> p b s", p=P)),
                 (lng[:, :], ln_g.rearrange("(o d) -> o d", o=1).broadcast_to([P, D])),
                 (lnb[:, :], ln_b.rearrange("(o d) -> o d", o=1).broadcast_to([P, D])),
                 (bo[:, :], b_out.rearrange("(o d) -> o d", o=1).broadcast_to([P, D]))]
        NSMALL = len(small)

        def gate_cols(n):
            return slice(n * GB * L, (n + 1) * GB * L)

        def expert_bounds(eng):
            eng.wait_ge(s_bnd, 1)
            return [0] + [eng.value_load(tsi[0:1, e:e + 1], min_val=e, max_val=MAXT) for e in range(1, E + 1)]

        block = ctx.enter_context(nc.Block())

        @block.sync
        def _(sp):
            sp.sem_inc(s_yst, 16)
            for q in range(QT):
                sp.dma_start(XN[:, q * TQ:(q + 1) * TQ, :], x_v[:, q * TQ:(q + 1) * TQ, :]).then_inc(s_x[q], 16)
            for dst, src in small:
                sp.dma_start(dst, src, allow_slow_non_contiguous=True).then_inc(s_small, 16)
            sp.wait_ge(s_zero, 1)
            for n in range(NZ):
                w = min(ZR, XSR - n * ZR) * D
                sp.dma_start(xs_z[:, n * ZR * D:n * ZR * D + w], ZERO[:, 0:w]).then_inc(s_fill, 16)
            sp.dma_start(ys_dram[NTOK:ROWS, :].rearrange("(p r) d -> p (r d)", p=P)[:, 0:ZR * D], ZERO).then_inc(s_fill, 16)
            sp.dma_start(ys_dram[NTOK:ROWS, :].rearrange("(p r) d -> p (r d)", p=P)[:, ZR * D:], ZERO[:, 0:YR * D - ZR * D]
                         ).then_inc(s_fill, 16)
            for k in range(2):
                sp.dma_start(W1RAW[raw_slot(k)], W1[k]).then_inc(s_w1[raw_slot(k)], 16)
            sp.wait_ge(s_nrm, 1)
            sp.wait_ge(s_nra, 1)
            for s in range(2):
                sp.dma_start(xin[s], XN[:, s * TPC:(s + 1) * TPC, :]).then_inc(s_xin[s], 16)
            sp.wait_ge(s_nrm, QT)
            sp.wait_ge(s_nra, QT)
            with sp.Fori(1, NCH // 2) as i:
                for s in range(2):
                    sp.wait_ge(s_xt[s], i)
                    sp.dma_start(xin[s], XN[:, bass.ds((i * 2 + s) * TPC, TPC), :]).then_inc(s_xin[s], 16)

            def load_w1(k):
                sp.dma_start(W1RAW[raw_slot(k)], W1[k % E]).then_inc(s_w1[raw_slot(k)], 16)

            def load_w2(k):
                sp.dma_start(W2S[k % 3], W2[k % E].rearrange("(k p) d -> p k d", p=P)).then_inc(s_w2[k % 3], 16)
                sp.dma_start(b2s[:, k % 3, :], b2[k % E:k % E + 1, :].broadcast_to([P, D])).then_inc(s_w2[k % 3], 16)

            bounds = expert_bounds(sp)
            sp.wait_ge(s_scat, 16 * NT)
            sp.dma_start(XSIN, xs_v[0]).then_inc(s_xs, 16)
            for s in range(2):
                sp.wait_ge(s_xt[s], NCH // 2)
                load_w2(s)
            sp.wait_ge(s_tt, 1)
            sp.dma_start(XSIN, xs_v[1]).then_inc(s_xs, 16)
            for hb in range(HB):
                sp.wait_ge(s_exp[hb], NCH)
                sp.wait_ge(s_dte[hb], NCH)
            load_w1(2)
            load_w2(2)
            w1_before = {1: [3], 2: [4, 5], 3: [6], 4: [7], 5: [8]}
            for g in range(E):
                if 1 <= g < E - 1:
                    sp.wait_ge(s_m2, bounds[g])
                    load_w2(g + 2)
                for k in w1_before.get(g, []):
                    if k == 4:
                        sp.wait_ge(s_earg, 1)
                    if k == 3 or k >= 6:
                        sp.wait_ge(s_ws, k if k == 3 else k - 2)
                    load_w1(k)
                with sp.Fori(bounds[g], bounds[g + 1]) as i:
                    sp.wait_ge(s_tt, i + 2)
                    sp.dma_start(XSIN, xs_v[bass.ds(i + 2, 1)].rearrange("o p h d -> p (o h) d")).then_inc(s_xs, 16)
                    sp.wait_ge(s_yad, i + 1)
                    sp.dma_start(ys_v[bass.ds(i, 1)].rearrange("o p h d -> p (o h) d"), YSB).then_inc(s_yst, 16)

            for n in range(NB8):
                if n % (NB8 // 2) == 0:
                    sp.wait_ge(s_yps, PPB if n == 0 else NPAIR)
                sp.dma_start(VV[n], x_v[:, n * TB8:(n + 1) * TB8, :]).then_inc(s_xr[n], 16)
            for n in range(NB8):
                if n == NB8 - 1:
                    sp.wait_ge(s_flast, 1)
                else:
                    sp.wait_ge(s_fo, n + 1)
                sp.dma_start(out_v[:, n * TB8:(n + 1) * TB8, :], VV[n]).then_inc(s_out, 16)
            sp.wait_ge(s_out, 16 * NB8)

        @block.gpsimd
        def _(pool):
            nc.gpsimd.memset(ZERO, 0.0).then_inc(s_zero, 1)
            nc.gpsimd.iota(jv[:, :], [[1, Q + 1]], base=0, channel_multiplier=0,
                           allow_small_or_imprecise_dtypes=True).then_inc(s_jv, 1)
            nc.gpsimd.iota(jr[:, :], [[-1, Q]], base=Q - 1, channel_multiplier=0,
                           allow_small_or_imprecise_dtypes=True).then_inc(s_jv, 1)
            nc.gpsimd.memset(identity[:, :], 0.0).then_inc(s_const, 1)
            nc.gpsimd.memset(ULT, 1.0).then_inc(s_const, 1)
            nc.gpsimd.memset(cmask[:, :], 1.0).then_inc(s_const, 1)
            pool.wait_ge(s_const, 3)
            nc.gpsimd.affine_select(out=identity[:, :], in_=identity[:, :], compare_op=ALU.not_equal, fill=1.0, base=0,
                                    pattern=[[-1, P]], channel_multiplier=1).then_inc(s_const, 1)
            nc.gpsimd.affine_select(out=ULT, in_=ULT, compare_op=ALU.is_gt, fill=0.0, base=0,
                                    pattern=[[1, P]], channel_multiplier=-1).then_inc(s_const, 1)
            nc.gpsimd.affine_select(out=cmask[:, :].rearrange("p (b c) -> p b c", c=NC),
                                    in_=cmask[:, :].rearrange("p (b c) -> p b c", c=NC), compare_op=ALU.is_gt,
                                    fill=0.0, base=0, pattern=[[0, B], [1, NC]], channel_multiplier=0).then_inc(s_const, 1)

            for q in range(QT):
                pool.wait_ge(s_nmr, q + 1)
                for t in range(q * TQ, (q + 1) * TQ - NACT):
                    ins = nc.gpsimd.tensor_scalar(XN[:, t, :], XN[:, t, :], mean[:, t:t + 1], rstd[:, t:t + 1],
                                                  ALU.subtract, ALU.mult)
                ins.then_inc(s_nrm, 1)

            pool.wait_ge(s_nrm, QT)
            pool.wait_ge(s_nra, QT)
            pool.wait_ge(s_pos, 1)
            pool.wait_ge(s_fill, 16 * (NZ + 2))
            for t in range(NT):
                nc.gpsimd.indirect_dma_start(out=xs_dram, out_offset=bass.IndirectOffsetOnAxis(ap=posi[:, t:t + 1], axis=0),
                                             in_=XN[:, t, :], in_offset=None).then_inc(s_scat, 16)

            def low_part(i):
                pool.wait_ge(s_xtr, i + 1)
                nc.gpsimd.tensor_tensor(XT[:, FT:2 * FT], XTF[:, :], XT[:, 0:FT].bitcast(F32), ALU.subtract
                                        ).then_inc(s_xlo, 1)

            bounds = expert_bounds(pool)
            low_part(0)
            for g in range(E):
                pool.wait_ge(s_w2[g % 3], 32 * (g // 3 + 1))
                pool.wait_ge(s_w2[(g + 1) % 3], 32 * ((g + 1) // 3 + 1))
                if g >= 1:
                    pool.wait_ge(s_yad, bounds[g])
                nc.gpsimd.tensor_tensor(b2p[:, :], b2s[:, g % 3, :], b2s[:, (g + 1) % 3, :], ALU.add).then_inc(s_b2, 1)
                pool.wait_ge(s_b2, 3 * g + 1)
                nc.gpsimd.tensor_scalar(b2p[:, :], b2p[:, :], 0.5, 0.0, ALU.mult, ALU.add).then_inc(s_b2, 1)
                pool.wait_ge(s_b2, 3 * g + 2)
                pool.wait_ge(s_small, 16 * NSMALL)
                nc.gpsimd.tensor_tensor(b2p[:, :], b2p[:, :], lnb[:, :], ALU.add).then_inc(s_b2, 1)
                pool.wait_ge(s_b2, 3 * g + 3)
                with pool.Fori(bounds[g], bounds[g + 1]) as i:
                    low_part(i + 1)
                    pool.wait_ge(s_ysb, i + 2)
                    nc.gpsimd.tensor_tensor(YSB, YSB, b2p[:, :].rearrange("p (o d) -> p o d", o=1).broadcast_to([P, FH, D]),
                                            ALU.add).then_inc(s_yad, 1)

            def gather(n):
                for t in range(TB8):
                    nc.gpsimd.indirect_dma_start(out=GA[n][:, t, :], out_offset=None, in_=ys_dram,
                                                 in_offset=bass.IndirectOffsetOnAxis(
                                                     ap=posi[:, n * TB8 + t:n * TB8 + t + 1], axis=0)).then_inc(s_gat[n], 16)

            def base(n):
                pool.wait_ge(s_gat[n], 16 * TB8)
                pool.wait_ge(s_xr[n], 16)
                nc.gpsimd.tensor_tensor(GA[n], GA[n], VV[n], ALU.add).then_inc(s_base, 1)

            pool.wait_ge(s_yst, bounds[E] * 16 + 16)
            pool.wait_ge(s_m2, bounds[E])
            pool.wait_ge(s_xs, bounds[E] * 16 + 32)
            pool.sem_inc(s_step, 1)
            pool.wait_ge(s_mat, 1)
            for n in range(NAR):
                gather(n)
            pool.wait_ge(s_yps, PPB)
            for n in range(NAR, NB8):
                gather(n)
                if n < NAR + 2:
                    base(2 * (n - NAR))
                    base(2 * (n - NAR) + 1)
            for n in range(NAR, NB8):
                base(n)
            pool.wait_ge(s_base, NB8)
            for n in range(NB8 - 1):
                if n < NPM:
                    pool.wait_ge(s_fn, n + 1)
                    if n >= AVF:
                        pool.wait_ge(s_fp, n - AVF + 1)
                    nc.gpsimd.tensor_tensor(VV[n], VV[n], lng_b, ALU.mult).then_inc(s_fg, 1)
                pool.wait_ge(s_fg, n + 1)
                nc.gpsimd.tensor_tensor(VV[n], VV[n], GA[n], ALU.add).then_inc(s_fo, 1)

        @block.scalar
        def _(act):
            act.sem_inc(s_ysb, 1)
            nc.scalar.preload_act_table_set("natural_log_exp_and_others")
            act.dma_start(WRAW[:, 0:HB, :], W_dt.rearrange("(b p) d -> p b d", p=P)).then_inc(s_wraw, 16)
            act.dma_start(WRAW[:, HB:2 * HB, :], W_x.rearrange("(b p) d -> p b d", p=P)).then_inc(s_wraw, 16)
            act.dma_start(WRAW[:, 2 * HB:3 * HB, :], W_g.rearrange("(b p) d -> p b d", p=P)).then_inc(s_wraw, 16)
            act.dma_start(WRAW[:, 3 * HB:4 * HB, :].rearrange("p b d -> p (b d)"), W_out).then_inc(s_wraw, 16)

            def quarter(q):
                act.wait_ge(s_lnv, q + 1)
                c = slice(q * TQ, (q + 1) * TQ)
                nc.scalar.activation(lt[5][:, c], lt[4][:, c], ACT.Ln).then_inc(s_act, 1)
                act.wait_ge(s_act, q + 1)
                nc.scalar.activation(lt[6][:, c], lt[5][:, c], ACT.Exp, scale=-0.5).then_inc(s_lny, 1)

            def normalise(q):
                act.wait_ge(s_nmr, q + 1)
                for t in range((q + 1) * TQ - NACT, (q + 1) * TQ):
                    ins = nc.scalar.activation(XN[:, t, :], XN[:, t, :], ACT.Identity, scale=rstd[:, t:t + 1],
                                               bias=nmr[:, t:t + 1])
                ins.then_inc(s_nra, 1)

            quarter(0)
            for q in range(1, QT):
                quarter(q)
                normalise(q - 1)
            act.wait_ge(s_wt, 4 * HB)
            for n in range(3 * HB):
                nc.scalar.activation(PW[:, 0, n, :], ps[n // 4][:, (n % 4) * P:(n % 4 + 1) * P], ACT.Copy).then_inc(s_wh, 1)
            normalise(QT - 1)

            def high(s, i):
                act.wait_ge(s_xt[s], i + 1)
                if not isinstance(i, int) or i:
                    act.wait_ge(s_pr[2][HB - 1], i * 2 + (s - 1))
                nc.scalar.activation(xh[s], ps[s], ACT.Copy).then_inc(s_hi[s], 1)

            def gate_input(c, odd):
                if odd:
                    act.wait_ge(s_pr[1][HB - 1], c + 1)
                    nc.scalar.activation(RB[:, HB - 1, bass.ds(c * CH, CH)], ps[4 + HB - 1], ACT.Identity,
                                         bias=bx[:, HB - 1:HB]).then_inc(s_ue[HB - 1], 1)
                for hb in range(HB):
                    act.wait_ge(s_pr[2][hb], c + 1)
                    nc.scalar.activation(RC[:, hb, bass.ds(c * CH, CH)], ps[6 + hb], ACT.Identity,
                                         bias=bg[:, hb:hb + 1]).then_inc(s_ge[hb], 1)

            def softplus(c, blocks=range(HB)):
                for hb in blocks:
                    act.wait_ge(s_min[hb], c + 1)
                    nc.scalar.activation(eb[hb], mb[hb], ACT.Exp).then_inc(s_exp[hb], 1)
                    act.wait_ge(s_exp[hb], c + 1)
                    nc.scalar.activation(eb[hb], eb[hb], ACT.Ln, bias=1.0, accum_out=acc1[:, hb, bass.ds(c, 1)]
                                         ).then_inc(s_ln[hb], 1)

            high(0, 0)
            high(1, 0)
            act.wait_ge(s_asp, 1)
            nc.scalar.activation(sv[:, :, :], sv[:, :, :], ACT.Exp).then_inc(s_asq, 1)
            act.wait_ge(s_asq, 1)
            nc.scalar.activation(sv[:, :, :], sv[:, :, :], ACT.Ln, bias=1.0).then_inc(s_asq, 1)
            act.wait_ge(s_vc, 1)
            bounds = expert_bounds(act)
            act.wait_ge(s_pos, 1)
            act.wait_ge(s_fill, 16 * (NZ + 2))
            softplus(0)
            high(0, 1)
            gate_input(0, False)
            softplus(1)
            with act.Fori(1, NCH // 2 - 1) as i:
                for s in range(2):
                    high(1 - s, i + s)
                    gate_input(i * 2 + (s - 1), s == 0)
                    softplus(i * 2 + s)
            high(1, NCH // 2 - 1)
            gate_input(NCH - 3, True)
            softplus(NCH - 2)
            gate_input(NCH - 2, False)

            def high_weights(k):
                act.wait_ge(s_w1[raw_slot(k)], 16)
                nc.scalar.activation(W1h[k], W1RAW[raw_slot(k)], ACT.Copy).then_inc(s_wsh, 1)

            high_weights(0)
            softplus(NCH - 1, [0])
            act.wait_ge(s_tt, 1)
            nc.scalar.activation(XTF[:, :], ps[0][:, 0:FT], ACT.Copy)
            act.wait_ge(s_pr[2][HB - 1], NCH)
            nc.scalar.activation(XT[:, 0:FT], ps[0][:, 0:FT], ACT.Copy).then_inc(s_xtr, 1)
            high_weights(1)
            gate_input(NCH - 1, True)
            softplus(NCH - 1, [1])
            nc.scalar.preload_act_table_set("sigmoid_and_others")

            NPIECE = HB * NGATE
            RCF = RC[:, :, :].rearrange("p b t -> p (b t)")

            def gate_piece(n):
                z = RCF[:, bass.ds(n * (GB * L), GB * L)]
                nc.scalar.activation(z, z, ACT.Sigmoid, scale=-1.0).then_inc(s_sig, 1)

            def place_tile(i):
                act.wait_ge(s_tt, i + 1)
                act.wait_ge(s_xlo, i)
                nc.scalar.activation(XTF[:, :], ps[4][:, 0:FT], ACT.Copy)
                nc.scalar.activation(XT[:, 0:FT], ps[4][:, 0:FT], ACT.Copy).then_inc(s_xtr, 1)

            for hb in range(HB):
                act.wait_ge(s_ge[hb], NCH)
                act.wait_ge(s_dte[hb], NCH)
                act.wait_ge(s_ln[hb], NCH)
            for g in range(E):
                if g == 2:
                    with act.If(bounds[2] < NPIECE):
                        with act.Fori(bounds[2], NPIECE) as n:
                            gate_piece(n)
                    nc.scalar.preload_act_table_set("natural_log_exp_and_others")
                    act.wait_ge(s_earg, 1)
                    nc.scalar.activation(EX, EX, ACT.Exp)
                    nc.scalar.activation(ER, ER, ACT.Exp).then_inc(s_eexp, 1)
                with act.Fori(bounds[g], bounds[g + 1]) as i:
                    for n in range(2):
                        e = (g + n) % E
                        for k in range(KB):
                            if k % 2 == 0:
                                act.wait_ge(s_m1[n], i * KB + (k + 2))
                            nc.scalar.activation(HID[n][:, k, :], ps[2 * n + k // 2][:, (k % 2) * FT:(k % 2 + 1) * FT],
                                                 ACT.Relu, bias=B1C[:, e, k:k + 1]).then_inc(s_re[n], 1)
                    place_tile(i + 1)
                    if g < 2:
                        with act.If(i < NPIECE):
                            gate_piece(nc.s_assert_within(i, 0, NPIECE - 1, skip_runtime_bounds_check_because="the If"))
                    act.wait_ge(s_m2, i + 1)
                    act.wait_ge(s_yst, i * 16 + 16)
                    for h in range(FH):
                        ins = nc.scalar.activation(YSB[:, h, :], ps[5 + h][:, 0:D], ACT.Copy, scale=0.5)
                    ins.then_inc(s_ysb, 1)

            def again(n):
                act.wait_ge(s_base, n + 1)
                for t in range(TB8):
                    ti_ = n * TB8 + t
                    ins = nc.scalar.activation(VV[n][:, t, :], VV[n][:, t, :], ACT.Identity, scale=rstd[:, ti_:ti_ + 1],
                                               bias=nmr[:, ti_:ti_ + 1])
                ins.then_inc(s_xa, 1)

            AHEAD = 4
            for r in range(NPAIR):
                hb, rp = divmod(r, PPB)
                act.wait_ge(s_yps, r + 1)
                nc.scalar.activation(UT[hb][:, 2 * rp:2 * rp + 2, :],
                                     PS[:, 2 + 2 * (r % 3):4 + 2 * (r % 3), 0:BC], ACT.Copy).then_inc(s_yev, 1)
                if r in (NPAIR - 9, NPAIR - 6):
                    again((r - NPAIR + 9) // 3)
            again(2)
            again(3)

            def apply(n):
                f = fs[n % 3]
                act.wait_ge(s_fr, n + 1)
                for t in range(TB8 if n < AVF else TB8 // 2):
                    ins = nc.scalar.activation(VV[n][:, t, :], vpsum(n, t), ACT.Identity,
                                               scale=f[3][:, t:t + 1], bias=f[4][:, t:t + 1])
                ins.then_inc(s_fn, 1)

            for n in range(NB8):
                f = fs[n % 3]
                act.wait_ge(s_fv, n + 1)
                nc.scalar.activation(f[2][:, :], f[1][:, :], ACT.Ln).then_inc(s_actl, 1)
                act.wait_ge(s_actl, n + 1)
                nc.scalar.activation(f[3][:, :], f[2][:, :], ACT.Exp, scale=-0.5).then_inc(s_fy, 1)
                if n >= 1:
                    apply(n - 1)
                if n + AHEAD - 1 < NB8 and n >= 1:
                    again(n + AHEAD - 1)
            apply(NB8 - 1)

        @block.vector
        def _(dve):
            count = [0]

            def link(ins):
                count[0] += 1
                ins.then_inc(s_dve, 1)
                dve.wait_ge(s_dve, count[0])

            V = nc.vector
            V.memset(ONE, 1.0)
            link(V.memset(ONEB, 1.0))
            link(V.memset(first[:, :], 0.0))
            for k in range(3):
                V.memset(first[Q * k:Q * k + 1, :], 1.0)
            V.memset(e9, 0.0)
            link(V.memset(ts9, 0.0))

            def refine(v, y, a, b_):
                link(V.tensor_tensor(a, y, y, ALU.mult))
                link(V.tensor_tensor(b_, a, v, ALU.mult))
                link(V.tensor_scalar(a, b_, -0.5, 1.5, ALU.mult, ALU.add))
                link(V.tensor_tensor(y, y, a, ALU.mult))

            def variance(st, m, v, t1, t2):
                V.tensor_tensor(m, st[:, :, 1], st[:, :, 4], ALU.add)
                V.tensor_tensor(t1, st[:, :, 1], st[:, :, 4], ALU.subtract)
                link(V.tensor_tensor(v, st[:, :, 2], st[:, :, 5], ALU.add))
                link(V.scalar_tensor_tensor(t2, t1, 0.25, t1, ALU.mult, ALU.mult))
                V.tensor_scalar(m, m, 0.5, None, ALU.mult)
                link(V.scalar_tensor_tensor(t1, v, 1.0 / D, t2, ALU.mult, ALU.add))

            xd = lt[9][:, 0:2 * TQ].rearrange("p (t k) -> p t k", k=2)
            def statistics(q):
                c = slice(q * TQ, (q + 1) * TQ)
                dve.wait_ge(s_x[q], 16)
                for t in range(q * TQ, (q + 1) * TQ):
                    ins = V.bn_stats(ST[:, t, :], XN[:, t, :])
                link(ins)
                variance(ST[:, c, :], mean[:, c], lt[3][:, c], lt[1][:, c], lt[2][:, c])
                V.tensor_scalar(lt[4][:, c], lt[1][:, c], EPS, None, ALU.add).then_inc(s_lnv, 1)

            def scales(q):
                c = slice(q * TQ, (q + 1) * TQ)
                dve.wait_ge(s_lny, q + 1)
                link(V.tensor_copy(rstd[:, c], lt[6][:, c]))
                refine(lt[4][:, c], rstd[:, c], lt[7][:, c], lt[8][:, c])
                link(V.tensor_tensor(xd, XN[:, c, 0:2], mean[:, c].rearrange("p (t o) -> p t o", o=1).broadcast_to([P, TQ, 2]),
                                     ALU.subtract))
                V.scalar_tensor_tensor(nmr[:, c], mean[:, c], -1.0, rstd[:, c], ALU.mult, ALU.mult).then_inc(s_nmr, 1)
                link(V.tensor_tensor(xd, xd, rstd[:, c].rearrange("p (t o) -> p t o", o=1).broadcast_to([P, TQ, 2]),
                                     ALU.mult))
                link(V.tensor_tensor(lt[0][:, c], xd[:, :, 0], xd[:, :, 1], ALU.add))

            statistics(0)
            for q in range(1, QT):
                statistics(q)
                scales(q - 1)
            scales(QT - 1)

            s_, a_, f_, g_, h_, w_ = lt[0], lt[1], lt[2], lt[3], lt[5], lt[7]
            link(V.scalar_tensor_tensor(a_, s_, -1.0, s_, ALU.mult, ALU.max))
            link(V.tensor_copy(ti, a_))
            link(V.tensor_copy(f_, ti))
            link(V.tensor_tensor(g_, f_, a_, ALU.is_gt))
            link(V.tensor_tensor(f_, f_, g_, ALU.subtract))
            for _ in range(2):
                link(V.tensor_scalar(g_, f_, float(E), -float(E), ALU.is_ge, ALU.mult))
                link(V.tensor_tensor(f_, f_, g_, ALU.add))
            link(V.tensor_scalar(w_, f_, -2.0, float(E), ALU.mult, ALU.add))
            link(V.scalar_tensor_tensor(h_, s_, 0.0, w_, ALU.is_lt, ALU.mult))
            link(V.tensor_tensor(h_, h_, f_, ALU.add))
            link(V.tensor_scalar(g_, h_, float(E), -float(E), ALU.is_ge, ALU.mult))
            link(V.tensor_tensor(h_, h_, g_, ALU.add))
            for e in range(E):
                ins = V.tensor_scalar(OH[:, e * NT:(e + 1) * NT], h_, float(e), None, ALU.is_equal)
            ins.then_inc(s_oh, 1)
            def low(s, i):
                dve.wait_ge(s_hi[s], i + 1)
                V.tensor_tensor(xl[s], ps[s], xh[s].bitcast(F32), ALU.subtract).then_inc(s_lo[s], 1)

            dve.wait_ge(s_wh, 3 * HB)
            for n in range(3 * HB):
                ins = V.tensor_tensor(PW[:, 1, n, :], ps[n // 4][:, (n % 4) * P:(n % 4 + 1) * P],
                                      PW[:, 0, n, :].bitcast(F32), ALU.subtract)
            ins.then_inc(s_wl, 1)
            V.tensor_copy(WoT[:, :, :].rearrange("p b d -> p (b d)"), ps[1][:, 2 * P:4 * P]).then_inc(s_wl, 1)
            dve.wait_ge(s_vt, 1)
            link(V.tensor_copy(VC[:, :], ps[2][:, 0:8 + E * KB]))
            V.tensor_scalar(cwn[:, :, :].rearrange("p b k -> p (b k)"), cw[:, :, :].rearrange("p b k -> p (b k)"),
                            -1.0, None, ALU.mult)
            V.tensor_scalar(cbn[:, :], cb, -1.0, None, ALU.mult)
            V.tensor_scalar(sv[:, :, :], Araw[:, :, :], SOFT, None, ALU.min).then_inc(s_asp, 1)
            link(V.tensor_scalar(sv2[:, :, :], Araw[:, :, :], SOFT, None, ALU.subtract))
            link(V.tensor_scalar(sv2[:, :, :], sv2[:, :, :], 0.0, None, ALU.max))
            V.tensor_scalar(cwn[:, :, 1], cwn[:, :, 1], 1.0, None, ALU.add).then_inc(s_vc, 1)
            dve.wait_ge(s_rank, 2)
            link(V.tensor_tensor_scan(PI, ONE, ps[7], 0.0, ALU.mult, ALU.add))
            PI3 = PI.rearrange("p (e t) -> p e t", e=E)
            V.tensor_tensor(PA, ps[6], PI, ALU.add)
            link(V.tensor_copy(e9[:, 1:E + 1], PI3[:, :, NT - 1]))
            cnt, qf, gt, nt, pad = e8
            V.tensor_tensor(PA, ps[7], PA, ALU.subtract)
            link(V.tensor_tensor(cnt, e9[:, 1:E + 1], e9[:, 0:E], ALU.subtract))
            link(V.tensor_scalar(qf, cnt, float(FT - 1), 1.0 / FT, ALU.add, ALU.mult))
            link(V.tensor_copy(e8i, qf))
            link(V.tensor_copy(nt, e8i))
            link(V.tensor_tensor(gt, nt, qf, ALU.is_gt))
            link(V.tensor_tensor(nt, nt, gt, ALU.subtract))
            link(V.tensor_scalar(nt, nt, 1.0, None, ALU.max))
            link(V.tensor_tensor_scan(ts9[:, 1:E + 1], ONE[:, 0:E], nt, 0.0, ALU.mult, ALU.add))
            V.tensor_copy(tsi[:, :], ts9).then_inc(s_bnd, 1)
            link(V.scalar_tensor_tensor(pad, ts9[:, 0:E], float(FT), e9[:, 0:E], ALU.mult, ALU.subtract))
            PA3 = PA.rearrange("p (e t) -> p e t", e=E)
            low(0, 0)
            link(V.tensor_tensor(PA3, pad.rearrange("p (e o) -> p e o", o=1).broadcast_to([P, E, NT]), PA3, ALU.subtract))
            link(V.tensor_tensor(PA, PA, OH, ALU.mult))
            link(V.tensor_reduce(lt[10], PA.rearrange("p (e t) -> p t e", e=E), AX_X, ALU.add))
            V.tensor_copy(posi[:, :], lt[10]).then_inc(s_pos, 1)

            def clamp(c, hb):
                dve.wait_ge(s_pr[0][hb], c + 1)
                if not isinstance(c, int) or c:
                    dve.wait_ge(s_exp[hb], c)
                V.tensor_scalar(mb[hb], ps[2 + hb], bdt[:, hb:hb + 1], SOFT, ALU.add, ALU.min).then_inc(s_min[hb], 1)
                dve.wait_ge(s_min[hb], c + 1)
                V.scalar_tensor_tensor(junk, ps[2 + hb], bdt[:, hb:hb + 1], mb[hb], ALU.add, ALU.subtract,
                                       accum_out=acc2[:, hb, bass.ds(c, 1)]).then_inc(s_dte[hb], 1)

            def split_low(k):
                dve.wait_ge(s_wsh, k + 1)
                V.tensor_tensor(W1l[k % 3], W1RAW[raw_slot(k)], W1h[k % 3].bitcast(F32), ALU.subtract).then_inc(s_ws, 1)

            def step(s, i, last=False):
                c = i * 2 + s
                clamp(c, 0)
                if not last:
                    low(1 - s, i + s)
                clamp(c, 1)
                if last:
                    split_low(0)
                for hb in range(HB - s):
                    dve.wait_ge(s_pr[1][hb], c + 1)
                    V.tensor_scalar(RB[:, hb, bass.ds(c * CH, CH)], ps[4 + hb], bx[:, hb:hb + 1], None, ALU.add
                                    ).then_inc(s_ue[hb], 1)

            step(0, 0)
            step(1, 0)
            with dve.Fori(1, NCH // 2 - 1) as i:
                step(0, i)
                step(1, i)
            step(0, NCH // 2 - 1)
            step(1, NCH // 2 - 1, last=True)

            split_low(1)
            bounds = expert_bounds(dve)
            for hb in range(HB):
                dve.wait_ge(s_dte[hb], NCH)
                dve.wait_ge(s_ln[hb], NCH)
                dve.wait_ge(s_ue[hb], NCH)
            V.tensor_reduce(dtv[:, :, 0], acc1[:, :, :], AX_X, ALU.add)
            link(V.tensor_reduce(dtv[:, :, 1], acc2[:, :, :], AX_X, ALU.add))
            link(V.tensor_tensor(dtv[:, :, 0], dtv[:, :, 0], dtv[:, :, 1], ALU.add))
            link(V.tensor_scalar(dtv[:, :, 0], dtv[:, :, 0], 1.0 / NTOK, DT_MIN, ALU.mult, ALU.max))
            link(V.tensor_scalar(dtv[:, :, 0], dtv[:, :, 0], DT_MAX, None, ALU.min))
            dve.wait_ge(s_asq, 2)
            link(V.tensor_tensor(Aneg[:, :, :], sv[:, :, :], sv2[:, :, :], ALU.add))
            link(V.tensor_scalar(Aneg[:, :, :], Aneg[:, :, :], -1.0, None, ALU.mult))
            for hb in range(HB):
                link(V.tensor_scalar(aval[:, hb, :], Aneg[:, hb, :], dtv[:, hb, 0:1], None, ALU.mult))

            def split_weights(k):
                dve.wait_ge(s_w1[raw_slot(k)], 16 * raw_loads(k))
                if k >= 3:
                    dve.wait_ge(s_m2, bounds[k - 2])
                dve.sem_inc(s_step2, 1)
                V.tensor_copy(W1h[k % 3], W1RAW[raw_slot(k)]).then_inc(s_wsh, 1)
                split_low(k)

            dve.wait_ge(s_ws, 2)

            for hb in range(HB):
                for n in range(NGATE):
                    c = gate_cols(n)
                    u, z = RB[:, hb, c], RC[:, hb, c]
                    u3 = u.rearrange("p (b l) -> p b l", l=L)
                    t3 = TG.rearrange("p (b l) -> p b l", l=L)
                    link(V.tensor_scalar(TG, u, cwn[:, hb, 1:2], cbn[:, hb:hb + 1], ALU.mult, ALU.add))
                    link(V.scalar_tensor_tensor(t3[:, :, 1:L], u3[:, :, 0:L - 1], cwn[:, hb, 0:1], t3[:, :, 1:L],
                                                ALU.mult, ALU.add))
                    link(V.scalar_tensor_tensor(t3[:, :, 0:L - 1], u3[:, :, 1:L], cwn[:, hb, 2:3], t3[:, :, 0:L - 1],
                                                ALU.mult, ALU.add))
                    dve.wait_ge(s_sig, hb * NGATE + n + 1)
                    link(V.tensor_tensor(TG, TG, z, ALU.mult))
                    link(V.tensor_tensor(z, u, TG, ALU.subtract))
                    if hb == 0 and n == 0:
                        dve.wait_ge(s_scat, 16 * NT)
                        dve.wait_ge(s_xin[0], 16 * NCH // 2)
                        dve.wait_ge(s_xin[1], 16 * NCH // 2)
                    w = GB * NC
                    link(V.transpose(UT[hb][:, :, n * w:(n + 1) * w].rearrange("p g c -> p c g"),
                                     z.rearrange("p (c i) -> p c i", i=Q)))
                    if hb == 0 and n == 0:
                        split_weights(2)

            dve.wait_ge(s_jv, 2)
            av = aval[:, :, :].rearrange("p b (s o) -> p b s o", o=1)
            for hb in range(HB):
                V.tensor_tensor(EX[:, hb], av[:, hb].broadcast_to([P, S, Q + 1]),
                                jv[:, :].rearrange("p (o j) -> p o j", o=1).broadcast_to([P, S, Q + 1]), ALU.mult)
                ins = V.tensor_tensor(ER[:, hb], av[:, hb].broadcast_to([P, S, Q]),
                                      jr[:, :].rearrange("p (o j) -> p o j", o=1).broadcast_to([P, S, Q]), ALU.mult)
            ins.then_inc(s_earg, 1)
            V.memset(INTRA.rearrange("p g m -> p (g m)"), 0.0)
            V.memset(INJ.rearrange("p g m -> p (g m)"), 0.0)
            V.memset(KP.rearrange("p b j -> p (b j)"), 0.0)
            V.memset(READ.rearrange("p g m -> p (g m)"), 0.0)
            dve.wait_ge(s_const, 6)
            link(V.tensor_copy(bop[:, :], bo[:, :]))
            link(V.tensor_tensor(bor[:, :], bo[:, :], bop[:, :], ALU.subtract))
            V.tensor_copy(bop[Q:2 * Q, :], bor[Q:2 * Q, :])
            link(V.tensor_copy(bop[2 * Q:, :], bor[2 * Q:, :]))
            link(V.tensor_tensor(bor[2 * Q:, :], bor[2 * Q:, :], bop[2 * Q:, :], ALU.subtract))
            link(V.tensor_copy(bop[2 * Q:, :], bor[2 * Q:, :]))
            link(V.tensor_reduce(half4[:, :, :], identity[:, :].rearrange("p (q h s) -> p h q s", q=NQ, h=2), AX_X, ALU.add))
            link(V.tensor_reduce(half[:, :], half4[:, :, :], AX_X, ALU.add))
            for k in range(3, E + 1):
                split_weights(k)
            dve.wait_ge(s_eexp, 1)
            V.tensor_scalar(sv[:, :, :], EX[:, :, :, 1], -1.0, None, ALU.add)
            link(V.tensor_scalar(sv2[:, :, :], Aneg[:, :, :], 1e-6, None, ALU.add))
            link(V.reciprocal(sv2[:, :, :], sv2[:, :, :]))
            link(V.tensor_tensor(sv[:, :, :], sv[:, :, :], sv2[:, :, :], ALU.mult))
            link(V.tensor_tensor(sv[:, :, :], sv[:, :, :], Bssm[:, :, :], ALU.mult))
            link(V.tensor_tensor(sv2[:, :, :], sv[:, :, :], Cssm[:, :, :], ALU.mult))
            KT = TA[:, 0:HB * Q * S].rearrange("p (b j s) -> p b j s", b=HB, s=S)
            for hb in range(HB):
                ins = V.tensor_tensor(KT[:, hb], EX[:, hb, :, 0:Q].rearrange("p s j -> p j s"),
                                      sv2[:, hb, :].rearrange("p (o s) -> p o s", o=1).broadcast_to([P, Q, S]), ALU.mult)
            link(ins)
            for hb in range(HB):
                ins = V.tensor_reduce(KP[:, hb, Q - 1:2 * Q - 1], KT[:, hb], AX_X, ALU.add)
            link(ins)
            TO = TA[:, 0:HB * Q * Q].rearrange("p (b i j) -> p b i j", b=HB, j=Q)
            TT = TB[:, 0:HB * Q * Q].rearrange("p (b g i) -> p b g i", b=HB, i=Q)
            for j in range(Q):
                ins = V.tensor_copy(TO[:, :, :, j], KP[:, :, Q - 1 - j:2 * Q - 1 - j])
            link(ins)
            link(V.transpose(TB[:, 0:HB * Q * Q].rearrange("p (b g i) -> p b i g", b=HB, i=Q), TO))
            IN5 = RB[:, 0, :].rearrange("p (b g q i) -> p b g q i", b=HB, q=NQ, i=Q)
            for q in range(NQ):
                r = slice(Q * q, Q * q + Q)
                for hb in range(HB):
                    ins = V.tensor_copy(IN5[r, hb, :, q, :], TT[r, hb])
            link(ins)
            IE = TA[:, 0:HB * S * Q].rearrange("p (b s j) -> p b s j", b=HB, s=S)
            IT = TB[:, 0:HB * S * Q].rearrange("p (b g s) -> p b g s", b=HB, s=S)
            for hb in range(HB):
                ins = V.tensor_tensor(IE[:, hb], ER[:, hb],
                                      sv[:, hb, :].rearrange("p (s o) -> p s o", o=1).broadcast_to([P, S, Q]), ALU.mult)
            link(ins)
            link(V.transpose(TB[:, 0:HB * S * Q].rearrange("p (b g s) -> p b s g", b=HB, s=S), IE))
            INJ5 = INJ.rearrange("p (b g) (q s) -> p b g q s", b=HB, q=NQ)
            for q in range(NQ):
                r = slice(Q * q, Q * q + Q)
                for hb in range(HB):
                    ins = V.tensor_copy(INJ5[r, hb, :, q, :], IT[r, hb])
            link(ins)
            RD = TA.rearrange("p (b i x) -> p b i x", b=HB, x=Q)
            for hb in range(HB):
                for rep in range(Q // S):
                    V.tensor_tensor(RD[:, hb, 0:Q, rep * S:(rep + 1) * S],
                                    EX[:, hb, :, 1:Q + 1].rearrange("p s j -> p j s"),
                                    Cssm[:, hb, :].rearrange("p (o s) -> p o s", o=1).broadcast_to([P, Q, S]), ALU.mult)
                    ins = V.tensor_copy(RD[:, hb, Q, rep * S:(rep + 1) * S], EX[:, hb, :, Q])
            link(ins)
            for hb in range(HB):
                ins = V.transpose(TB.rearrange("p (b g i) -> p b i g", b=HB, i=Q + 1)[:, hb],
                                  RD[:, hb])
            link(ins)
            RT = TB.rearrange("p (r a i) -> p a r i", a=2, i=Q + 1)
            for ab in range(2):
                for q in range(NQ):
                    src = slice(Q * q, Q * (q + 1))
                    dst = slice(Q * (2 * ab + q // 2), Q * (2 * ab + q // 2 + 1))
                    V.tensor_scalar(READ[dst, :, q * Q:(q + 1) * Q], RT[src, ab, :, 0:Q], half[src, q % 2:q % 2 + 1], None,
                                    ALU.mult)
                    ins = V.tensor_scalar(AP2[dst, q % 2, :], RT[src, ab, :, Q], half[src, q % 2:q % 2 + 1], None, ALU.mult)
            link(ins)
            link(V.tensor_tensor(A32[:, :], AP2[:, 0, :], AP2[:, 1, :], ALU.add))
            dve.wait_ge(s_re[0], bounds[E] * KB)
            for n in range(2):
                ins = V.memset(ps[n][:, 0:BC].rearrange("p (b c) -> p b c", c=NC)[:, :, 0], 0.0)
            ins.then_inc(s_mat, 1)

            def y_piece(hb, n):
                if n == 0:
                    dve.wait_ge(s_yev, (hb + 1) * PPB)
                w = BC // NYP
                V.transpose(YT[hb][:, n * w * Q:(n + 1) * w * Q].rearrange("p (c i) -> p c i", i=Q),
                            UT[hb][:, :, n * w:(n + 1) * w].rearrange("p g c -> p c g")).then_inc(s_ytr, 1)

            dve.wait_ge(s_m2, bounds[E])
            for r in range(NPAIR):
                if r >= 2:
                    dve.wait_ge(s_yps, r - 1)
                V.tensor_scalar(D0[r % 2], cmask[:, :], A32[:, r:r + 1], None, ALU.mult).then_inc(s_d0, 1)
                dve.wait_ge(s_d0, r + 1)
                dve.wait_ge(s_inj, r + 1)
                V.tensor_tensor_scan(SX[r % 2], D0[r % 2], ps[r % 2][:, 0:BC], 0.0, ALU.mult, ALU.add).then_inc(s_scan, 1)
                if 1 <= r - PPB <= NYP:
                    y_piece(0, r - PPB - 1)
            for n in range(2):
                y_piece(1, n)

            def sums(n):
                st, f = FST[n % 2], fs[n % 3]
                for t in range(TB8):
                    if t % 4 == 0:
                        dve.wait_ge(s_po, 2 * n + t // 4 + 1)
                    ins = V.bn_stats(st[:, t, :], vpsum(n, t))
                link(ins)
                if n >= 3:
                    dve.wait_ge(s_fn, n - 2)
                variance(st[:, :, :], f[0][:, :], f[1][:, :], f[2][:, :], f[4][:, :])
                V.tensor_scalar(f[1][:, :], f[2][:, :], EPS, None, ALU.add).then_inc(s_fv, 1)

            def finish(n):
                vv = VV[n]
                if n < NPM:
                    return
                dve.wait_ge(s_fn, n + 1)
                dve.wait_ge(s_fg, n)
                if n >= AVF:
                    dve.wait_ge(s_fp, n - AVF + 1)
                V.tensor_tensor(vv, vv, lng_b, ALU.mult).then_inc(s_fg, 1)
                if n == NB8 - 1:
                    dve.wait_ge(s_fg, n + 1)
                    dve.wait_ge(s_base, NB8)
                    V.tensor_tensor(vv, vv, GA[n], ALU.add).then_inc(s_flast, 1)

            sums(0)
            for n in range(NB8):
                f = fs[n % 3]
                dve.wait_ge(s_fy, n + 1)
                refine(f[1][:, :], f[3][:, :], f[2][:, :], f[4][:, :])
                V.scalar_tensor_tensor(f[4][:, :], f[0][:, :], -1.0, f[3][:, :], ALU.mult, ALU.mult).then_inc(s_fr, 1)
                dve.wait_ge(s_fr, n + 1)
                vv = VV[n]
                for t in range(TB8 // 2, TB8 if n >= AVF else 0):
                    ins = V.tensor_scalar(vv[:, t, :], vpsum(n, t), f[3][:, t:t + 1], f[4][:, t:t + 1], ALU.mult, ALU.add)
                if n >= AVF:
                    ins.then_inc(s_fp, 1)
                for k in range(2 * n + 2, min(2 * n + 4, NYP)):
                    y_piece(1, k)
                if n + 1 < NB8:
                    sums(n + 1)
                if n >= 1:
                    finish(n - 1)
            finish(NB8 - 1)

        @block.tensor
        def _(pe):
            T = nc.tensor
            pe.wait_ge(s_const, 6)
            pe.wait_ge(s_wraw, 64)
            for n in range(4 * HB):
                T.transpose(ps[n // 4][:, (n % 4) * P:(n % 4 + 1) * P], WRAW[:, n, :], identity[:, :]).then_inc(s_wt, 1)
            pe.wait_ge(s_small, 16 * NSMALL)
            R = 8 + E * KB
            T.transpose(ps[2][:, 0:R], vrows[:, :], identity[0:R, 0:R]).then_inc(s_vt, 1)
            pe.wait_ge(s_oh, 1)
            T.matmul(ps[6], ULT, OH, start=True, stop=True).then_inc(s_rank, 1)
            T.matmul(ps[7], ONEB, OH, start=True, stop=True).then_inc(s_rank, 1)

            def transpose_tile(i, bank):
                pe.wait_ge(s_xs, i * 16 + 16)
                for h in range(FH):
                    ins = T.transpose(ps[bank][:, h * P:(h + 1) * P], XSIN[:, h, :], identity[:, :])
                ins.then_inc(s_tt, 1)

            def transpose_chunk(s, i):
                pe.wait_ge(s_xin[s], (i + 1) * 16)
                if not isinstance(i, int) or i:
                    pe.wait_ge(s_lo[s], i)
                for t in range(TPC):
                    ins = T.transpose(ps[s][:, t * P:(t + 1) * P], xin[s][:, t, :], identity[:, :])
                ins.then_inc(s_xt[s], 1)

            def project(s, i, parts=range(3)):
                c = i * 2 + s
                pe.wait_ge(s_lo[s], i + 1)
                for j in parts:
                    free = (s_dte, s_ue, s_ge)[j]
                    for hb in range(HB):
                        if not isinstance(c, int) or c:
                            pe.wait_ge(free[hb], c)
                        n, bank = j * HB + hb, ps[2 + 2 * j + hb]
                        T.matmul(bank, PW[:, 0, n, :], xh[s], start=True, stop=False)
                        T.matmul(bank, PW[:, 0, n, :], xl[s], start=False, stop=False)
                        T.matmul(bank, PW[:, 1, n, :], xh[s], start=False, stop=True).then_inc(s_pr[j][hb], 1)

            pe.wait_ge(s_wl, 2)
            transpose_chunk(0, 0)
            transpose_chunk(1, 0)
            pe.wait_ge(s_vc, 1)
            project(0, 0, [0, 1])
            pe.wait_ge(s_pos, 1)
            project(0, 0, [2])
            bounds = expert_bounds(pe)
            transpose_chunk(0, 1)
            project(1, 0)
            with pe.Fori(1, NCH // 2 - 1) as i:
                transpose_chunk(1, i)
                project(0, i)
                transpose_chunk(0, i + 1)
                project(1, i)
            i = NCH // 2 - 1
            transpose_chunk(1, i)
            project(0, i)
            transpose_tile(0, 0)
            project(1, i)

            for hb in range(HB):
                pe.wait_ge(s_dte[hb], NCH)
            for g in range(E):
                if g == 0:
                    pe.wait_ge(s_ws, 1)
                    pe.wait_ge(s_w2[0], 32)
                with pe.Fori(bounds[g], bounds[g + 1]) as i:
                    pe.wait_ge(s_xlo, i + 1)
                    for n in range(2):
                        slot = (g + n) % 3
                        if n == 1:
                            pe.wait_ge(s_ws, g + 2)
                        for k in range(KB):
                            bank = ps[2 * n + k // 2][:, (k % 2) * FT:(k % 2 + 1) * FT]
                            w = slice(k * P, (k + 1) * P)
                            T.matmul(bank, W1h[slot][:, w], XT[:, 0:FT], start=True, stop=False)
                            T.matmul(bank, W1h[slot][:, w], XT[:, FT:2 * FT], start=False, stop=False)
                            T.matmul(bank, W1l[slot][:, w], XT[:, 0:FT], start=False, stop=True).then_inc(s_m1[n], 1)
                    if g == 0:
                        pe.wait_ge(s_ue[0], NCH)
                    transpose_tile(i + 1, 4)
                    if g == 0:
                        pe.wait_ge(s_ue[1], NCH)
                        pe.wait_ge(s_ge[0], NCH)
                    pe.wait_ge(s_ysb, i + 1)
                    for n in range(2):
                        slot = (g + n) % 3
                        if n == 1:
                            pe.wait_ge(s_w2[slot], 32 * ((g + 1) // 3 + 1))
                        for k in range(KB):
                            pe.wait_ge(s_re[n], i * KB + (k + 1))
                            for h in range(FH):
                                ins = T.matmul(ps[5 + h][:, 0:D], HID[n][:, k, h * P:(h + 1) * P], W2S[slot][:, k, :],
                                               start=(n == 0 and k == 0), stop=(n == 1 and k == KB - 1))
                    ins.then_inc(s_m2, 1)

            pe.wait_ge(s_mat, 1)

            def inject(r):
                hb, rp = divmod(r, PPB)
                if r >= 2:
                    pe.wait_ge(s_scan, r - 1)
                for ab in range(2):
                    g = 2 * rp + ab
                    u = UT[hb][:, g, :].rearrange("p (b c) -> p b c", c=NC)[:, :, 0:NC - 1]
                    dst = ps[r % 2][64 * ab:64 * ab + 64, 0:BC].rearrange("p (b c) -> p b c", c=NC)[:, :, 1:NC]
                    ins = T.matmul(dst, INJ[:, hb * NG + g, :], u, start=True, stop=True)
                ins.then_inc(s_inj, 1)

            inject(0)
            for r in range(NPAIR):
                hb, rp = divmod(r, PPB)
                if r >= 3:
                    pe.wait_ge(s_yev, r - 2)
                if r + 1 < NPAIR:
                    inject(r + 1)
                if r == 1:
                    pe.wait_ge(s_xtr, bounds[E] + 1)
                    pe.wait_ge(s_ysb, bounds[E] + 1)
                banks = [ps[2 + 2 * (r % 3) + ab][:, 0:BC] for ab in range(2)]
                for ab in range(2):
                    g = 2 * rp + ab
                    T.matmul(banks[ab], INTRA[:, hb * NG + g, :], UT[hb][:, g, :], start=True, stop=False)
                pe.wait_ge(s_scan, r + 1)
                for ab in range(2):
                    rows = slice(64 * ab, 64 * ab + 64)
                    ins = T.matmul(banks[ab], READ[rows, r, :], SX[r % 2][rows, :], start=False, stop=True)
                ins.then_inc(s_yps, 1)

            pe.wait_ge(s_yev, NPAIR)
            for n in range(NT // 4):
                pe.wait_ge(s_ytr, NYP + n * NYP // (NT // 4) + 1)
                pe.wait_ge(s_xa, n // 2 + 1)
                if n >= 8:
                    pe.wait_ge(s_fn, n // 2 - 3)
                    if n // 2 - 4 >= AVF:
                        pe.wait_ge(s_fp, n // 2 - 3 - AVF)
                for t in range(4):
                    tt = 4 * n + t
                    dst = ps[n % 8][:, t * D:(t + 1) * D]
                    T.matmul(dst, first[:, :], bop[:, :], start=True, stop=False)
                    for hb in range(HB):
                        T.matmul(dst, YT[hb][:, tt * P:(tt + 1) * P], WoT[:, hb, :], start=False, stop=False)
                    ins = T.matmul(dst, identity[:, :], VV[n // 2][:, tt % TB8, :], start=False, stop=True)
                ins.then_inc(s_po, 1)


_INS = ['x', 'W_x', 'b_x', 'W_g', 'b_g', 'conv_w', 'conv_b', 'A_raw', 'B_ssm', 'C_ssm', 'W_dt', 'b_dt', 'W_out', 'b_out',
        'ln_g', 'ln_b']
_INS = ['L0_attn_' + n for n in _INS] + ['L0_ffn_' + n for n in ('W1', 'b1', 'W2', 'b2')]
_OUTS = [((32, 256, 128), 'float32')]


def kernel(**inputs):
    import numpy as _np
    import concourse.bacc as _bacc
    from concourse import mybir as _mybir
    from concourse.bass_utils import run_bass_kernel_spmd as _run

    nc = _bacc.Bacc("TRN2", target_bir_lowering=False, num_devices=1, dynamic_dma_scratch_size=8192)
    arrays, args = {}, []
    for name in _INS:
        a = _np.ascontiguousarray(inputs[name])
        arrays[f"in_{name}_dram"] = a
        args.append(nc.dram_tensor(f"in_{name}_dram", a.shape, _mybir.dt.from_np(a.dtype), kind="ExternalInput").ap())
    for i, (shape, dtype) in enumerate(_OUTS):
        dt = _mybir.dt.from_np(_np.dtype(dtype))
        args.append(nc.dram_tensor(f"out_{i}_dram", shape, dt, kind="ExternalOutput").ap())
    ssm_moe_layer(nc, *args)
    r = _run(nc, [arrays], core_ids=[0])
    got = tuple(r.results[0][f"out_{i}_dram"] for i in range(len(_OUTS)))
    return got[0]
```
